# Optimizing a Trainium2 kernel written in Bass

```python
import numpy as np
import jax
import jax.numpy as jnp

def _softmax(x, axis=-1):
    return jax.nn.softmax(x, axis=axis)

def _gelu(x):
    return jax.nn.gelu(x, approximate=True)

def _silu(x):
    return jax.nn.silu(x)

def _sigmoid(x):
    return jax.nn.sigmoid(x)

def _layernorm(x, axis=-1, eps=1e-05):
    m = jnp.mean(x, axis=axis, keepdims=True)
    v = jnp.var(x, axis=axis, keepdims=True)
    return (x - m) / jnp.sqrt(v + eps)

def _scatter_add(tgt, idx, src, axis=0):
    return tgt.at[idx].add(src)

def _segment_sum(src, seg, n):
    return jax.ops.segment_sum(src, seg, n)
kernel_name = 'mk_gps_d1_gnn_r8_4ab911'

def setup_inputs(seed: int=0):
    np.random.seed(seed)
    _w = jnp.asarray

    def _rec_inputs():
        import jax
        import jax.numpy as jnp
        _gk = jax.random.key(seed)
        x = -6.415e-05 + 1 * jax.random.normal(jax.random.fold_in(_gk, 1), (1250, 1024), jnp.float32)
        src = jax.random.randint(jax.random.fold_in(_gk, 2), (20000,), 0, 1250, jnp.int32)
        dst = jnp.minimum((1250 * jax.random.uniform(jax.random.fold_in(_gk, 3), (20000,)) ** 2.0).astype(jnp.int32), 9999)
        _o = jnp.argsort(dst, stable=True)
        src = src[_o]
        dst = dst[_o]
        return (x, src, dst)
    x, src, dst = _rec_inputs()

    def _L0_gnn_setup():
        import jax, jax.numpy as jnp
        import numpy as np
        NEG_SLOPE = 0.1
        EPS = 1e-05
        key = jax.random.key(seed)
        k1, k2, k3, k4, k5 = jax.random.split(key, 5)
        N, E, DIN, DOUT = (1250, 20000, 1024, 1024)
        x = jax.random.normal(k1, (N, DIN), dtype=jnp.float32)
        W = jax.random.normal(k2, (DIN, DOUT), dtype=jnp.float32) * 0.02
        a = jax.random.normal(k3, (1, 2 * DOUT), dtype=jnp.float32) * 0.02
        src = jax.random.randint(k4, (E,), 0, N, dtype=jnp.int64)
        dst = jax.random.randint(k5, (E,), 0, N, dtype=jnp.int64)
        return {'x': x, 'W': W, 'a': a, 'src': src, 'dst': dst}
    _L0_gnn_all = _L0_gnn_setup()
    _L0_gnn_in = {k: v for k, v in _L0_gnn_all.items() if k in ('W', 'a')}
    del _L0_gnn_all

    def _L0_mix_setup():
        import jax, jax.numpy as jnp
        import numpy as np
        import math
        D_MODEL = 1024
        N_HEAD = 16
        D_HEAD = D_MODEL // N_HEAD
        D_KMAP = 128
        D_INNER = 512

        def _layer_norm(x, g, b, eps=1e-05):
            mu = jnp.mean(x, axis=-1, keepdims=True)
            var = jnp.mean(jnp.square(x - mu), axis=-1, keepdims=True)
            return (x - mu) * jax.lax.rsqrt(var + eps) * g + b

        def _fourier_kernel(x, proj_mat):
            p = jnp.einsum('blhd,dm->blhm', x, proj_mat) / math.sqrt(D_HEAD)
            return jnp.concatenate([jnp.cos(p), jnp.sin(p)], axis=-1) / math.sqrt(D_KMAP)
        key = jax.random.key(seed)
        ks = jax.random.split(key, 12)
        s = 0.02
        return {'x': jax.random.normal(ks[0], (4, 512, D_MODEL), dtype=jnp.float32), 'proj_mat': jax.random.normal(ks[1], (D_HEAD, D_KMAP), dtype=jnp.float32), 'wq': jax.random.normal(ks[2], (D_MODEL, D_MODEL), dtype=jnp.float32) * s, 'bq': jnp.zeros((D_MODEL,), jnp.float32), 'wk': jax.random.normal(ks[3], (D_MODEL, D_MODEL), dtype=jnp.float32) * s, 'bk': jnp.zeros((D_MODEL,), jnp.float32), 'wv': jax.random.normal(ks[4], (D_MODEL, D_MODEL), dtype=jnp.float32) * s, 'bv': jnp.zeros((D_MODEL,), jnp.float32), 'wo': jax.random.normal(ks[5], (D_MODEL, D_MODEL), dtype=jnp.float32) * s, 'bo': jnp.zeros((D_MODEL,), jnp.float32), 'ln1_g': jnp.ones((D_MODEL,), jnp.float32), 'ln1_b': jnp.zeros((D_MODEL,), jnp.float32), 'w1': jax.random.normal(ks[6], (D_MODEL, D_INNER), dtype=jnp.float32) * s, 'b1': jnp.zeros((D_INNER,), jnp.float32), 'w2': jax.random.normal(ks[7], (D_INNER, D_MODEL), dtype=jnp.float32) * s, 'b2': jnp.zeros((D_MODEL,), jnp.float32), 'ln2_g': jnp.ones((D_MODEL,), jnp.float32), 'ln2_b': jnp.zeros((D_MODEL,), jnp.float32)}
    _L0_mix_all = _L0_mix_setup()
    _L0_mix_in = {k: v for k, v in _L0_mix_all.items() if k in ('proj_mat', 'wq', 'bq', 'wk', 'bk', 'wv', 'bv', 'wo', 'bo', 'ln1_g', 'ln1_b', 'w1', 'b1', 'w2', 'b2', 'ln2_g', 'ln2_b')}
    del _L0_mix_all

    def _L0_ffn_setup():
        import jax, jax.numpy as jnp
        import numpy as np
        HIDDEN = 1024
        INNER = 512

        def _weight_quant(w):
            scale = 1.0 / jnp.clip(jnp.mean(jnp.abs(w)), 1e-05)
            wq = jnp.clip(jnp.round(w * scale), -1.0, 1.0) / scale
            return w + jax.lax.stop_gradient(wq - w)

        def _act_quant(x):
            scale = 127.0 / jnp.clip(jnp.max(jnp.abs(x), axis=-1, keepdims=True), 1e-05)
            xq = jnp.clip(jnp.round(x * scale), -128.0, 127.0) / scale
            return x + jax.lax.stop_gradient(xq - x)

        def _bitlinear(x, w):
            return jnp.einsum('bsi,oi->bso', _act_quant(x), _weight_quant(w))
        key = jax.random.key(seed)
        k0, k1, k2, k3 = jax.random.split(key, 4)
        x = jax.random.normal(k0, (4, 256, HIDDEN), dtype=jnp.float32)
        w_gate = jax.random.normal(k1, (INNER, HIDDEN), dtype=jnp.float32) / np.sqrt(HIDDEN)
        w_up = jax.random.normal(k2, (INNER, HIDDEN), dtype=jnp.float32) / np.sqrt(HIDDEN)
        w_down = jax.random.normal(k3, (HIDDEN, INNER), dtype=jnp.float32) / np.sqrt(INNER)
        return {'x': x, 'w_gate': w_gate, 'w_up': w_up, 'w_down': w_down}
    _L0_ffn_all = _L0_ffn_setup()
    _L0_ffn_in = {k: v for k, v in _L0_ffn_all.items() if k in ('w_gate', 'w_up', 'w_down')}
    del _L0_ffn_all
    return {'x': x, 'src': src, 'dst': dst, 'L0_gnn_W': _L0_gnn_in['W'], 'L0_gnn_a': _L0_gnn_in['a'], 'L0_mix_proj_mat': _L0_mix_in['proj_mat'], 'L0_mix_wq': _L0_mix_in['wq'], 'L0_mix_bq': _L0_mix_in['bq'], 'L0_mix_wk': _L0_mix_in['wk'], 'L0_mix_bk': _L0_mix_in['bk'], 'L0_mix_wv': _L0_mix_in['wv'], 'L0_mix_bv': _L0_mix_in['bv'], 'L0_mix_wo': _L0_mix_in['wo'], 'L0_mix_bo': _L0_mix_in['bo'], 'L0_mix_ln1_g': _L0_mix_in['ln1_g'], 'L0_mix_ln1_b': _L0_mix_in['ln1_b'], 'L0_mix_w1': _L0_mix_in['w1'], 'L0_mix_b1': _L0_mix_in['b1'], 'L0_mix_w2': _L0_mix_in['w2'], 'L0_mix_b2': _L0_mix_in['b2'], 'L0_mix_ln2_g': _L0_mix_in['ln2_g'], 'L0_mix_ln2_b': _L0_mix_in['ln2_b'], 'L0_ffn_w_gate': _L0_ffn_in['w_gate'], 'L0_ffn_w_up': _L0_ffn_in['w_up'], 'L0_ffn_w_down': _L0_ffn_in['w_down']}

def reference(x, src, dst, L0_gnn_W, L0_gnn_a, L0_mix_proj_mat, L0_mix_wq, L0_mix_bq, L0_mix_wk, L0_mix_bk, L0_mix_wv, L0_mix_bv, L0_mix_wo, L0_mix_bo, L0_mix_ln1_g, L0_mix_ln1_b, L0_mix_w1, L0_mix_b1, L0_mix_w2, L0_mix_b2, L0_mix_ln2_g, L0_mix_ln2_b, L0_ffn_w_gate, L0_ffn_w_up, L0_ffn_w_down):
    import jax
    import jax.numpy as jnp

    def _L0_gnn_ref(x, W, a, src, dst):
        import jax, jax.numpy as jnp
        import numpy as np
        NEG_SLOPE = 0.1
        EPS = 1e-05
        N = x.shape[0]
        d = W.shape[1]
        h = x @ W
        a_l, a_r = (a[0, :d], a[0, d:])
        al = h @ a_l
        ar = h @ a_r
        e = jnp.exp(-jax.nn.leaky_relu(al[src] + ar[dst], negative_slope=NEG_SLOPE))
        rowsum = jax.ops.segment_sum(e, src, num_segments=N)
        h_prime = jax.ops.segment_sum(e[:, None] * h[dst], src, num_segments=N)
        h_prime = h_prime / (rowsum[:, None] + EPS)
        return jax.nn.elu(h_prime)

    def _L0_mix_ref(x, proj_mat, wq, bq, wk, bk, wv, bv, wo, bo, ln1_g, ln1_b, w1, b1, w2, b2, ln2_g, ln2_b):
        import jax, jax.numpy as jnp
        import numpy as np
        import math
        D_MODEL = 1024
        N_HEAD = 16
        D_HEAD = D_MODEL // N_HEAD
        D_KMAP = 128
        D_INNER = 512

        def _layer_norm(x, g, b, eps=1e-05):
            mu = jnp.mean(x, axis=-1, keepdims=True)
            var = jnp.mean(jnp.square(x - mu), axis=-1, keepdims=True)
            return (x - mu) * jax.lax.rsqrt(var + eps) * g + b

        def _fourier_kernel(x, proj_mat):
            p = jnp.einsum('blhd,dm->blhm', x, proj_mat) / math.sqrt(D_HEAD)
            return jnp.concatenate([jnp.cos(p), jnp.sin(p)], axis=-1) / math.sqrt(D_KMAP)
        B, L, _ = x.shape
        x2 = _layer_norm(x, ln1_g, ln1_b)
        q = (x2 @ wq + bq).reshape(B, L, N_HEAD, D_HEAD)
        k = (x2 @ wk + bk).reshape(B, L, N_HEAD, D_HEAD)
        v = (x2 @ wv + bv).reshape(B, L, N_HEAD, D_HEAD)
        qp = _fourier_kernel(q, proj_mat)
        kp = _fourier_kernel(k, proj_mat)
        kv = jnp.einsum('blhm,blhd->bhmd', kp, v)
        attn = jnp.einsum('blhm,bhmd->blhd', qp, kv)
        attn = attn.reshape(B, L, D_MODEL) @ wo + bo
        x = x + attn
        x2 = _layer_norm(x, ln2_g, ln2_b)
        h = jax.nn.relu(x2 @ w1 + b1)
        x = x + (h @ w2 + b2)
        return x

    def _L0_ffn_ref(x, w_gate, w_up, w_down):
        import jax, jax.numpy as jnp
        import numpy as np
        HIDDEN = 1024
        INNER = 512

        def _weight_quant(w):
            scale = 1.0 / jnp.clip(jnp.mean(jnp.abs(w)), 1e-05)
            wq = jnp.clip(jnp.round(w * scale), -1.0, 1.0) / scale
            return w + jax.lax.stop_gradient(wq - w)

        def _act_quant(x):
            scale = 127.0 / jnp.clip(jnp.max(jnp.abs(x), axis=-1, keepdims=True), 1e-05)
            xq = jnp.clip(jnp.round(x * scale), -128.0, 127.0) / scale
            return x + jax.lax.stop_gradient(xq - x)

        def _bitlinear(x, w):
            return jnp.einsum('bsi,oi->bso', _act_quant(x), _weight_quant(w))
        gate = jax.nn.silu(_bitlinear(x, w_gate))
        up = _bitlinear(x, w_up)
        return _bitlinear(gate * up, w_down)
    xn = _layernorm(x, axis=-1)
    x = x + _L0_gnn_ref(xn, L0_gnn_W, L0_gnn_a, src, dst) + _L0_mix_ref(xn[None], L0_mix_proj_mat, L0_mix_wq, L0_mix_bq, L0_mix_wk, L0_mix_bk, L0_mix_wv, L0_mix_bv, L0_mix_wo, L0_mix_bo, L0_mix_ln1_g, L0_mix_ln1_b, L0_mix_w1, L0_mix_b1, L0_mix_w2, L0_mix_b2, L0_mix_ln2_g, L0_mix_ln2_b)[0]
    x = x + _L0_ffn_ref(_layernorm(x, axis=-1)[None], L0_ffn_w_gate, L0_ffn_w_up, L0_ffn_w_down)[0]
    return x

_drawn_inputs = setup_inputs


def setup_inputs(seed=0):
    import zlib

    import numpy as np

    out = dict(_drawn_inputs(seed))
    spreads = {'L0_mix_bq': (0.0, 0.732),
     'L0_mix_bk': (0.0, 0.735),
     'L0_mix_bv': (0.0, 0.1),
     'L0_mix_bo': (0.0, 0.8),
     'L0_mix_ln1_g': (1.0, 0.2),
     'L0_mix_ln1_b': (0.0, 0.1),
     'L0_mix_b1': (0.0, 0.8),
     'L0_mix_b2': (0.0, 0.8),
     'L0_mix_ln2_g': (1.0, 0.6),
     'L0_mix_ln2_b': (0.0, 0.8)}
    factors = {'L0_gnn_W': 8.0,
     'L0_gnn_a': 8.0,
     'L0_mix_wk': 2.881,
     'L0_mix_w1': 8.0,
     'L0_mix_w2': 8.0,
     'L0_ffn_w_gate': 8.0,
     'L0_ffn_w_up': 8.0,
     'L0_ffn_w_down': 8.0}
    for name, (base, spread) in spreads.items():
        noise = np.random.default_rng([zlib.crc32(name.encode()), seed]).standard_normal(out[name].shape)
        drawn = base * np.exp(spread * noise) if base else spread * noise
        out[name] = jnp.asarray(drawn.astype(out[name].dtype))
    for name, factor in factors.items():
        out[name] = (out[name] * factor).astype(out[name].dtype)
    return out
```

```python
from contextlib import ExitStack

import concourse.bass as bass
from concourse import mybir

ALU = mybir.AluOpType
ACT = mybir.ActivationFunctionType
AX = mybir.AxisListType
F32 = mybir.dt.float32
F32R = mybir.dt.float32r
BF16 = mybir.dt.bfloat16
FP16 = mybir.dt.float16
I32 = mybir.dt.int32
U16 = mybir.dt.uint16

N, D = 1250, 1024
E = 20000
T = 125
NT = N // T
K8 = D // 128
C = 4
GROUP = C * T
NG = E // GROUP
FF = 512
HEADS, DH, KMAP = 16, 64, 128
PAIRS = HEADS // 2
LN_EPS = 1e-5
GNN_EPS = 1e-5
SLOPE = 0.1
FLT_MAX = 3.4028234e38
MAGIC = 12582912.0
TWO_PI = 6.2831850051879883
HALF_PI = 1.5707963267948966
THIRDS = [(0, 418), (418, 416), (834, 416)]
H_EXT = D + 2
H_COLS = H_EXT // 3


def f32(ap):
    return ap.bitcast(F32)


class Core:

    def __init__(self, nc, stack, inputs, out):
        self.nc, self.stack, self.inp, self.out = nc, stack, inputs, out
        self.sems = []
        self.waits_passed = nc.alloc_semaphore(name="waits_passed")

    def passed(self, engine):
        engine.sem_inc(self.waits_passed, 1)

    def sem(self, name):
        self.sems.append(self.nc.alloc_semaphore(name=name))
        return self.sems[-1]

    def renew_semaphores(self):
        self.nc.clear_and_free_semaphores(self.sems)
        self.nc.all_engine_barrier()
        self.sems = []

    def keep(self, name, shape, dt):
        return self.stack.enter_context(self.nc.sbuf_tensor(name, shape, dt))


def spread(vector, rows):
    return vector.rearrange("(a n) -> a n", a=1).to_broadcast([rows, vector.shape[0]])


def count_edges(core, w_hi, w_lo):
    nc, inp = core.nc, core.inp
    x, W = inp["x"], inp["L0_gnn_W"]
    with ExitStack() as ctx:
        def sb(name, shape, dt):
            return ctx.enter_context(nc.sbuf_tensor(name, shape, dt))

        def ps(name, shape, dt=F32):
            return ctx.enter_context(nc.psum_tensor(name, shape, dt))

        edges_i = sb("edges_i", [NG, 2, GROUP], I32)
        edges_f = sb("edges_f", [NG, 2, GROUP], F32)
        bounds = sb("bounds", [NG, 2], F32)
        ends = sb("ends", [T, NG, 2 * C], F32)
        now = sb("now", [T, 2 * C], F32)
        iota_i = sb("iota_i", [T, N], I32)
        iota_h = sb("iota_h", [T, N], FP16)
        tab_i = sb("tab_i", [1, 3, NT, NG], I32)
        tab = sb("tab", [1, 3, NT, NG], F32)
        hit = sb("hit", [1, 3, NT, NG], F32)
        row2 = sb("row2", [1, 2, NG], F32)
        span = sb("span", [1, 4, NT], F32)
        span_i = sb("span_i", [1, 2, NT], I32)
        iota_t = sb("iota_t", [T, T], FP16)
        hot_s = sb("hot_s", [T, C, N], BF16)
        hot_d = sb("hot_d", [T, C, T], BF16)
        zeros = sb("zeros", [T, T], BF16)
        zero_rows = sb("zero_rows", [T, 418], BF16)
        x_in = sb("x_in", [T, 2, D], F32)
        junk = sb("junk", [T, D], F32)
        w_in = sb("w_in", [128, 2, D], F32)

        f_in = sb("f_in", [128, 2, FF * D // 128], F32)
        below = sb("below", [128, FF * D // 128], BF16)
        ternary = sb("ternary_out", [128, FF * D // 128], BF16)
        ones = sb("ones", [128, 128], F32)
        mag = sb("magnitude_sums", [128, 3], F32)
        w_scale = sb("w_scale", [128, 3], F32)

        p_ends = ps("p_ends", [128, 512])
        p_bound = ps("p_bound", [128, 512])
        p_cnt = ps("p_cnt", [128, 2, 3, 512])

        s_edges = core.sem("edges_loaded")
        s_efl = core.sem("edges_as_floats")
        s_prep = core.sem("edge_tables_step")
        s_ident = core.ident_ready
        s_iota = core.sem("iotas_written")
        s_iotah = core.sem("iota_half_ready")
        s_tr = core.sem("edge_transposes_done")
        s_span = core.sem("spans_ready")
        s_step = core.sem("span_step")
        s_now = core.sem("group_at_hand")
        s_hot = core.sem("onehots_ready")
        s_used = core.sem("onehot_slots_free")
        s_zero = core.sem("zero_operands_ready")
        s_tile = core.sem("tile_counted")
        s_kept = core.sem("counts_kept")
        s_x = [core.sem(f"x_loaded{i}") for i in range(2)]
        s_xfree = core.sem("x_summed")
        s_chain = core.sem("stat_step")
        s_w = [core.sem(f"w_loaded{i}") for i in range(2)]
        s_whi = core.sem("w_hi_done")
        s_wlo = core.sem("w_lo_done")

        s_fin = [core.sem(f"feed_forward_weight_loaded{i}") for i in range(2)]
        s_again = core.sem("up_loaded_again")
        s_mag = core.sem("magnitudes_summed")
        s_tot = core.sem("magnitudes_totalled")
        s_sc = core.sem("weight_scale_step")
        s_tern = core.sem("ternary_step")
        s_ones = core.sem("ones_written1")
        s_tst = core.sem("ternary_stored")

        block = ctx.enter_context(nc.Block())
        GATE, UP, DOWN = 0, 1, 2

        def ffn_weight(n):
            w = (inp["L0_ffn_w_gate"], inp["L0_ffn_w_up"], inp["L0_ffn_w_down"])[n]
            return w.rearrange("(a p) n -> p a n", p=128)

        def in_slot(slot, n):
            return f_in[:, slot, :].rearrange("p (a n) -> p a n", a=8 if n == DOWN else 4)

        LOADS = [(GATE, 0), (UP, 1), (DOWN, 0), (GATE, 1)]

        @block.sync
        def _(sp):
            sp.dma_start(edges_i[:, 0, :], inp["src"].rearrange("(g e) -> g e", g=NG)).then_inc(s_edges, 16)
            sp.dma_start(edges_i[:, 1, :], inp["dst"].rearrange("(g e) -> g e", g=NG)).then_inc(s_edges, 16)
            for n, slot in LOADS:
                if n != GATE and slot == 0:
                    sp.wait_ge(s_mag, 1)
                if n == GATE and slot == 1:
                    sp.wait_ge(s_mag, 2)
                sp.dma_start(in_slot(slot, n), ffn_weight(n)).then_inc(s_fin[slot], 16)
            for k in range(K8):
                if k >= 2:
                    sp.wait_ge(s_wlo, k - 1)
                sp.dma_start(w_in[:, k % 2, :], W[k * 128:(k + 1) * 128, :]).then_inc(s_w[k % 2], 16)

            for p in range(2):
                sp.dma_start(x_in[:, p, :], x[p * T:(p + 1) * T, :]).then_inc(s_x[p], 16)
            with sp.Fori(2, NT - 1, 2) as i:
                for p in range(2):
                    sp.wait_ge(s_xfree, i + p - 1)
                    sp.dma_start(x_in[:, p, :], x[bass.ds((i + p) * T, T), :]).then_inc(s_x[p], 16)

        @block.gpsimd
        def _(pool):
            pool.memset(core.ident[:], 0.0).then_inc(s_prep, 1)
            pool.memset(zeros[:], 0.0).then_inc(s_zero, 1)
            pool.memset(zero_rows[:], 0.0).then_inc(s_zero, 1)
            pool.memset(ones[:], 1.0).then_inc(s_ones, 1)
            pool.iota(tab_i[:, 0, :, :], pattern=[[T, NT], [0, NG]], base=0, channel_multiplier=0).then_inc(s_iota, 1)
            pool.iota(tab_i[:, 1, :, :], pattern=[[T, NT], [0, NG]], base=T, channel_multiplier=0).then_inc(s_iota, 1)
            pool.iota(tab_i[:, 2, :, :], pattern=[[0, NT], [1, NG]], base=-NG, channel_multiplier=0).then_inc(s_iota, 1)
            pool.iota(iota_i[:], pattern=[[1, N]], base=0, channel_multiplier=0).then_inc(s_iota, 1)
            pool.wait_ge(s_prep, 1)
            pool.affine_select(out=core.ident[:], in_=core.ident[:], compare_op=ALU.not_equal, fill=1.0,
                               base=0, pattern=[[-1, 128]], channel_multiplier=1).then_inc(s_ident, 1)
            for k in range(K8):
                pool.wait_ge(s_whi, k + 1)
                pool.tensor_tensor(w_lo[:, k, :], w_in[:, k % 2, :], f32(w_hi[:, k, :]), ALU.subtract).then_inc(s_wlo, 1)
            pool.wait_ge(s_sc, 2)
            for step, (n, slot, s_in, loads) in enumerate(((DOWN, 0, s_fin[0], 2), (GATE, 1, s_fin[1], 2), (UP, 0, s_again, 1))):
                pool.wait_ge(s_in, 16 * loads)
                pool.tensor_scalar(f_in[:, slot, :], f_in[:, slot, :], w_scale[:, n:n + 1], None, ALU.mult).then_inc(s_tern, 1)
                pool.wait_ge(s_tern, 3 * step + 1)
                pool.tensor_scalar(below[:], f_in[:, slot, :], -0.5, None, ALU.is_lt)
                pool.wait_ge(s_tst, 16 * step)
                pool.tensor_scalar(ternary[:], f_in[:, slot, :], 0.5, None, ALU.is_gt).then_inc(s_tern, 1)
                pool.wait_ge(s_tern, 3 * step + 2)
                pool.tensor_tensor(ternary[:], ternary[:], below[:], ALU.subtract).then_inc(s_tern, 1)
                pool.wait_ge(s_tern, 3 * step + 3)
                if n == DOWN:
                    pool.dma_start(in_slot(0, UP), ffn_weight(UP)).then_inc(s_again, 16)
                pool.dma_start(core.ternary_dram[n], ternary[:]).then_inc(s_tst, 16)
            pool.wait_ge(s_tst, 48)

        @block.scalar
        def _(act):
            def split_w(k):
                act.wait_ge(s_w[k % 2], 16 * (k // 2 + 1))
                act.activation(w_hi[:, k, :], w_in[:, k % 2, :], ACT.Copy).then_inc(s_whi, 1)

            for n, slot, loads in ((GATE, 0, 1), (UP, 1, 1), (DOWN, 0, 2)):
                act.wait_ge(s_fin[slot], 16 * loads)
                act.wait_ge(s_mag, n)
                act.activation(below[:], f_in[:, slot, :], ACT.Abs, accum_out=mag[:, n:n + 1]).then_inc(s_mag, 1)
            for k in range(K8):
                split_w(k)

            def sums(t, slot):
                act.wait_ge(s_x[slot], 16 + 8 * (t - slot))
                mean, var, col = core.mean, core.var, bass.ds(t, 1)
                act.activation(junk[:], x_in[:, slot, :], ACT.Identity, accum_out=mean[:, col]).then_inc(s_chain, 1)
                act.wait_ge(s_chain, 1 + 3 * t)
                act.mul(core.negmean[:, col], mean[:, col], -1.0 / D).then_inc(s_chain, 1)
                act.wait_ge(s_chain, 2 + 3 * t)
                act.activation(junk[:], x_in[:, slot, :], ACT.Square, bias=core.negmean[:, col],
                               accum_out=var[:, col]).then_inc(s_chain, 1)
                act.wait_ge(s_chain, 3 + 3 * t)
                act.sem_inc(s_xfree, 1)

            def keep_counts(t, par):
                act.wait_ge(s_tile, t + 1)
                for n, (a, w) in enumerate(THIRDS):
                    last = act.activation(core.counts[:, bass.ds(t, 1), a:a + w], p_cnt[0:T, par, n:n + 1, 0:w], ACT.Copy)
                last.then_inc(s_kept, 1)

            with act.Fori(0, NT - 1, 2) as i:
                for p in range(2):
                    sums(i + p, p)
                    keep_counts(i + p, p)

        @block.vector
        def _(dve):
            dve.wait_ge(s_edges, 32)
            dve.tensor_copy(edges_f[:], edges_i[:]).then_inc(s_efl, 1)
            dve.wait_ge(s_efl, 1)
            dve.tensor_reduce(bounds[:, 0:1], edges_f[:, 1, :], AX.X, ALU.min).then_inc(s_efl, 1)
            dve.tensor_reduce(bounds[:, 1:2], edges_f[:, 1, :], AX.X, ALU.max).then_inc(s_efl, 1)
            dve.wait_ge(s_iota, 4)
            dve.tensor_copy(iota_h[:], iota_i[:]).then_inc(s_iotah, 1)
            dve.tensor_copy(tab[:], tab_i[:]).then_inc(s_iotah, 1)
            dve.wait_ge(s_tr, 1)
            dve.tensor_copy(ends[:], p_ends[0:T, 0:2 * C * NG].rearrange("p (a g) -> p g a", a=2 * C)).then_inc(s_iotah, 1)
            dve.tensor_copy(row2[:], p_bound[0:1, 0:2 * NG].rearrange("p (a g) -> p a g", a=2)).then_inc(s_iotah, 1)
            dve.wait_ge(s_iotah, 4)
            least = row2[:, 0:1, :].to_broadcast([1, NT, NG])
            most = row2[:, 1:2, :].to_broadcast([1, NT, NG])
            step = [0]

            def chain(ins):
                step[0] += 1
                ins.then_inc(s_step, 1)
                dve.wait_ge(s_step, step[0])

            chain(dve.tensor_tensor(hit[:, 0], least, tab[:, 1], ALU.is_lt))
            chain(dve.tensor_tensor(hit[:, 1], most, tab[:, 0], ALU.is_ge))
            chain(dve.tensor_tensor(hit[:, 0], hit[:, 0], hit[:, 1], ALU.mult))
            chain(dve.tensor_tensor(hit[:, 1], hit[:, 0], tab[:, 2], ALU.mult))
            chain(dve.tensor_reduce(span[:, 0], hit[:, 1], AX.X, ALU.min))
            chain(dve.tensor_scalar(span[:, 0], span[:, 0], float(NG), float(NG - 1), ALU.add, ALU.min))
            chain(dve.tensor_scalar(hit[:, 2], tab[:, 2], float(NG + 1), None, ALU.add))
            chain(dve.tensor_tensor(hit[:, 1], hit[:, 0], hit[:, 2], ALU.mult))
            chain(dve.tensor_reduce(span[:, 1], hit[:, 1], AX.X, ALU.max))
            chain(dve.tensor_scalar(span[:, 2], span[:, 0], 1.0, None, ALU.add))
            chain(dve.tensor_tensor(span[:, 3], span[:, 1], span[:, 2], ALU.max))
            chain(dve.tensor_copy(span_i[:, 0], span[:, 0]))
            dve.tensor_copy(span_i[:, 1], span[:, 3]).then_inc(s_span, 1)
            dve.wait_ge(s_span, 1)

            def onehots(chunks):
                for j in range(C):
                    if j % 2 == 0:
                        dve.wait_ge(s_used, chunks + j + 2)
                    dve.tensor_scalar(hot_s[:, j, :], iota_h[:], now[:, j:j + 1], None, ALU.is_equal)
                    dve.tensor_scalar(hot_d[:, j, :], iota_t[:], now[:, C + j:C + j + 1], None,
                                      ALU.is_equal).then_inc(s_hot, 1)

            with dve.register("chunks_done") as done, dve.register("copies_made") as copies:
                dve.reg_mov(done, 0)
                dve.reg_mov(copies, 0)
                def tile_onehots(t):
                    dve.wait_ge(s_hot, dve.snap(done, min_val=0, max_val=NT * NG * C))
                    dve.tensor_copy(iota_t[:], iota_h[:, bass.ds(t * T, T)]).then_inc(s_now, 1)
                    dve.reg_add(copies, copies, 1)
                    first = dve.value_load(span_i[0:1, 0, bass.ds(t, 1)], min_val=0, max_val=NG - 1)
                    past = dve.value_load(span_i[0:1, 1, bass.ds(t, 1)], min_val=1, max_val=NG)
                    with dve.Fori(first, past) as g:
                        before = dve.snap(done, min_val=0, max_val=NT * NG * C)
                        dve.wait_ge(s_hot, before)
                        dve.tensor_copy(now[:], ends[:, bass.ds(g, 1), :].rearrange("p a c -> p (a c)")).then_inc(s_now, 1)
                        dve.reg_add(copies, copies, 1)
                        dve.wait_ge(s_now, dve.snap(copies, min_val=0, max_val=NT * (NG + 1)))
                        onehots(before)
                        dve.reg_add(done, done, C)

                with dve.Fori(0, 2) as t:
                    tile_onehots(t)
                dve.wait_ge(s_tot, 1)
                dve.tensor_scalar(core.w_mean[:], p_bound[:, 0:3], 1.0 / (FF * D), 1e-5, ALU.mult, ALU.max).then_inc(s_sc, 1)
                dve.wait_ge(s_sc, 1)
                dve.reciprocal(w_scale[:], core.w_mean[:]).then_inc(s_sc, 1)
                with dve.Fori(2, NT) as t:
                    tile_onehots(t)

        @block.tensor
        def _(pe):
            pe.wait_ge(s_ident, 1)
            pe.wait_ge(s_efl, 3)
            ident = core.ident
            for a in range(2 * C):
                pe.transpose(p_ends[0:T, a * NG:(a + 1) * NG], edges_f[:, a // C, (a % C) * T:(a % C + 1) * T],
                             ident[0:NG, 0:NG])
            for a in range(2):
                last = pe.transpose(p_bound[0:1, a * NG:(a + 1) * NG], bounds[:, a:a + 1], ident[0:NG, 0:NG])
            last.then_inc(s_tr, 1)
            pe.sem_inc(s_used, C)
            pe.wait_ge(s_zero, 2)
            pe.wait_ge(s_span, 1)

            def count_tile(t, par, done):
                for n, (a, w) in enumerate(THIRDS):
                    pe.matmul(p_cnt[0:T, par, n, 0:w], zeros[:], zero_rows[:, 0:w], start=True, stop=False)
                first = pe.value_load(span_i[0:1, 0, bass.ds(t, 1)], min_val=0, max_val=NG - 1)
                past = pe.value_load(span_i[0:1, 1, bass.ds(t, 1)], min_val=1, max_val=NG)
                with pe.Fori(first, past):
                    before = pe.snap(done, min_val=0, max_val=NT * NG * C)
                    for j in range(C):
                        pe.wait_ge(s_hot, before + j + 1)
                        for n, (a, w) in enumerate(THIRDS):
                            last = pe.matmul(p_cnt[0:T, par, n, 0:w], hot_d[:, j, :], hot_s[:, j, a:a + w],
                                             start=False, stop=False)
                        last.then_inc(s_used, 1)
                    pe.reg_add(done, done, C)
                for n, (a, w) in enumerate(THIRDS):
                    last = pe.matmul(p_cnt[0:T, par, n, 0:w], zeros[:], zero_rows[:, 0:w], start=False, stop=True)
                last.then_inc(s_tile, 1)

            with pe.register("chunks_done") as done:
                pe.reg_mov(done, 0)
                for par in range(2):
                    count_tile(par, par, done)
                pe.wait_ge(s_mag, 3)
                pe.wait_ge(s_ones, 1)
                pe.matmul(p_bound[:, 0:3], ones[:], mag[:], start=True, stop=True).then_inc(s_tot, 1)
                with pe.Fori(2, NT - 1, 2) as i:
                    for par in range(2):
                        pe.wait_ge(s_kept, i + par - 1)
                        count_tile(i + par, par, done)


def node_features(core, w_hi, w_lo):
    nc, inp = core.nc, core.inp
    x = inp["x"]
    h_hi, h_lo = core.h_hi, core.h_lo
    with ExitStack() as ctx:
        def sb(name, shape, dt):
            return ctx.enter_context(nc.sbuf_tensor(name, shape, dt))

        def ps(name, shape, dt=F32):
            return ctx.enter_context(nc.psum_tensor(name, shape, dt))

        x_in = sb("x_in2", [T, 2, D], F32)
        xn = sb("xn", [T, D], F32)
        xt_hi = sb("xt_hi", [128, 2, K8, T], F32R)
        xt_lo = sb("xt_lo", [128, 2, K8, T], F32R)
        a_lr = sb("a_lr", [T, 2 * D], F32)
        p_tr = ps("p_tr", [128, 2, 512])
        p_h = ps("p_h", [128, 2, 2, 512])
        p_junk = ps("p_junk", [128, 2, 512])

        s_a = core.sem("a_loaded")
        s_x = [core.sem(f"x2_loaded{i}") for i in range(2)]
        s_step = core.sem("rstd_step")
        s_ones = core.sem("h_ones_written")
        s_xn = core.sem("xn_ready")
        s_tr = core.sem("xn_transposed")
        s_thi = core.sem("xt_hi_ready")
        s_tlo = core.sem("xt_lo_ready")
        s_h = core.sem("h_product_done")
        s_hhi = core.sem("h_hi_kept")
        s_hdone = core.sem("h_psum_free")
        s_dot = core.sem("dot_products_done")

        block = ctx.enter_context(nc.Block())

        @block.sync
        def _(sp):
            def load(i, slot):
                sp.dma_start(x_in[:, slot, :], x[bass.ds(i * T, T), :]).then_inc(s_x[slot], 16)

            for i in range(2):
                load(i, i)
            sp.dma_start(a_lr[:], inp["L0_gnn_a"].to_broadcast([T, 2 * D])).then_inc(s_a, 16)
            with sp.Fori(2, NT - 1, 2) as i:
                for p in range(2):
                    sp.wait_ge(s_xn, i + p - 1)
                    load(i + p, p)

        @block.gpsimd
        def _(pool):
            pool.memset(f32(h_hi[:, :, D:D + 1]), 1.0).then_inc(s_ones, 1)
            pool.memset(f32(h_hi[:, :, D + 1:]), 0.0).then_inc(s_ones, 1)
            pool.memset(f32(h_lo[:, :, D:]), 0.0).then_inc(s_ones, 1)
            pool.wait_ge(s_ones, 3)

        @block.scalar
        def _(act):
            act.wait_ge(s_step, 1)
            act.activation(core.root[:], core.var[:], ACT.Sqrt).then_inc(s_step, 1)

            def keep_xt_hi(i, slot, reuse=True):
                act.wait_ge(s_tr, i + 1)
                if reuse:
                    act.wait_ge(s_h, i - 1)
                act.activation(xt_hi[:, slot].rearrange("p (a k) t -> p a (k t)", a=2), p_tr[:, :, 0:4 * T],
                               ACT.Copy).then_inc(s_thi, 1)

            def keep_h_hi(i, slot):
                act.wait_ge(s_h, i + 1)
                act.activation(h_hi[:, bass.ds(i, 1), 0:D], p_h[0:T, slot], ACT.Copy).then_inc(s_hhi, 1)

            keep_xt_hi(0, 0, reuse=False)
            with act.Fori(1, NT - 2, 2) as i:
                for p in range(2):
                    keep_xt_hi(i + p, 1 - p)
                    keep_h_hi(i + p - 1, p)
            keep_xt_hi(NT - 1, 1)
            keep_h_hi(NT - 2, 0)
            keep_h_hi(NT - 1, 1)

        @block.vector
        def _(dve):
            mean, var, root, rstd, tmp = core.negmean, core.var, core.root, core.rstd, core.tmp
            dve.tensor_scalar(var[:], var[:], 1.0 / D, LN_EPS, ALU.mult, ALU.add).then_inc(s_step, 1)
            dve.wait_ge(s_step, 2)
            dve.reciprocal(tmp[:], root[:]).then_inc(s_step, 1)
            dve.wait_ge(s_step, 3)
            dve.tensor_tensor(root[:], var[:], tmp[:], ALU.mult).then_inc(s_step, 1)
            dve.wait_ge(s_step, 4)
            dve.tensor_tensor(var[:], root[:], tmp[:], ALU.mult).then_inc(s_step, 1)
            dve.wait_ge(s_step, 5)
            dve.tensor_scalar(root[:], var[:], -0.5, 1.5, ALU.mult, ALU.add).then_inc(s_step, 1)
            dve.wait_ge(s_step, 6)
            dve.tensor_tensor(rstd[:], root[:], tmp[:], ALU.mult).then_inc(s_step, 1)
            dve.wait_ge(s_step, 7)

            def normalise(i, slot, first=False):
                dve.wait_ge(s_x[slot], 16 + 8 * (i - slot))
                if not first:
                    dve.wait_ge(s_tr, i)
                dve.tensor_scalar(xn[:], x_in[:, slot, :], mean[:, bass.ds(i, 1)], rstd[:, bass.ds(i, 1)],
                                  ALU.add, ALU.mult).then_inc(s_xn, 1)

            def keep_xt_lo(i, slot):
                dve.wait_ge(s_thi, i + 1)
                dve.tensor_tensor(xt_lo[:, slot].rearrange("p (a k) t -> p a (k t)", a=2), p_tr[:, :, 0:4 * T],
                                  f32(xt_hi[:, slot]).rearrange("p (a k) t -> p a (k t)", a=2),
                                  ALU.subtract).then_inc(s_tlo, 1)

            def keep_h(i, slot):
                dve.wait_ge(s_hhi, i + 1)
                dve.tensor_tensor(h_lo[:, bass.ds(i, 1), 0:D].rearrange("p a (b n) -> p (a b) n", b=2), p_h[0:T, slot],
                                  f32(h_hi[:, bass.ds(i, 1), 0:D]).rearrange("p a (b n) -> p (a b) n", b=2), ALU.subtract)
                for n, dot in enumerate((core.al, core.ar)):
                    dve.wait_ge(s_dot, 2 * i + n)
                    last = dve.scalar_tensor_tensor(
                        p_junk[0:T], p_h[0:T, slot], 1.0, a_lr[:, n * D:(n + 1) * D].rearrange("p (b n) -> p b n", b=2),
                        ALU.mult, ALU.mult, accum_out=dot[:, bass.ds(i, 1)])
                    last.then_inc(s_dot, 1)
                dve.wait_ge(s_dot, 2 * i + 2)
                dve.sem_inc(s_hdone, 1)

            normalise(0, 0, first=True)
            keep_xt_lo(0, 0)
            normalise(1, 1)
            dve.wait_ge(s_a, 16)
            with dve.Fori(1, NT - 2, 2) as i:
                for p in range(2):
                    keep_xt_lo(i + p, 1 - p)
                    normalise(i + p + 1, p)
                    keep_h(i + p - 1, p)
            keep_xt_lo(NT - 1, 1)
            keep_h(NT - 2, 0)
            keep_h(NT - 1, 1)

        @block.tensor
        def _(pe):
            def transposes(i, first=False):
                pe.wait_ge(s_xn, i + 1)
                if not first:
                    pe.wait_ge(s_tlo, i)
                for k in range(K8):
                    last = pe.transpose(p_tr[:, k // 4, (k % 4) * T:(k % 4 + 1) * T], xn[:, k * 128:(k + 1) * 128],
                                        core.ident[0:T, 0:T])
                last.then_inc(s_tr, 1)

            def products(i, slot, reuse=True):
                pe.wait_ge(s_tlo, i + 1)
                if reuse:
                    pe.wait_ge(s_hdone, i - 1)
                for n in range(2):
                    cols = slice(n * 512, (n + 1) * 512)
                    for k in range(K8):
                        for m, (left, right) in enumerate(((xt_lo, w_hi), (xt_hi, w_lo), (xt_hi, w_hi))):
                            last = pe.matmul(p_h[0:T, slot, n, :], left[:, slot, k, :], right[:, k, cols],
                                             start=(k == 0 and m == 0), stop=(k == K8 - 1 and m == 2))
                last.then_inc(s_h, 1)

            transposes(0, first=True)
            transposes(1)
            products(0, 0, reuse=False)
            with pe.Fori(1, NT - 2, 2) as i:
                for p in range(2):
                    transposes(i + p + 1)
                    products(i + p, 1 - p)
            products(NT - 1, 1)


def inverse_root(dve, s_step, at, var, root, tmp, rstd):
    dve.wait_ge(s_step, at)
    dve.reciprocal(tmp, root).then_inc(s_step, 1)
    dve.wait_ge(s_step, at + 1)
    dve.tensor_tensor(root, var, tmp, ALU.mult).then_inc(s_step, 1)
    dve.wait_ge(s_step, at + 2)
    dve.tensor_tensor(var, root, tmp, ALU.mult).then_inc(s_step, 1)
    dve.wait_ge(s_step, at + 3)
    dve.tensor_scalar(root, var, -0.5, 1.5, ALU.mult, ALU.add).then_inc(s_step, 1)
    dve.wait_ge(s_step, at + 4)
    dve.tensor_tensor(rstd, root, tmp, ALU.mult).then_inc(s_step, 1)
    dve.wait_ge(s_step, at + 5)


def attend_over_edges(core):
    nc, inp = core.nc, core.inp
    x, h_hi, h_lo, counts = inp["x"], core.h_hi, core.h_lo, core.counts
    with ExitStack() as ctx:
        def sb(name, shape, dt=F32):
            return ctx.enter_context(nc.sbuf_tensor(name, shape, dt))

        al_all = sb("al_all", [T, N])
        z = sb("z", [T, 2, NT, T])
        y = sb("y", [T, 2, NT, T])
        a_hi = sb("a_hi", [T, 2, NT, T], F32R)
        a_lo = sb("a_lo", [T, 2, NT, T], F32R)
        x_in = sb("x_in3", [T, 2, D])
        low = sb("low", [T, 3, H_COLS])
        high = sb("high", [T, 3, H_COLS])
        elu = sb("elu", [T, 3, H_COLS])
        gnn = sb("gnn", [T, 2, D])
        junk = sb("junk3", [T, D])
        rsum = sb("rsum", [T, 2])
        nb = sb("nb", [T, NT])
        nb2 = sb("nb2", [T, NT])
        sum2 = sb("sum2", [T, NT])
        nmean2 = sb("nmean2", [T, NT])
        p_o = ctx.enter_context(nc.psum_tensor("p_o", [128, 2, 3, 512], F32))

        s_al = core.sem("al_spread_in_psum")
        s_alk = core.sem("al_spread_kept")
        s_nb = core.sem("nb_ready")
        s_z = core.sem("scores_ready")
        s_y = core.sem("leaky_ready")
        s_e = core.sem("edge_exp_ready")
        s_a = core.sem("edge_weights_ready")
        s_ahi = core.sem("a_hi_ready")
        s_alo = core.sem("a_lo_ready")
        s_o = core.sem("attended_in_psum")
        s_rs = core.sem("row_sum_step")
        s_m = core.sem("below_zero_ready")
        s_em = core.sem("below_zero_exp")
        s_hp = core.sem("above_zero_ready")
        s_elu = core.sem("elu_ready")
        s_gnn = core.sem("gnn_tile_ready")
        s_stat = core.sem("second_stat_step")
        s_x = [core.sem(f"x3_loaded{i}") for i in range(2)]
        s_st = [core.sem(f"gnn_stored{i}") for i in range(2)]
        s_step = core.sem("rstd2_step")

        block = ctx.enter_context(nc.Block())

        @block.sync
        def _(sp):
            for p in range(2):
                sp.dma_start(x_in[:, p, :], x[p * T:(p + 1) * T, :]).then_inc(s_x[p], 16)

            def store(i, slot):
                sp.wait_ge(s_gnn, i + 1)
                sp.dma_start(core.gnn_dram[bass.ds(i * T, T), :], gnn[:, slot, :]).then_inc(s_st[slot], 16)

            with sp.Fori(2, NT - 1, 2) as i:
                for p in range(2):
                    store(i + p - 2, p)
                    sp.wait_ge(s_stat, 4 * (i + p) - 4)
                    sp.dma_start(x_in[:, p, :], x[bass.ds((i + p) * T, T), :]).then_inc(s_x[p], 16)
            for i in range(NT - 2, NT):
                store(i, i % 2)
            for p in range(2):
                sp.wait_ge(s_st[p], 16 * NT // 2)

        @block.gpsimd
        def _(pool):
            def weights_lo(i, slot):
                pool.wait_ge(s_ahi, i + 1)
                pool.tensor_tensor(a_lo[:, slot], z[:, slot], f32(a_hi[:, slot]), ALU.subtract).then_inc(s_alo, 1)

            def add_x(i, slot, reuse=True):
                pool.wait_ge(s_elu, i + 1)
                if reuse:
                    pool.wait_ge(s_st[slot], 8 * (i - slot))
                pool.tensor_tensor(gnn[:, slot, :], elu[:].rearrange("p a n -> p (a n)")[:, 0:D], x_in[:, slot, :],
                                   ALU.add).then_inc(s_gnn, 1)

            weights_lo(0, 0)
            weights_lo(1, 1)
            add_x(0, 0, reuse=False)
            weights_lo(2, 0)
            add_x(1, 1, reuse=False)
            with pool.Fori(3, NT - 1, 2) as i:
                for p in range(2):
                    weights_lo(i + p, 1 - p)
                    add_x(i + p - 1, p)
            weights_lo(NT - 1, 1)
            add_x(NT - 2, 0)
            add_x(NT - 1, 1)

        @block.scalar
        def _(act):
            act.wait_ge(s_al, 1)
            for b in range(3):
                w = min(4, NT - 4 * b) * T
                last = act.activation(al_all[:, 4 * b * T:4 * b * T + w], p_o[0:T, 1, b, 0:w], ACT.Copy)
            last.then_inc(s_alk, 1)

            def exps(i, slot):
                act.wait_ge(s_y, i + 1)
                act.activation(y[:, slot], y[:, slot], ACT.Exp, scale=-1.0).then_inc(s_e, 1)

            def weights_hi(i, slot, reuse=True):
                act.wait_ge(s_a, i + 1)
                if reuse:
                    act.wait_ge(s_o, i - 1)
                act.activation(a_hi[:, slot], z[:, slot], ACT.Copy).then_inc(s_ahi, 1)

            def stats(i, slot):
                act.wait_ge(s_x[slot], 16 + 8 * (i - slot))
                col = bass.ds(i, 1)
                act.wait_ge(s_stat, 4 * i)
                act.activation(junk[:], x_in[:, slot, :], ACT.Identity, scale=core.rstd[:, col], bias=nb[:, col],
                               accum_out=sum2[:, col]).then_inc(s_stat, 1)
                act.wait_ge(s_stat, 4 * i + 1)
                act.mul(nmean2[:, col], sum2[:, col], -1.0 / D).then_inc(s_stat, 1)
                act.wait_ge(s_stat, 4 * i + 2)
                act.activation(nb2[:, col], nmean2[:, col], ACT.Identity, bias=nb[:, col]).then_inc(s_stat, 1)
                act.wait_ge(s_stat, 4 * i + 3)
                act.activation(junk[:], x_in[:, slot, :], ACT.Square, scale=core.rstd[:, col], bias=nb2[:, col],
                               accum_out=core.var[:, col]).then_inc(s_stat, 1)

            def elu_parts(i, slot):
                act.wait_ge(s_m, i + 1)
                act.wait_ge(s_elu, i)
                act.activation(high[:], p_o[0:T, slot, :, 0:H_COLS], ACT.Relu, scale=rsum[:, 1:2]).then_inc(s_hp, 1)
                act.activation(low[:], low[:], ACT.Exp).then_inc(s_em, 1)

            exps(0, 0)
            weights_hi(0, 0, reuse=False)
            act.wait_ge(s_nb, 1)
            stats(0, 0)
            exps(1, 1)
            weights_hi(1, 1, reuse=False)
            stats(1, 1)
            elu_parts(0, 0)
            with act.Fori(2, NT - 1, 2) as i:
                for p in range(2):
                    exps(i + p, p)
                    weights_hi(i + p, p)
                    stats(i + p, p)
                    elu_parts(i + p - 1, 1 - p)
            elu_parts(NT - 1, 1)
            act.wait_ge(s_step, 1)
            act.activation(core.root[:], core.var[:], ACT.Sqrt).then_inc(s_step, 1)

        @block.vector
        def _(dve):
            dve.tensor_tensor(nb[:], core.negmean[:], core.rstd[:], ALU.mult).then_inc(s_nb, 1)
            dve.wait_ge(s_alk, 1)

            def scores(i, slot, reuse=True):
                if reuse:
                    dve.wait_ge(s_alo, i - 1)
                dve.tensor_tensor(z[:, slot], al_all[:, bass.ds(i * T, T)].rearrange("p (a s) -> p a s", a=1).to_broadcast([T, NT, T]),
                                  core.ar[:].rearrange("p (d a) -> p d a", a=1).to_broadcast([T, NT, T]), ALU.add).then_inc(s_z, 1)
                dve.wait_ge(s_z, i + 1)
                dve.scalar_tensor_tensor(y[:, slot], z[:, slot], SLOPE, z[:, slot], ALU.mult, ALU.max).then_inc(s_y, 1)

            def weights(i, slot):
                dve.wait_ge(s_e, i + 1)
                dve.scalar_tensor_tensor(z[:, slot], y[:, slot], FLT_MAX, counts[:, :, bass.ds(i * T, T)],
                                         ALU.min, ALU.mult).then_inc(s_a, 1)

            def elu_parts(i, slot):
                dve.wait_ge(s_o, i + 1)
                dve.wait_ge(s_hp, i)
                dve.tensor_scalar(rsum[:, 0:1], p_o[0:T, slot, 2, D - 2 * H_COLS:D - 2 * H_COLS + 1], GNN_EPS, None,
                                  ALU.add).then_inc(s_rs, 1)
                dve.wait_ge(s_rs, 2 * i + 1)
                dve.reciprocal(rsum[:, 1:2], rsum[:, 0:1]).then_inc(s_rs, 1)
                dve.wait_ge(s_rs, 2 * i + 2)
                dve.tensor_scalar(low[:], p_o[0:T, slot, :, 0:H_COLS], rsum[:, 1:2], 0.0, ALU.mult, ALU.min).then_inc(s_m, 1)

            def elu_sum(i):
                dve.wait_ge(s_em, i + 1)
                dve.wait_ge(s_hp, i + 1)
                dve.wait_ge(s_gnn, i)
                dve.scalar_tensor_tensor(elu[:], low[:], -1.0, high[:], ALU.add, ALU.add).then_inc(s_elu, 1)

            scores(0, 0, reuse=False)
            weights(0, 0)
            scores(1, 1, reuse=False)
            weights(1, 1)
            elu_parts(0, 0)
            elu_sum(0)
            with dve.Fori(2, NT - 1, 2) as i:
                for p in range(2):
                    scores(i + p, p)
                    weights(i + p, p)
                    elu_parts(i + p - 1, 1 - p)
                    elu_sum(i + p - 1)
            elu_parts(NT - 1, 1)
            elu_sum(NT - 1)
            dve.wait_ge(s_stat, 4 * NT)
            dve.tensor_scalar(core.var[:], core.var[:], 1.0 / D, LN_EPS, ALU.mult, ALU.add).then_inc(s_step, 1)
            inverse_root(dve, s_step, 2, core.var[:], core.root[:], core.tmp[:], core.rstd2[:])
            dve.tensor_tensor(core.ln_scale[:], core.rstd[:], core.rstd2[:], ALU.mult).then_inc(s_step, 1)
            dve.tensor_tensor(core.ln_shift[:], nb2[:], core.rstd2[:], ALU.mult).then_inc(s_step, 1)
            dve.tensor_copy(core.xn_shift[:], nb[:]).then_inc(s_step, 1)
            dve.wait_ge(s_step, 10)

        @block.tensor
        def _(pe):
            for i in range(NT):
                last = pe.matmul(p_o[0:T, 1, i // 4, (i % 4) * T:(i % 4 + 1) * T], core.al[:, i:i + 1].to_broadcast([T, T]),
                                 core.ident[0:T, 0:T], start=True, stop=True)
            last.then_inc(s_al, 1)

            def products(i, slot, reuse=True):
                pe.wait_ge(s_alo, i + 1)
                if reuse:
                    pe.wait_ge(s_em, i - 1)
                    pe.wait_ge(s_hp, i - 1)
                for n in range(3):
                    cols = slice(n * H_COLS, (n + 1) * H_COLS)
                    for d in range(NT):
                        for m, (left, right) in enumerate(((a_lo, h_hi), (a_hi, h_lo), (a_hi, h_hi))):
                            last = pe.matmul(p_o[0:T, slot, n, 0:H_COLS], left[:, slot, d, :], right[:, d, cols],
                                             start=(d == 0 and m == 0), stop=(d == NT - 1 and m == 2))
                last.then_inc(s_o, 1)

            products(0, 0, reuse=False)
            pe.wait_ge(s_alk, 1)
            products(1, 1, reuse=False)
            with pe.Fori(2, NT - 1, 2) as i:
                for p in range(2):
                    products(i + p, p)


COLUMNS = ["L0_mix_ln1_g", "L0_mix_ln1_b", "L0_mix_bk", "L0_mix_bv", "L0_mix_bq", "L0_mix_ln2_g", "L0_mix_ln2_b",
           "L0_mix_b1"]
COLUMN_AT = {name: slice(n * K8, n * K8 + (FF // 128 if name == "L0_mix_b1" else K8)) for n, name in enumerate(COLUMNS)}
COLUMN_COUNT = COLUMN_AT["L0_mix_b1"].stop


def transpose_second_norm(core):
    nc, inp = core.nc, core.inp
    x, x2_hi, x2_lo = inp["x"], core.x2_hi, core.x2_lo
    with ExitStack() as ctx:
        def sb(name, shape, dt=F32):
            return ctx.enter_context(nc.sbuf_tensor(name, shape, dt))

        x_in = sb("x_in4", [T, 2, D])
        z = sb("z4", [T, 2, D])
        vectors = sb("vectors", [COLUMN_COUNT, 128])
        scaled = sb("scaled4", [128, 2, K8, T])
        x2 = sb("x2", [128, 2, K8, T])
        p_t = ctx.enter_context(nc.psum_tensor("p_t", [128, 2, 2, 512], F32))

        p_col = ctx.enter_context(nc.psum_tensor("p_col", [128, 512], F32))

        s_vec = core.sem("vectors_loaded")
        s_vt = core.sem("vectors_transposed")
        s_gb = core.sem("columns_ready")
        s_x = [core.sem(f"x4_loaded{i}") for i in range(2)]
        s_z = core.sem("z4_ready")
        s_t = core.sem("z4_transposed")
        s_g = core.sem("scaled4_ready")
        s_x2 = core.sem("x2_ready")
        s_hi = core.sem("x2_hi_ready")
        s_lo = core.sem("x2_lo_ready")

        block = ctx.enter_context(nc.Block())

        @block.sync
        def _(sp):
            def load(i, slot):
                sp.dma_start(x_in[:, slot, :], x[bass.ds(i * T, T), :]).then_inc(s_x[slot], 16)

            load(0, 0)
            load(1, 1)
            for name in COLUMNS:
                sp.dma_start(vectors[COLUMN_AT[name], :], inp[name].rearrange("(k p) -> k p", p=128)).then_inc(s_vec, 16)
            with sp.Fori(2, NT - 1, 2) as i:
                for p in range(2):
                    sp.wait_ge(s_z, i + p - 1)
                    load(i + p, p)

        @block.scalar
        def _(act):
            def normalise(i, slot, reuse=True):
                act.wait_ge(s_x[slot], 16 + 8 * (i - slot))
                if reuse:
                    act.wait_ge(s_t, i - 1)
                act.activation(z[:, slot], x_in[:, slot], ACT.Identity, scale=core.ln_scale[:, bass.ds(i, 1)],
                               bias=core.ln_shift[:, bass.ds(i, 1)]).then_inc(s_z, 1)

            def keep_hi(i, slot):
                act.wait_ge(s_x2, i + 1)
                act.activation(x2_hi[:, :, bass.ds(i * T, T)], x2[:, slot], ACT.Copy).then_inc(s_hi, 1)

            normalise(0, 0, reuse=False)
            normalise(1, 1, reuse=False)
            keep_hi(0, 0)
            with act.Fori(2, NT - 1, 2) as i:
                for p in range(2):
                    normalise(i + p, p)
                    keep_hi(i + p - 1, 1 - p)
            keep_hi(NT - 1, 1)

        @block.tensor
        def _(pe):
            def transposes(i, slot, reuse=True):
                pe.wait_ge(s_z, i + 1)
                if reuse:
                    pe.wait_ge(s_g, i - 1)
                for k in range(K8):
                    last = pe.transpose(p_t[:, slot, k // 4, (k % 4) * T:(k % 4 + 1) * T],
                                        z[:, slot, k * 128:(k + 1) * 128], core.ident[0:T, 0:T])
                last.then_inc(s_t, 1)

            pe.wait_ge(s_vec, 16 * len(COLUMNS))
            count = COLUMN_COUNT
            pe.transpose(p_col[:, 0:count], vectors[:], core.ident[0:count, 0:count]).then_inc(s_vt, 1)
            transposes(0, 0, reuse=False)
            transposes(1, 1, reuse=False)
            with pe.Fori(2, NT - 1, 2) as i:
                for p in range(2):
                    transposes(i + p, p)

        @block.vector
        def _(dve):
            dve.wait_ge(s_vt, 1)
            dve.tensor_copy(core.cols[:], p_col[:, 0:COLUMN_COUNT]).then_inc(s_gb, 1)
            dve.wait_ge(s_gb, 1)
            g = core.cols[:, COLUMN_AT["L0_mix_ln1_g"]]

            def halves(ap):
                return ap.rearrange("p (a k) t -> p a k t", a=2)

            def scale(i, slot, reuse=True):
                dve.wait_ge(s_t, i + 1)
                if reuse:
                    dve.wait_ge(s_x2, i - 1)
                dve.tensor_tensor(halves(scaled[:, slot]), p_t[:, slot, :, 0:4 * T].rearrange("p a (k t) -> p a k t", k=4),
                                  halves(g.rearrange("p (k t) -> p k t", t=1)).to_broadcast([128, 2, 4, T]),
                                  ALU.mult).then_inc(s_g, 1)

            def keep_lo(i, slot):
                dve.wait_ge(s_hi, i + 1)
                cols = bass.ds(i * T, T)
                dve.tensor_tensor(x2_lo[:, :, cols], x2[:, slot], f32(x2_hi[:, :, cols]), ALU.subtract).then_inc(s_lo, 1)

            scale(0, 0, reuse=False)
            scale(1, 1, reuse=False)
            keep_lo(0, 0)
            with dve.Fori(2, NT - 1, 2) as i:
                for p in range(2):
                    scale(i + p, p)
                    keep_lo(i + p - 1, 1 - p)
            keep_lo(NT - 1, 1)

        @block.gpsimd
        def _(pool):
            pool.wait_ge(s_gb, 1)
            b = core.cols[:, COLUMN_AT["L0_mix_ln1_b"]]

            def shift(i, slot, reuse=True):
                pool.wait_ge(s_g, i + 1)
                if reuse:
                    pool.wait_ge(s_lo, i - 1)
                pool.tensor_tensor(x2[:, slot], scaled[:, slot], b.rearrange("p (k t) -> p k t", t=1).to_broadcast([128, K8, T]),
                                   ALU.add).then_inc(s_x2, 1)

            shift(0, 0, reuse=False)
            shift(1, 1, reuse=False)
            with pool.Fori(2, NT - 1, 2) as i:
                for p in range(2):
                    shift(i + p, p)


STEPS = 5
CHUNK = 2 * T
KEY, VALUE, QUERY = 0, 1, 2
V_GROUPS = [(0, 3), (3, 3), (6, 4)]


def linear_attention(core):
    nc, inp = core.nc, core.inp
    x2_hi, x2_lo = core.x2_hi, core.x2_lo
    weights = [inp["L0_mix_wk"], inp["L0_mix_wv"], inp["L0_mix_wq"]]
    with ExitStack() as ctx:
        def sb(name, shape, dt=F32):
            return ctx.enter_context(nc.sbuf_tensor(name, shape, dt))

        def ps(name, shape):
            return ctx.enter_context(nc.psum_tensor(name, shape, F32))

        w_in = [sb(f"w_in_{n}", [128, K8, 128]) for n in "kvq"]
        w_hi = [sb(f"w_hi_{n}", [128, K8, 128], F32R) for n in "kvq"]
        w_lo = [sb(f"w_lo_{n}", [128, K8, 128], F32R) for n in "kvq"]
        bias = [core.cols[:, COLUMN_AT[f"L0_mix_b{n}"]] for n in "kvq"]
        proj = sb("proj", [128, 2, KMAP])
        proj_hi = sb("proj_hi", [128, 2, KMAP], F32R)
        proj_lo = sb("proj_lo", [128, 2, KMAP], F32R)
        half_pi = sb("half_pi", [128, 1])
        k_hi = sb("k_hi", [128, N], F32R)
        k_lo = sb("k_lo", [128, N], F32R)
        q_hi = sb("q_hi", [128, N], F32R)
        q_lo = sb("q_lo", [128, N], F32R)
        v_t = sb("v_t", [128, N])
        v_hi = sb("v_hi", [T, NT, 128], F32R)
        v_lo = sb("v_lo", [T, NT, 128], F32R)
        whole = sb("whole_turns", [128, 2, 512])
        part = sb("part_turn", [128, 2, 512])
        away = sb("part_turn_below", [128, 2, 512])
        cs = sb("cos_sin", [128, 2, 1024])
        cs_hi = sb("cos_sin_hi", [128, 2, 1024], F32R)
        cs_lo = sb("cos_sin_lo", [128, 2, 1024], F32R)
        kv_t = sb("kv_t", [128, 4, 128])
        kv_hi = sb("kv_hi", [128, 4, 128], F32R)
        kv_lo = sb("kv_lo", [128, 4, 128], F32R)
        attn_t = sb("attn_t", [128, N])
        p_w = ps("p_w", [128, 3, 512])
        p_p = ps("p_p", [128, 2, 512])
        p_kv = ps("p_kv", [128, 512])
        p_at = ps("p_at", [128, 512])
        p_tr = ps("p_tr5", [128, 4, 128])

        s_w = [core.sem(f"weights_loaded_{n}") for n in "kvq"]
        s_whi = [core.sem(f"weights_hi_{n}") for n in "kvq"]
        s_wlo = [core.sem(f"weights_lo_{n}") for n in "kvq"]
        s_zero = core.sem("zeros_written5")
        s_proj = core.sem("projection_loaded")
        s_prep = core.sem("projection_step")
        s_prod = core.sem("third_product_done")
        s_kqhi = core.sem("key_or_query_hi_kept")
        s_klo = core.sem("keys_kept")
        s_qlo = core.sem("queries_kept")
        s_vt = core.sem("values_kept")
        s_tr = core.sem("transposes_done5")
        s_trhi = core.sem("transposed_hi_kept")
        s_trlo = core.sem("transposed_kept")
        s_p = core.sem("phases_in_psum")
        s_whole = core.sem("whole_turns_ready")
        s_part = core.sem("part_turns_ready")
        s_away = core.sem("part_turns_abs_ready")
        s_cs = core.sem("cos_sin_ready")
        s_cshi = core.sem("cos_sin_hi_ready")
        s_cslo = core.sem("cos_sin_lo_ready")
        s_used = core.sem("cos_sin_used")
        s_kvt = core.sem("kv_copied")
        s_at = core.sem("attention_in_psum")
        s_atk = core.sem("attention_kept")
        s_st = core.sem("attention_stored")

        block = ctx.enter_context(nc.Block())

        def done(j, k):
            return 2 * STEPS * j + k + 1

        def two_back(j, k):
            return 2 * STEPS * j + max(k - 1, 0)

        def keys_view(buf, slot):
            return buf[0:T, slot].rearrange("p (i h c m) -> p i h c m", i=2, h=2, c=2)

        def step_view(buf, k, c):
            if k < STEPS:
                return buf[0:T, k % 2].rearrange("p (i c m) -> p i c m", i=4, c=2)[:, :, c, :]
            return buf[:, k % 2, 0:4 * CHUNK].rearrange("p (h c t) -> p h c t", h=2, c=2)[:, :, c, :]

        def flat(buf, k):
            return buf[0:T, k % 2, 0:512] if k < STEPS else buf[:, k % 2, 0:2 * CHUNK]

        def rows(buf, k):
            if k < STEPS:
                return flat(buf, k).rearrange("p (i m) -> p i m", i=4)
            return flat(buf, k).rearrange("p (h t) -> p h t", h=2)

        def full(buf, k):
            return buf[0:T, k % 2, :] if k < STEPS else buf[:, k % 2, 0:4 * CHUNK]

        @block.sync
        def _(sp):
            def load(which, j):
                sp.dma_start(w_in[which][:], weights[which][:, bass.ds(j * 128, 128)].rearrange("(k p) n -> p k n", p=128)
                             ).then_inc(s_w[which], 16)

            load(KEY, 0)
            load(VALUE, 0)
            sp.wait_ge(s_zero, 1)
            for h in range(2):
                sp.dma_start(proj[h * DH:(h + 1) * DH, h, :], inp["L0_mix_proj_mat"]).then_inc(s_proj, 16)
            load(QUERY, 0)

            def store(j):
                sp.wait_ge(s_atk, STEPS * j + STEPS)
                sp.dma_start(core.attn_dram[bass.ds(j * 128, 128), :], attn_t[:]).then_inc(s_st, 16)

            with sp.Fori(0, PAIRS - 1) as j:
                for which in (KEY, VALUE, QUERY):
                    sp.wait_ge(s_wlo[which], j + 1)
                    load(which, j + 1)
                store(j)
            store(PAIRS - 1)
            sp.wait_ge(s_st, 16 * PAIRS)

        @block.gpsimd
        def _(pool):
            pool.memset(proj[:], 0.0).then_inc(s_zero, 1)
            pool.memset(half_pi[:], HALF_PI).then_inc(s_zero, 1)
            pool.memset(f32(kv_hi[:]), 0.0).then_inc(s_zero, 1)
            pool.memset(f32(kv_lo[:]), 0.0).then_inc(s_zero, 1)

            def split_lo(which, j):
                pool.wait_ge(s_whi[which], j + 1)
                pool.tensor_tensor(w_lo[which][:], w_in[which][:], f32(w_hi[which][:]), ALU.subtract).then_inc(s_wlo[which], 1)

            def keep_lo(j, k):
                pool.wait_ge(s_cshi, done(j, k))
                pool.tensor_tensor(full(cs_lo, k), full(cs, k), f32(full(cs_hi, k)), ALU.subtract).then_inc(s_cslo, 1)

            for which in (KEY, VALUE):
                split_lo(which, 0)
            pool.wait_ge(s_proj, 32)
            pool.tensor_scalar(proj[:], proj[:], 1.0 / (DH ** 0.5 * 2 * 3.141592653589793), None, ALU.mult).then_inc(s_prep, 1)
            pool.wait_ge(s_prep, 1)
            pool.tensor_copy(proj_hi[:], proj[:]).then_inc(s_prep, 1)
            pool.wait_ge(s_prep, 2)
            pool.tensor_tensor(proj_lo[:], proj[:], f32(proj_hi[:]), ALU.subtract).then_inc(s_prep, 1)
            split_lo(QUERY, 0)

            def pair(j, more):
                keep_lo(j, 0)
                keep_lo(j, 1)
                keep_lo(j, 2)
                if more:
                    split_lo(KEY, j + 1)
                keep_lo(j, 3)
                keep_lo(j, 4)
                if more:
                    split_lo(VALUE, j + 1)
                keep_lo(j, 5)
                keep_lo(j, 6)
                if more:
                    split_lo(QUERY, j + 1)
                for k in range(7, 2 * STEPS):
                    keep_lo(j, k)

            with pool.Fori(0, PAIRS - 1) as j:
                pair(j, True)
            pair(PAIRS - 1, False)

        @block.scalar
        def _(act):
            def split_hi(which, j):
                act.wait_ge(s_w[which], 16 * j + 16)
                act.activation(w_hi[which][:], w_in[which][:], ACT.Copy).then_inc(s_whi[which], 1)

            def keep_run(which, j, n):
                a, w = THIRDS[n]
                act.wait_ge(s_prod, 9 * j + 3 * which + n + 1)
                core.passed(act)
                out = (k_hi, v_t, q_hi)[which]
                act.activation(out[:, a:a + w], p_w[:, n, 0:w], ACT.Identity, bias=bias[which][:, bass.ds(j, 1)]
                               ).then_inc(s_vt if which == VALUE else s_kqhi, 1)

            def keep_v(j, group):
                first, count = V_GROUPS[group]
                act.wait_ge(s_tr, 4 * j + group + 1)
                act.activation(v_hi[:, first:first + count, :], p_tr[0:T, 0:count, :], ACT.Copy).then_inc(s_trhi, 1)

            def keep_kv(j):
                act.wait_ge(s_tr, 4 * j + 4)
                for h in range(2):
                    last = act.activation(kv_hi[:, 2 * h:2 * h + 2, h * DH:(h + 1) * DH],
                                          p_tr[:, 2 * h:2 * h + 2, h * DH:(h + 1) * DH], ACT.Copy, scale=1.0 / KMAP)
                last.then_inc(s_trhi, 1)

            def cos_sin(j, k):
                act.wait_ge(s_part, done(j, k))
                act.wait_ge(s_cslo, two_back(j, k))
                act.activation(step_view(cs, k, 1), rows(part, k), ACT.Sin, scale=TWO_PI)
                act.wait_ge(s_away, done(j, k))
                act.activation(step_view(cs, k, 0), rows(away, k), ACT.Sin, scale=TWO_PI,
                               bias=half_pi[0:T if k < STEPS else 128, :]).then_inc(s_cs, 1)

            def keep_attention(j, c):
                act.wait_ge(s_at, STEPS * j + c + 1)
                act.activation(attn_t[:, c * CHUNK:(c + 1) * CHUNK], p_at[:, 0:CHUNK], ACT.Copy).then_inc(s_atk, 1)

            for which in (KEY, VALUE):
                split_hi(which, 0)
            for n in range(3):
                keep_run(KEY, 0, n)
            split_hi(QUERY, 0)
            for n in range(3):
                keep_run(VALUE, 0, n)
            act.wait_ge(s_zero, 4)
            keep_v(0, 0)
            keep_v(0, 1)

            def pair(j, more):
                cos_sin(j, 0)
                cos_sin(j, 1)
                keep_run(QUERY, j, 0)
                keep_v(j, 2)
                cos_sin(j, 2)
                cos_sin(j, 3)
                keep_run(QUERY, j, 1)
                if more:
                    split_hi(KEY, j + 1)
                cos_sin(j, 4)
                keep_run(QUERY, j, 2)
                if more:
                    split_hi(VALUE, j + 1)
                cos_sin(j, 5)
                cos_sin(j, 6)
                if more:
                    keep_run(KEY, j + 1, 0)
                    split_hi(QUERY, j + 1)
                keep_kv(j)
                if more:
                    keep_run(KEY, j + 1, 1)
                act.wait_ge(s_st, 16 * j)
                keep_attention(j, 0)
                cos_sin(j, 7)
                if more:
                    keep_run(KEY, j + 1, 2)
                keep_attention(j, 1)
                cos_sin(j, 8)
                if more:
                    keep_run(VALUE, j + 1, 0)
                keep_attention(j, 2)
                cos_sin(j, 9)
                if more:
                    keep_run(VALUE, j + 1, 1)
                    keep_v(j + 1, 0)
                keep_attention(j, 3)
                if more:
                    keep_run(VALUE, j + 1, 2)
                    keep_v(j + 1, 1)
                keep_attention(j, 4)

            with act.Fori(0, PAIRS - 1) as j:
                pair(j, True)
            pair(PAIRS - 1, False)

        @block.vector
        def _(dve):
            def keep_run(which, j, n):
                a, w = THIRDS[n]
                dve.wait_ge(s_kqhi, 6 * j + (3 if which == QUERY else 0) + n + 1)
                hi, lo, s = (k_hi, k_lo, s_klo) if which == KEY else (q_hi, q_lo, s_qlo)
                dve.scalar_tensor_tensor(lo[:, a:a + w], p_w[:, n, 0:w], bias[which][:, bass.ds(j, 1)], f32(hi[:, a:a + w]),
                                         ALU.add, ALU.subtract).then_inc(s, 1)

            def keep_v(j, group):
                first, count = V_GROUPS[group]
                dve.wait_ge(s_trhi, 4 * j + group + 1)
                dve.tensor_tensor(v_lo[:, first:first + count, :], p_tr[0:T, 0:count, :],
                                  f32(v_hi[:, first:first + count, :]), ALU.subtract).then_inc(s_trlo, 1)

            def keep_kv(j):
                dve.wait_ge(s_trhi, 4 * j + 4)
                for h in range(2):
                    block_h = (slice(None), slice(2 * h, 2 * h + 2), slice(h * DH, (h + 1) * DH))
                    last = dve.scalar_tensor_tensor(kv_lo[block_h], p_tr[block_h], 1.0 / KMAP, f32(kv_hi[block_h]),
                                                    ALU.mult, ALU.subtract)
                last.then_inc(s_trlo, 1)

            def phases(j, k):
                dve.wait_ge(s_p, done(j, k))
                dve.wait_ge(s_part, two_back(j, k))
                dve.tensor_scalar(flat(whole, k), flat(p_p, k), MAGIC, -MAGIC, ALU.add, ALU.add).then_inc(s_whole, 1)
                dve.wait_ge(s_whole, done(j, k))
                dve.wait_ge(s_cs, two_back(j, k))
                dve.tensor_tensor(flat(part, k), flat(p_p, k), flat(whole, k), ALU.subtract).then_inc(s_part, 1)
                dve.wait_ge(s_part, done(j, k))
                dve.scalar_tensor_tensor(flat(away, k), flat(part, k), -1.0, flat(part, k), ALU.mult, ALU.min).then_inc(s_away, 1)

            def keep_hi(j, k):
                dve.wait_ge(s_cs, done(j, k))
                dve.wait_ge(s_used, two_back(j, k))
                dve.tensor_copy(full(cs_hi, k), full(cs, k)).then_inc(s_cshi, 1)

            def copy_kv(j):
                dve.wait_ge(s_used, done(j, STEPS - 1))
                dve.tensor_copy(kv_t[:], p_kv[:].rearrange("p (b m) -> p b m", b=4)).then_inc(s_kvt, 1)

            for n in range(3):
                keep_run(KEY, 0, n)
            dve.wait_ge(s_zero, 4)
            keep_v(0, 0)
            keep_v(0, 1)

            def pair(j, more):
                phases(j, 0)
                phases(j, 1)
                keep_hi(j, 0)
                keep_run(QUERY, j, 0)
                keep_hi(j, 1)
                keep_v(j, 2)
                phases(j, 2)
                phases(j, 3)
                keep_hi(j, 2)
                keep_run(QUERY, j, 1)
                phases(j, 4)
                keep_hi(j, 3)
                keep_hi(j, 4)
                keep_run(QUERY, j, 2)
                phases(j, 5)
                phases(j, 6)
                copy_kv(j)
                keep_hi(j, 5)
                if more:
                    keep_run(KEY, j + 1, 0)
                keep_kv(j)
                keep_hi(j, 6)
                if more:
                    keep_run(KEY, j + 1, 1)
                phases(j, 7)
                if more:
                    keep_run(KEY, j + 1, 2)
                keep_hi(j, 7)
                phases(j, 8)
                keep_hi(j, 8)
                phases(j, 9)
                if more:
                    keep_v(j + 1, 0)
                keep_hi(j, 9)
                if more:
                    keep_v(j + 1, 1)

            with dve.Fori(0, PAIRS - 1) as j:
                pair(j, True)
            pair(PAIRS - 1, False)

        @block.tensor
        def _(pe):
            def product(which, j, n, first=0, past=K8):
                a, w = THIRDS[n]
                if first == 0:
                    pe.wait_ge(s_wlo[which], j + 1)
                for k in range(first, past):
                    for m, (left, right) in enumerate(((w_lo, x2_hi), (w_hi, x2_lo), (w_hi, x2_hi))):
                        last = pe.matmul(p_w[:, n, 0:w], left[which][:, k, :], right[:, k, a:a + w],
                                         start=(k == 0 and m == 0), stop=(k == K8 - 1 and m == 2))
                if past == K8:
                    last.then_inc(s_prod, 1)

            def key_run(j, n):
                pe.wait_ge(s_qlo, 3 * j - 2 + n)
                product(KEY, j, n)

            def value_run(j, n):
                pe.wait_ge(s_klo, 3 * j + n + 1)
                product(VALUE, j, n)

            def query_run(j, n, first=0, past=K8):
                if first == 0:
                    pe.wait_ge(s_vt, 3 * j + n + 1)
                product(QUERY, j, n, first, past)

            def transpose_v(j, group):
                first, count = V_GROUPS[group]
                pe.wait_ge(s_vt, 3 * j + group + 1)
                pe.wait_ge(s_trlo, 4 * j + group)
                for i in range(count):
                    tile = slice((first + i) * T, (first + i + 1) * T)
                    last = pe.transpose(p_tr[0:T, i, :], v_t[:, tile], core.ident[:])
                last.then_inc(s_tr, 1)

            def transpose_kv(j):
                pe.wait_ge(s_kvt, j + 1)
                pe.wait_ge(s_trlo, 4 * j + 3)
                for b in range(4):
                    last = pe.transpose(p_tr[:, b, :], kv_t[:, b, :], core.ident[:])
                last.then_inc(s_tr, 1)

            def key_phases(j, k):
                pe.wait_ge(s_klo, 3 * j + (2 * T * (k + 1) - 1) // 417 + 1)
                pe.wait_ge(s_part, two_back(j, k))
                for i in range(2):
                    tile = slice((2 * k + i) * T, (2 * k + i + 1) * T)
                    for m, (left, right) in enumerate(((k_lo, proj_hi), (k_hi, proj_lo), (k_hi, proj_hi))):
                        last = pe.matmul(p_p[0:T, k % 2, i * 256:(i + 1) * 256], left[:, tile], right[:].rearrange("p h m -> p (h m)"),
                                         start=(m == 0), stop=(m == 2))
                last.then_inc(s_p, 1)

            def query_phases(j, k):
                c = k - STEPS
                pe.wait_ge(s_qlo, 3 * j + (CHUNK * (c + 1) - 1) // 417 + 1)
                pe.wait_ge(s_part, two_back(j, k))
                for h in range(2):
                    for m, (left, right) in enumerate(((proj_lo, q_hi), (proj_hi, q_lo), (proj_hi, q_hi))):
                        last = pe.matmul(p_p[:, k % 2, h * CHUNK:(h + 1) * CHUNK], left[:, h, :], right[:, c * CHUNK:(c + 1) * CHUNK],
                                         start=(m == 0), stop=(m == 2))
                last.then_inc(s_p, 1)

            def accumulate_kv(j, k):
                if k == 0:
                    pe.wait_ge(s_kvt, j)
                pe.wait_ge(s_trlo, 4 * j + (1, 2, 2, 3, 3)[k])
                pe.wait_ge(s_cslo, done(j, k))
                hi, lo = keys_view(cs_hi, k % 2), keys_view(cs_lo, k % 2)
                for i in range(2):
                    for m, (left, right) in enumerate(((v_lo, hi), (v_hi, lo), (v_hi, hi))):
                        last = pe.matmul(p_kv[:], left[:, 2 * k + i, :], right[:, i].rearrange("p h c m -> p (h c m)"),
                                         start=(k == 0 and i == 0 and m == 0), stop=(k == STEPS - 1 and i == 1 and m == 2))
                last.then_inc(s_used, 1)

            def attend(j, k):
                c = k - STEPS
                pe.wait_ge(s_trlo, 4 * j + 4)
                pe.wait_ge(s_cslo, done(j, k))
                pe.wait_ge(s_atk, STEPS * j + c)
                for b in range(4):
                    cols = slice(b * CHUNK, (b + 1) * CHUNK)
                    for m, (left, right) in enumerate(((kv_lo, cs_hi), (kv_hi, cs_lo), (kv_hi, cs_hi))):
                        last = pe.matmul(p_at[:, 0:CHUNK], left[:, b, :], right[:, k % 2, cols],
                                         start=(b == 0 and m == 0), stop=(b == 3 and m == 2))
                last.then_inc(s_at, 1)
                pe.wait_ge(s_at, STEPS * j + c + 1)
                pe.sem_inc(s_used, 1)

            for n in range(3):
                product(KEY, 0, n)
            for n in range(3):
                value_run(0, n)
            transpose_v(0, 0)
            transpose_v(0, 1)
            pe.wait_ge(s_prep, 3)

            def pair(j, more):
                key_phases(j, 0)
                key_phases(j, 1)
                query_run(j, 0)
                transpose_v(j, 2)
                accumulate_kv(j, 0)
                key_phases(j, 2)
                query_run(j, 1, 0, K8 // 2)
                accumulate_kv(j, 1)
                key_phases(j, 3)
                query_run(j, 1, K8 // 2, K8)
                accumulate_kv(j, 2)
                key_phases(j, 4)
                query_run(j, 2, 0, K8 // 2)
                accumulate_kv(j, 3)
                query_run(j, 2, K8 // 2, K8)
                query_phases(j, 5)
                query_phases(j, 6)
                accumulate_kv(j, 4)
                if more:
                    key_run(j + 1, 0)
                transpose_kv(j)
                if more:
                    key_run(j + 1, 1)
                attend(j, 5)
                query_phases(j, 7)
                if more:
                    key_run(j + 1, 2)
                attend(j, 6)
                query_phases(j, 8)
                if more:
                    value_run(j + 1, 0)
                attend(j, 7)
                query_phases(j, 9)
                if more:
                    value_run(j + 1, 1)
                    transpose_v(j + 1, 0)
                attend(j, 8)
                if more:
                    value_run(j + 1, 2)
                    transpose_v(j + 1, 1)
                attend(j, 9)

            with pe.Fori(0, PAIRS - 1) as j:
                pair(j, True)
            pair(PAIRS - 1, False)


def column_stats(act, s_stat, count, junk, rows_in, sums, neg_mean, squares, scale=None, shift=None, both=None):
    act.wait_ge(s_stat, count)
    if scale is None:
        act.activation(junk, rows_in, ACT.Identity, accum_out=sums).then_inc(s_stat, 1)
    else:
        act.activation(junk, rows_in, ACT.Identity, scale=scale, bias=shift, accum_out=sums).then_inc(s_stat, 1)
    act.wait_ge(s_stat, count + 1)
    act.mul(neg_mean, sums, -1.0 / D).then_inc(s_stat, 1)
    act.wait_ge(s_stat, count + 2)
    act.activation(junk, rows_in, ACT.Square, bias=neg_mean, accum_out=squares).then_inc(s_stat, 1)


def project_attention(core):
    nc, inp, x1 = core.nc, core.inp, core.rows
    with ExitStack() as ctx:
        def sb(name, shape, dt=F32):
            return ctx.enter_context(nc.sbuf_tensor(name, shape, dt))

        w_in = sb("wo_in", [128, 2, D])
        w_hi = sb("wo_hi", [128, K8, D], F32R)
        w_lo = sb("wo_lo", [128, K8, D], F32R)
        at_in = sb("at_in", [128, 2, K8, T])
        at_hi = sb("at_hi", [128, 2, K8, T], F32R)
        at_lo = sb("at_lo", [128, 2, K8, T], F32R)
        bo = sb("bo", [T, D])
        x_in = sb("x_in6", [T, 2, D])
        xn = sb("xn6", [T, 2, D])
        junk = sb("junk6", [T, D])
        sums = sb("sums6", [T, NT])
        p_o = ctx.enter_context(nc.psum_tensor("p_o6", [128, 2, 2, 512], F32))

        s_w = [core.sem(f"wo_loaded{i}") for i in range(2)]
        s_whi = core.sem("wo_hi_ready")
        s_wlo = core.sem("wo_lo_ready")
        s_bo = core.sem("bo_loaded")
        s_in = [core.sem(f"attention_loaded{i}") for i in range(2)]
        s_x = [core.sem(f"x6_loaded{i}") for i in range(2)]
        s_ahi = core.sem("at_hi_ready")
        s_alo = core.sem("at_lo_ready")
        s_xn = core.sem("xn6_ready")
        s_xb = core.sem("xn_plus_bo_ready")
        s_o = core.sem("wo_product_done")
        s_x1 = core.sem("x1_ready")
        s_stat = core.sem("x1_stat_step")
        s_step = core.sem("rstd6_step")

        block = ctx.enter_context(nc.Block())

        @block.sync
        def _(sp):
            def load(i, slot):
                sp.dma_start(at_in[:, slot], core.attn_dram[:, bass.ds(i * T, T)].rearrange("(k p) t -> p k t", p=128)
                             ).then_inc(s_in[slot], 16)
                sp.dma_start(x_in[:, slot], inp["x"][bass.ds(i * T, T), :]).then_inc(s_x[slot], 16)

            for k in range(K8):
                if k >= 2:
                    sp.wait_ge(s_wlo, k - 1)
                sp.dma_start(w_in[:, k % 2, :], inp["L0_mix_wo"][k * 128:(k + 1) * 128, :]).then_inc(s_w[k % 2], 16)
                if k == 1:
                    load(0, 0)
                if k == 3:
                    sp.dma_start(bo[:], spread(inp["L0_mix_bo"], T)).then_inc(s_bo, 16)
                    load(1, 1)
            with sp.Fori(2, NT - 1, 2) as i:
                for p in range(2):
                    sp.wait_ge(s_alo, i + p - 1)
                    sp.wait_ge(s_xn, i + p - 1)
                    load(i + p, p)

        @block.scalar
        def _(act):
            def attention_hi(i, slot, reuse=True):
                act.wait_ge(s_in[slot], 16 + 8 * (i - slot))
                if reuse:
                    act.wait_ge(s_o, i - 1)
                act.activation(at_hi[:, slot], at_in[:, slot], ACT.Copy).then_inc(s_ahi, 1)

            def residual(i, slot, reuse=True):
                act.wait_ge(s_x[slot], 16 + 8 * (i - slot))
                if reuse:
                    act.wait_ge(s_x1, i - 1)
                act.activation(xn[:, slot], x_in[:, slot], ACT.Identity, scale=core.rstd[:, bass.ds(i, 1)],
                               bias=core.xn_shift[:, bass.ds(i, 1)]).then_inc(s_xn, 1)

            def stats(i):
                col = bass.ds(i, 1)
                act.wait_ge(s_x1, i + 1)
                column_stats(act, s_stat, 3 * i, junk[:], x1[:, col, :].rearrange("p a n -> p (a n)"), sums[:, col],
                             core.negmean[:, col], core.var[:, col])

            for k in range(K8):
                act.wait_ge(s_w[k % 2], 16 * (k // 2 + 1))
                act.activation(w_hi[:, k, :], w_in[:, k % 2, :], ACT.Copy).then_inc(s_whi, 1)
                if k == 1:
                    attention_hi(0, 0, reuse=False)
                    residual(0, 0, reuse=False)
            attention_hi(1, 1, reuse=False)
            residual(1, 1, reuse=False)
            stats(0)
            with act.Fori(2, NT - 1, 2) as i:
                for p in range(2):
                    attention_hi(i + p, p)
                    residual(i + p, p)
                    stats(i + p - 1)
            stats(NT - 1)
            act.wait_ge(s_step, 1)
            act.activation(core.root[:], core.var[:], ACT.Sqrt).then_inc(s_step, 1)

        @block.gpsimd
        def _(pool):
            def attention_lo(i, slot):
                pool.wait_ge(s_ahi, i + 1)
                pool.tensor_tensor(at_lo[:, slot], at_in[:, slot], f32(at_hi[:, slot]), ALU.subtract).then_inc(s_alo, 1)

            def add_bias(i, slot):
                pool.wait_ge(s_xn, i + 1)
                pool.tensor_tensor(xn[:, slot], xn[:, slot], bo[:], ALU.add).then_inc(s_xb, 1)

            for k in range(K8):
                pool.wait_ge(s_whi, k + 1)
                pool.tensor_tensor(w_lo[:, k, :], w_in[:, k % 2, :], f32(w_hi[:, k, :]), ALU.subtract).then_inc(s_wlo, 1)
                if k == 1:
                    attention_lo(0, 0)
            pool.wait_ge(s_bo, 16)
            add_bias(0, 0)
            attention_lo(1, 1)
            add_bias(1, 1)
            with pool.Fori(2, NT - 1, 2) as i:
                for p in range(2):
                    attention_lo(i + p, p)
                    add_bias(i + p, p)

        @block.vector
        def _(dve):
            def add(i, slot):
                dve.wait_ge(s_o, i + 1)
                dve.wait_ge(s_xb, i + 1)
                dve.tensor_tensor(x1[:, bass.ds(i, 1), :].rearrange("p a (b n) -> p (a b) n", b=2), p_o[0:T, slot],
                                  xn[:, slot].rearrange("p (b n) -> p b n", b=2), ALU.add).then_inc(s_x1, 1)

            with dve.Fori(0, NT - 1, 2) as i:
                for p in range(2):
                    add(i + p, p)
            dve.wait_ge(s_stat, 3 * NT)
            dve.tensor_scalar(core.var[:], core.var[:], 1.0 / D, LN_EPS, ALU.mult, ALU.add).then_inc(s_step, 1)
            inverse_root(dve, s_step, 2, core.var[:], core.root[:], core.tmp[:], core.rstd[:])
            dve.tensor_tensor(core.ln_shift[:], core.negmean[:], core.rstd[:], ALU.mult).then_inc(s_step, 1)
            dve.wait_ge(s_step, 8)

        @block.tensor
        def _(pe):
            def products(i, slot, first=False, reuse=True):
                pe.wait_ge(s_alo, i + 1)
                if reuse:
                    pe.wait_ge(s_x1, i - 1)
                for k in range(K8):
                    if first:
                        pe.wait_ge(s_wlo, k + 1)
                    for m, (left, right) in enumerate(((at_lo, w_hi), (at_hi, w_lo), (at_hi, w_hi))):
                        for n in range(2):
                            last = pe.matmul(p_o[0:T, slot, n, :], left[:, slot, k, :], right[:, k, n * 512:(n + 1) * 512],
                                             start=(k == 0 and m == 0), stop=(k == K8 - 1 and m == 2))
                last.then_inc(s_o, 1)

            products(0, 0, first=True, reuse=False)
            products(1, 1, reuse=False)
            with pe.Fori(2, NT - 1, 2) as i:
                for p in range(2):
                    products(i + p, p)


def feed_forward(core):
    nc, inp, rows = core.nc, core.inp, core.rows
    F4 = FF // 128
    g2, b2c = core.cols[:, COLUMN_AT["L0_mix_ln2_g"]], core.cols[:, COLUMN_AT["L0_mix_ln2_b"]]
    b1c = core.cols[:, COLUMN_AT["L0_mix_b1"]]
    with ExitStack() as ctx:
        def sb(name, shape, dt=F32):
            return ctx.enter_context(nc.sbuf_tensor(name, shape, dt))

        w_in = sb("w12_in", [128, 2, D])
        w1_hi = sb("w1_hi", [128, K8, FF], F32R)
        w1_lo = sb("w1_lo", [128, K8, FF], F32R)
        w2_hi = sb("w2_hi", [128, F4, D], F32R)
        w2_lo = sb("w2_lo", [128, F4, D], F32R)
        b2 = sb("b2", [T, D])
        z = sb("z7", [T, 2, D])
        scaled = sb("scaled7", [128, K8, T])
        x2 = sb("x2_7", [128, K8, T])
        x2_hi = sb("x2_hi7", [128, K8, CHUNK], F32R)
        x2_lo = sb("x2_lo7", [128, K8, CHUNK], F32R)
        hid = sb("hidden", [128, F4, CHUNK])
        hid_hi = sb("hidden_hi", [128, F4, CHUNK], F32R)
        hid_lo = sb("hidden_lo", [128, F4, CHUNK], F32R)
        gnn_in = sb("gnn_in", [T, 2, D])
        junk = sb("junk7", [T, D])
        sums = sb("sums7", [T, NT])
        p_t = ctx.enter_context(nc.psum_tensor("p_t7", [128, 2, 512], F32))
        p_1 = ctx.enter_context(nc.psum_tensor("p_hidden", [128, 2, 512], F32))
        p_2 = ctx.enter_context(nc.psum_tensor("p_w2", [128, 2, 2, 512], F32))

        s_w = [core.sem(f"w12_loaded{i}") for i in range(2)]
        s_whi = core.sem("w12_hi_ready")
        s_wlo = core.sem("w12_lo_ready")
        s_b2 = core.sem("b2_loaded")
        s_g = [core.sem(f"gnn_loaded{i}") for i in range(2)]
        s_q = core.sem("ternary_weights_loaded")
        s_z = core.sem("z7_ready")
        s_t = core.sem("z7_transposed")
        s_sc = core.sem("scaled7_ready")
        s_x2 = core.sem("x2_7_ready")
        s_xhi = core.sem("x2_hi7_ready")
        s_xlo = core.sem("x2_lo7_ready")
        s_1 = core.sem("hidden_product_done")
        s_h = core.sem("hidden_ready")
        s_hhi = core.sem("hidden_hi_ready")
        s_hlo = core.sem("hidden_lo_ready")
        s_gb = core.sem("gnn_plus_b2_ready")
        s_xg = core.sem("residuals_ready")
        s_2 = core.sem("w2_product_done")
        s_y = core.sem("y_ready")
        s_stat = core.sem("y_stat_step")
        s_step = core.sem("rstd7_step")

        block = ctx.enter_context(nc.Block())
        CH = NT // 2

        def w_part(n):
            if n < K8 // 2:
                return (inp["L0_mix_w1"][n * 256:(n + 1) * 256, :].rearrange("(a p) f -> p a f", p=128),
                        w1_hi[:, 2 * n:2 * n + 2, :], w1_lo[:, 2 * n:2 * n + 2, :], 2)
            n -= K8 // 2
            return (inp["L0_mix_w2"][n * 128:(n + 1) * 128, :].rearrange("(a p) f -> p a f", p=128),
                    w2_hi[:, n:n + 1, :], w2_lo[:, n:n + 1, :], 1)

        PARTS = K8 // 2 + F4

        @block.sync
        def _(sp):
            def load(i, slot):
                sp.dma_start(gnn_in[:, slot], core.gnn_dram[bass.ds(i * T, T), :]).then_inc(s_g[slot], 16)

            for n in range(PARTS):
                if n >= 2:
                    sp.wait_ge(s_wlo, n - 1)
                dram, _, _, a = w_part(n)
                sp.dma_start(w_in[:, n % 2, :].rearrange("p (a f) -> p a f", a=a), dram).then_inc(s_w[n % 2], 16)
            sp.dma_start(b2[:], spread(inp["L0_mix_b2"], T)).then_inc(s_b2, 16)
            load(0, 0)
            load(1, 1)
            for n in range(3):
                sp.dma_start(core.ternary[:, n, :], core.ternary_dram[n]).then_inc(s_q, 16)
            with sp.Fori(2, NT - 1, 2) as i:
                for p in range(2):
                    sp.wait_ge(s_xg, i + p - 1)
                    load(i + p, p)
            sp.wait_ge(s_q, 48)

        @block.scalar
        def _(act):
            def split(n):
                _, hi, _, a = w_part(n)
                act.wait_ge(s_w[n % 2], 16 * (n // 2 + 1))
                act.activation(hi, w_in[:, n % 2, :].rearrange("p (a f) -> p a f", a=a), ACT.Copy).then_inc(s_whi, 1)

            def normalise(i, slot, reuse=True):
                if reuse:
                    act.wait_ge(s_t, i - 1)
                col = bass.ds(i, 1)
                act.activation(z[:, slot], rows[:, col, :].rearrange("p a n -> p (a n)"), ACT.Identity,
                               scale=core.rstd[:, col], bias=core.ln_shift[:, col]).then_inc(s_z, 1)

            def x2_half(c, half):
                act.wait_ge(s_x2, 2 * c + half + 1)
                act.wait_ge(s_1, F4 * c)
                act.activation(x2_hi[:, :, half * T:(half + 1) * T], x2[:], ACT.Copy).then_inc(s_xhi, 1)

            def hidden(c, f):
                act.wait_ge(s_1, F4 * c + f + 1)
                act.wait_ge(s_hlo, c)
                act.activation(hid[:, f, :], p_1[:, f % 2, 0:CHUNK], ACT.Relu, bias=b1c[:, f:f + 1]).then_inc(s_h, 1)

            def stats(i):
                col = bass.ds(i, 1)
                act.wait_ge(s_y, i + 1)
                column_stats(act, s_stat, 3 * i, junk[:], rows[:, col, :].rearrange("p a n -> p (a n)"), sums[:, col],
                             core.negmean[:, col], core.var[:, col])

            normalise(0, 0, reuse=False)
            normalise(1, 1, reuse=False)
            for n in range(PARTS):
                split(n)
                if n < 2:
                    x2_half(0, n)

            def chunk(c, more, first=False):
                if more:
                    normalise(2 * c + 2, 0)
                    normalise(2 * c + 3, 1)
                for f in range(F4):
                    hidden(c, f)
                if more:
                    x2_half(c + 1, 0)
                if not first:
                    stats(2 * c - 2)
                    stats(2 * c - 1)
                if more:
                    x2_half(c + 1, 1)

            chunk(0, True, first=True)
            with act.Fori(1, CH - 1) as c:
                chunk(c, True)
            chunk(CH - 1, False)
            stats(NT - 2)
            stats(NT - 1)
            act.wait_ge(s_step, 1)
            act.activation(core.root[:], core.var[:], ACT.Sqrt).then_inc(s_step, 1)

        @block.gpsimd
        def _(pool):
            def shift(i, reuse=True):
                pool.wait_ge(s_sc, i + 1)
                if reuse:
                    pool.wait_ge(s_xlo, i)
                pool.tensor_tensor(x2[:], scaled[:], b2c.rearrange("p (k t) -> p k t", t=1).to_broadcast([128, K8, T]),
                                   ALU.add).then_inc(s_x2, 1)

            def residual(i, slot):
                pool.wait_ge(s_g[slot], 16 + 8 * (i - slot))
                pool.tensor_tensor(gnn_in[:, slot], gnn_in[:, slot], b2[:], ALU.add).then_inc(s_gb, 1)
                pool.wait_ge(s_gb, i + 1)
                pool.wait_ge(s_z, i + 1)
                pool.tensor_tensor(rows[:, bass.ds(i, 1), :].rearrange("p a n -> p (a n)"),
                                   rows[:, bass.ds(i, 1), :].rearrange("p a n -> p (a n)"), gnn_in[:, slot],
                                   ALU.add).then_inc(s_xg, 1)

            def split(n):
                _, hi, lo, a = w_part(n)
                pool.wait_ge(s_whi, n + 1)
                pool.tensor_tensor(lo, w_in[:, n % 2, :].rearrange("p (a f) -> p a f", a=a), f32(hi), ALU.subtract).then_inc(s_wlo, 1)

            def hidden_lo(c):
                pool.wait_ge(s_hhi, c + 1)
                pool.tensor_tensor(hid_lo[:], hid[:], f32(hid_hi[:]), ALU.subtract).then_inc(s_hlo, 1)

            shift(0, reuse=False)
            shift(1)
            for n in range(PARTS):
                split(n)
            pool.wait_ge(s_b2, 16)

            def chunk(c, more):
                if more:
                    shift(2 * c + 2)
                hidden_lo(c)
                residual(2 * c, 0)
                residual(2 * c + 1, 1)
                if more:
                    shift(2 * c + 3)

            with pool.Fori(0, CH - 1) as c:
                chunk(c, True)
            chunk(CH - 1, False)

        @block.vector
        def _(dve):
            def scale(i, reuse=True):
                dve.wait_ge(s_t, i + 1)
                if reuse:
                    dve.wait_ge(s_x2, i)
                dve.tensor_tensor(scaled[:].rearrange("p (a k) t -> p a k t", a=2),
                                  p_t[:, :, 0:4 * T].rearrange("p a (k t) -> p a k t", k=4),
                                  g2.rearrange("p (a k t) -> p a k t", a=2, t=1).to_broadcast([128, 2, 4, T]),
                                  ALU.mult).then_inc(s_sc, 1)

            def x2_half(c, half):
                dve.wait_ge(s_xhi, 2 * c + half + 1)
                cols = slice(half * T, (half + 1) * T)
                dve.tensor_tensor(x2_lo[:, :, cols], x2[:], f32(x2_hi[:, :, cols]), ALU.subtract).then_inc(s_xlo, 1)

            def hidden_hi(c):
                dve.wait_ge(s_h, F4 * (c + 1))
                dve.wait_ge(s_2, 2 * c)
                dve.tensor_copy(hid_hi[:], hid[:]).then_inc(s_hhi, 1)

            def add(i, slot):
                dve.wait_ge(s_2, i + 1)
                dve.wait_ge(s_xg, i + 1)
                out = rows[:, bass.ds(i, 1), :].rearrange("p a (b n) -> p (a b) n", b=2)
                dve.tensor_tensor(out, p_2[0:T, slot], out, ALU.add).then_inc(s_y, 1)

            scale(0, reuse=False)
            scale(1)
            x2_half(0, 0)
            x2_half(0, 1)

            def chunk(c, more):
                if more:
                    scale(2 * c + 2)
                hidden_hi(c)
                if more:
                    x2_half(c + 1, 0)
                    scale(2 * c + 3)
                add(2 * c, 0)
                if more:
                    x2_half(c + 1, 1)
                add(2 * c + 1, 1)

            with dve.Fori(0, CH - 1) as c:
                chunk(c, True)
            chunk(CH - 1, False)
            dve.wait_ge(s_stat, 3 * NT)
            dve.tensor_scalar(core.var[:], core.var[:], 1.0 / D, LN_EPS, ALU.mult, ALU.add).then_inc(s_step, 1)
            inverse_root(dve, s_step, 2, core.var[:], core.root[:], core.tmp[:], core.rstd[:])
            dve.tensor_tensor(core.ln_shift[:], core.negmean[:], core.rstd[:], ALU.mult).then_inc(s_step, 1)
            dve.wait_ge(s_step, 8)

        @block.tensor
        def _(pe):
            def transposes(i, slot, reuse=True):
                pe.wait_ge(s_z, i + 1)
                if reuse:
                    pe.wait_ge(s_sc, i)
                for k in range(K8):
                    last = pe.transpose(p_t[:, k // 4, (k % 4) * T:(k % 4 + 1) * T], z[:, slot, k * 128:(k + 1) * 128],
                                        core.ident[0:T, 0:T])
                last.then_inc(s_t, 1)

            def hidden(c, first=False):
                pe.wait_ge(s_xlo, 2 * c + 2)
                if first:
                    pe.wait_ge(s_wlo, K8 // 2)
                for f in range(F4):
                    if not (first and f < 2):
                        pe.wait_ge(s_h, F4 * c + f - 1)
                    for k in range(K8):
                        for m, (left, right) in enumerate(((w1_lo, x2_hi), (w1_hi, x2_lo), (w1_hi, x2_hi))):
                            last = pe.matmul(p_1[:, f % 2, 0:CHUNK], left[:, k, f * 128:(f + 1) * 128], right[:, k, :],
                                             start=(k == 0 and m == 0), stop=(k == K8 - 1 and m == 2))
                    last.then_inc(s_1, 1)

            def outer(c, first=False):
                pe.wait_ge(s_hlo, c + 1)
                if first:
                    pe.wait_ge(s_wlo, PARTS)
                for i in range(2):
                    if not first:
                        pe.wait_ge(s_y, 2 * c + i - 1)
                    tile = slice(i * T, (i + 1) * T)
                    for n in range(2):
                        for f in range(F4):
                            for m, (left, right) in enumerate(((hid_lo, w2_hi), (hid_hi, w2_lo), (hid_hi, w2_hi))):
                                last = pe.matmul(p_2[0:T, i, n, :], left[:, f, tile], right[:, f, n * 512:(n + 1) * 512],
                                                 start=(f == 0 and m == 0), stop=(f == F4 - 1 and m == 2))
                    last.then_inc(s_2, 1)

            def chunk(c, more, first=False):
                hidden(c, first)
                if more:
                    transposes(2 * c + 2, 0)
                    transposes(2 * c + 3, 1)
                outer(c, first)

            transposes(0, 0, reuse=False)
            transposes(1, 1)
            chunk(0, True, first=True)
            with pe.Fori(1, CH - 1) as c:
                chunk(c, True)
            chunk(CH - 1, False)


def quantised_forward(core):
    nc, rows, out = core.nc, core.rows, core.out
    F4 = FF // 128
    with ExitStack() as ctx:
        def sb(name, shape, dt=F32):
            return ctx.enter_context(nc.sbuf_tensor(name, shape, dt))

        def ps(name, shape, dt=F32):
            return ctx.enter_context(nc.psum_tensor(name, shape, dt))

        ident_b = sb("ident_b", [128, 128], BF16)
        w_gate = sb("gate_t", [128, K8, FF], BF16)
        w_up = sb("up_t", [128, K8, FF], BF16)
        w_down = sb("down_t", [128, F4, D], BF16)
        z = sb("z8", [T, 2, D])
        most = sb("most", [T, 2, 4])
        small = sb("limited8", [T, 2, D])
        lifted = sb("lifted8", [T, 2, D])
        xq = sb("x_rounded", [T, 2, D], BF16)
        xt = sb("x_rounded_t", [128, 2, K8, T], BF16)
        factor = sb("factors", [T, 2, 4])
        gate = sb("gate", [T, FF])
        hid = sb("hidden8", [T, FF])
        most2 = sb("most_hidden", [T, 4])
        small2 = sb("limited_hidden", [T, FF])
        lifted2 = sb("lifted_hidden", [T, FF])
        hq = sb("hidden_rounded", [T, FF], BF16)
        ht = sb("hidden_rounded_t", [128, F4, T], BF16)
        result = sb("result", [T, 2, D])
        p_tr = ps("p_tr8", [128, 2, K8, 128], BF16)
        p_gu = ps("p_gate_up", [128, 2, 2, 512])
        p_d = ps("p_down", [128, 2, 512])

        s_ib = core.sem("ident_b_ready")
        s_wt = core.sem("weights_transposed")
        s_wk = [core.sem(f"weights_kept{i}") for i in range(2)]
        s_z = core.sem("z8_ready")
        s_m = core.sem("row_scale_step")
        s_small = core.sem("limited8_ready")
        s_lift = core.sem("lifted8_ready")
        s_xq = core.sem("x_rounded_ready")
        s_xt = core.sem("x_transposed8")
        s_xk = core.sem("x_transposed_kept")
        s_gu = core.sem("gate_up_done")
        s_gate = core.sem("silu_ready")
        s_hid = core.sem("hidden8_ready")
        s_m2 = core.sem("hidden_scale_step")
        s_small2 = core.sem("limited_hidden_ready")
        s_lift2 = core.sem("lifted_hidden_ready")
        s_hq = core.sem("hidden_rounded_ready")
        s_ht = core.sem("hidden_transposed")
        s_hk = core.sem("hidden_transposed_kept")
        s_d = core.sem("down_done")
        s_out = core.sem("result_ready")
        s_st = [core.sem(f"result_stored{i}") for i in range(2)]

        block = ctx.enter_context(nc.Block())

        def rounds(n):
            matrix, part = n // 4, n % 4
            if matrix < 2:
                blocks = [(part * 8 + k) * 128 for k in range(K8)]
                target = (w_gate, w_up)[matrix][:, :, part * 128:(part + 1) * 128]
                return blocks, target, (lambda p: p)
            blocks = [((2 * part + a) * F4 + k) * 128 for k in range(F4) for a in range(2)]
            target = w_down[:, :, part * 256:(part + 1) * 256]
            return blocks, target, (lambda p: p.rearrange("p (k a) n -> p k (a n)", a=2))

        @block.sync
        def _(sp):
            def store(i, slot):
                sp.wait_ge(s_out, i + 1)
                sp.dma_start(out[bass.ds(i * T, T), :], result[:, slot]).then_inc(s_st[slot], 16)

            with sp.Fori(0, NT - 1, 2) as i:
                for p in range(2):
                    store(i + p, p)
            for p in range(2):
                sp.wait_ge(s_st[p], 16 * NT // 2)

        @block.gpsimd
        def _(pool):
            pool.tensor_copy(ident_b[:], core.ident[:]).then_inc(s_ib, 1)

            def limit(i, slot):
                pool.wait_ge(s_m, 4 * i + 4)
                pool.wait_ge(s_lift, i - 1)
                core.passed(pool)
                pool.tensor_scalar(small[:, slot], z[:, slot], most[:, slot, 3:4], 127.0, ALU.mult, ALU.min).then_inc(s_small, 1)

            def limit_hidden(i):
                pool.wait_ge(s_m2, 4 * i + 4)
                pool.wait_ge(s_lift2, i)
                core.passed(pool)
                pool.tensor_scalar(small2[:], hid[:], most2[:, 3:4], 127.0, ALU.mult, ALU.min).then_inc(s_small2, 1)

            pool.wait_ge(s_m, 4)
            pool.tensor_scalar(small[:, 0], z[:, 0], most[:, 0, 3:4], 127.0, ALU.mult, ALU.min).then_inc(s_small, 1)
            with pool.Fori(0, NT - 3, 2) as i:
                for p in range(2):
                    limit(i + p + 1, 1 - p)
                    limit_hidden(i + p)
            limit(NT - 1, 1)
            limit_hidden(NT - 2)
            limit_hidden(NT - 1)

        @block.scalar
        def _(act):
            def normalise(i, slot, reuse=True):
                if reuse:
                    act.wait_ge(s_small, i - 1)
                col = bass.ds(i, 1)
                act.activation(z[:, slot], rows[:, col, :].rearrange("p a n -> p (a n)"), ACT.Identity,
                               scale=core.rstd[:, col], bias=core.ln_shift[:, col]).then_inc(s_z, 1)

            def round_x(i, slot, reuse=True):
                act.wait_ge(s_lift, i + 1)
                if reuse:
                    act.wait_ge(s_xt, i - 1)
                act.activation(xq[:, slot], lifted[:, slot], ACT.Copy, bias=-MAGIC).then_inc(s_xq, 1)

            def silu(i, slot):
                act.wait_ge(s_gu, i + 1)
                act.wait_ge(s_hid, i)
                act.activation(gate[:], p_gu[0:T, slot, 0, :], ACT.Silu, scale=factor[:, slot, 0:1]).then_inc(s_gate, 1)

            def round_hidden(i):
                act.wait_ge(s_lift2, i + 1)
                act.wait_ge(s_ht, i)
                act.activation(hq[:], lifted2[:], ACT.Copy, bias=-MAGIC).then_inc(s_hq, 1)

            def keep_hidden(i):
                act.wait_ge(s_ht, i + 1)
                act.wait_ge(s_d, i)
                act.activation(ht[:], p_tr[:, 1, 0:F4, 0:T], ACT.Copy).then_inc(s_hk, 1)

            normalise(0, 0, reuse=False)
            normalise(1, 1, reuse=False)
            for n in range(1, 12, 2):
                blocks, target, view = rounds(n)
                act.wait_ge(s_wt, n + 1)
                act.activation(target, view(p_tr[:, 1]), ACT.Copy).then_inc(s_wk[1], 1)
            round_x(0, 0, reuse=False)

            def tile(i, slot, more, two_more=True):
                if more:
                    if two_more:
                        normalise(i + 2, slot)
                    round_x(i + 1, 1 - slot)
                silu(i, slot)
                round_hidden(i)
                keep_hidden(i)

            normalise_ahead = NT - 2
            round_x(1, 1, reuse=False)
            silu(0, 0)
            normalise(2, 0)
            round_hidden(0)
            keep_hidden(0)
            silu(1, 1)
            round_x(2, 0)
            normalise(3, 1)
            round_hidden(1)
            keep_hidden(1)
            with act.Fori(2, normalise_ahead - 1, 2) as i:
                for p in range(2):
                    silu(i + p, p)
                    round_x(i + p + 1, 1 - p)
                    normalise(i + p + 2, p)
                    round_hidden(i + p)
                    keep_hidden(i + p)
            silu(NT - 2, 0)
            round_x(NT - 1, 1)
            round_hidden(NT - 2)
            keep_hidden(NT - 2)
            silu(NT - 1, 1)
            round_hidden(NT - 1)
            keep_hidden(NT - 1)

        @block.vector
        def _(dve):
            def row_scale(i, values, most, s, factors, slot):
                dve.tensor_reduce(most[:, 0:1], values, AX.X, ALU.max, apply_absolute_value=True).then_inc(s, 1)
                dve.wait_ge(s, 4 * i + 1)
                dve.tensor_scalar(most[:, 1:2], most[:, 0:1], 1e-5, None, ALU.max).then_inc(s, 1)
                dve.wait_ge(s, 4 * i + 2)
                dve.reciprocal(most[:, 2:3], most[:, 1:2]).then_inc(s, 1)
                for n in factors:
                    dve.scalar_tensor_tensor(factor[:, slot, n:n + 1], most[:, 1:2], 1.0 / 127.0,
                                             core.w_mean[0:T, n:n + 1], ALU.mult, ALU.mult)
                dve.wait_ge(s, 4 * i + 3)
                dve.tensor_scalar(most[:, 3:4], most[:, 2:3], 127.0, None, ALU.mult).then_inc(s, 1)

            def scale_x(i, slot, reuse=True):
                dve.wait_ge(s_z, i + 1)
                if reuse:
                    dve.wait_ge(s_small, i - 1)
                    dve.wait_ge(s_hid, i - 1)
                row_scale(i, z[:, slot], most[:, slot], s_m, (0, 1), slot)

            def lift(i, slot, reuse=True):
                dve.wait_ge(s_small, i + 1)
                if reuse:
                    dve.wait_ge(s_xq, i - 1)
                dve.tensor_scalar(lifted[:, slot], small[:, slot], -128.0, MAGIC, ALU.max, ALU.add).then_inc(s_lift, 1)

            def keep_x(i, slot, reuse=True):
                dve.wait_ge(s_xt, i + 1)
                if reuse:
                    dve.wait_ge(s_gu, i - 1)
                dve.tensor_copy(xt[:, slot], p_tr[:, 0, :, 0:T]).then_inc(s_xk, 1)

            def hidden(i, slot):
                dve.wait_ge(s_gate, i + 1)
                dve.wait_ge(s_small2, i)
                dve.scalar_tensor_tensor(hid[:], p_gu[0:T, slot, 1, :], factor[:, slot, 1:2], gate[:], ALU.mult,
                                         ALU.mult).then_inc(s_hid, 1)
                dve.wait_ge(s_hid, i + 1)
                dve.wait_ge(s_out, i)
                row_scale(i, hid[:], most2, s_m2, (2,), 0)

            def lift_hidden(i):
                dve.wait_ge(s_small2, i + 1)
                dve.wait_ge(s_hq, i)
                dve.tensor_scalar(lifted2[:], small2[:], -128.0, MAGIC, ALU.max, ALU.add).then_inc(s_lift2, 1)

            def finish(i, slot, reuse=True):
                dve.wait_ge(s_d, i + 1)
                if reuse:
                    dve.wait_ge(s_st[slot], 8 * (i - slot))
                dve.scalar_tensor_tensor(result[:, slot].rearrange("p (b n) -> p b n", b=2), p_d[0:T], factor[:, 0, 2:3],
                                         rows[:, bass.ds(i, 1), :].rearrange("p a (b n) -> p (a b) n", b=2),
                                         ALU.mult, ALU.add).then_inc(s_out, 1)

            scale_x(0, 0, reuse=False)
            for n in range(0, 12, 2):
                blocks, target, view = rounds(n)
                dve.wait_ge(s_wt, n + 1)
                dve.tensor_copy(target, view(p_tr[:, 0])).then_inc(s_wk[0], 1)
            lift(0, 0, reuse=False)
            scale_x(1, 1, reuse=False)
            keep_x(0, 0, reuse=False)
            lift(1, 1, reuse=False)

            def tile(i, slot, ahead=2, reuse=True):
                if ahead > 0:
                    keep_x(i + 1, 1 - slot, reuse)
                hidden(i, slot)
                if ahead > 1:
                    scale_x(i + 2, slot)
                lift_hidden(i)
                if ahead > 1:
                    lift(i + 2, slot)
                finish(i, slot, reuse)

            tile(0, 0, reuse=False)
            tile(1, 1, reuse=True)
            with dve.Fori(2, NT - 3, 2) as i:
                for p in range(2):
                    tile(i + p, p)
            tile(NT - 2, 0, ahead=1)
            tile(NT - 1, 1, ahead=0)

        @block.tensor
        def _(pe):
            pe.wait_ge(s_ib, 1)
            for n in range(12):
                if n >= 2:
                    pe.wait_ge(s_wk[n % 2], n // 2)
                blocks, _, _ = rounds(n)
                for b, at in enumerate(blocks):
                    last = pe.transpose(p_tr[:, n % 2, b, :], core.ternary[:, n // 4, at:at + 128], ident_b[:])
                last.then_inc(s_wt, 1)
            for p in range(2):
                pe.wait_ge(s_wk[p], 6)

            def transpose_x(i, slot):
                pe.wait_ge(s_xq, i + 1)
                pe.wait_ge(s_xk, i)
                for k in range(K8):
                    last = pe.transpose(p_tr[:, 0, k, 0:T], xq[:, slot, k * 128:(k + 1) * 128], ident_b[0:T, 0:T])
                last.then_inc(s_xt, 1)

            def gate_up(i, slot, reuse=True):
                pe.wait_ge(s_xk, i + 1)
                if reuse:
                    pe.wait_ge(s_hid, i - 1)
                for n, w in enumerate((w_gate, w_up)):
                    for k in range(K8):
                        last = pe.matmul(p_gu[0:T, slot, n, :], xt[:, slot, k, :], w[:, k, :], start=(k == 0), stop=(k == K8 - 1))
                last.then_inc(s_gu, 1)

            def down(i):
                pe.wait_ge(s_hq, i + 1)
                pe.wait_ge(s_hk, i)
                for k in range(F4):
                    last = pe.transpose(p_tr[:, 1, k, 0:T], hq[:, k * 128:(k + 1) * 128], ident_b[0:T, 0:T])
                last.then_inc(s_ht, 1)
                pe.wait_ge(s_hk, i + 1)
                pe.wait_ge(s_out, i)
                for n in range(2):
                    for k in range(F4):
                        last = pe.matmul(p_d[0:T, n, :], ht[:, k, :], w_down[:, k, n * 512:(n + 1) * 512],
                                         start=(k == 0), stop=(k == F4 - 1))
                last.then_inc(s_d, 1)

            transpose_x(0, 0)
            gate_up(0, 0, reuse=False)
            transpose_x(1, 1)
            gate_up(1, 1, reuse=False)
            down(0)
            with pe.Fori(2, NT - 1, 2) as i:
                for p in range(2):
                    transpose_x(i + p, p)
                    gate_up(i + p, p)
                    down(i + p - 1)
            down(NT - 1)


def gps_layer_kernel(nc, inputs, out):
    with ExitStack() as stack:
        core = Core(nc, stack, inputs, out)
        core.ident = core.keep("ident", [128, 128], F32)
        core.ident_ready = core.sem("ident_ready")
        core.mean = core.keep("row_sums", [T, NT], F32)
        core.negmean = core.keep("neg_means", [T, NT], F32)
        core.var = core.keep("variances", [T, NT], F32)
        core.root = core.keep("roots", [T, NT], F32)
        core.tmp = core.keep("first_rstd", [T, NT], F32)
        core.rstd = core.keep("rstd", [T, NT], F32)
        core.rstd2 = core.keep("rstd2", [T, NT], F32)
        core.ln_scale = core.keep("ln_scale", [T, NT], F32)
        core.ln_shift = core.keep("ln_shift", [T, NT], F32)
        core.xn_shift = core.keep("xn_shift", [T, NT], F32)
        core.gnn_dram = nc.dram_tensor("gnn_dram", (N, D), F32).ap()
        core.ternary_dram = [nc.dram_tensor(f"ternary_dram{n}", (128, FF * D // 128), BF16).ap() for n in range(3)]
        core.w_mean = core.keep("w_mean", [128, 3], F32)
        core.al = core.keep("al", [T, NT], F32)
        core.ar = core.keep("ar", [T, NT], F32)
        with ExitStack() as gnn:
            core.counts = gnn.enter_context(nc.sbuf_tensor("counts", [T, NT, N], U16))
            with nc.sbuf_tensor("w_hi", [128, K8, D], F32R, side="right") as w_hi, \
                 nc.sbuf_tensor("w_lo", [128, K8, D], F32R, side="right") as w_lo:
                count_edges(core, w_hi, w_lo)
                core.h_hi = gnn.enter_context(nc.sbuf_tensor("h_hi", [T, NT, H_EXT], F32R))
                core.h_lo = gnn.enter_context(nc.sbuf_tensor("h_lo", [T, NT, H_EXT], F32R))
                node_features(core, w_hi, w_lo)
            attend_over_edges(core)
        core.attn_dram = nc.dram_tensor("attn_dram", (D, N), F32).ap()
        core.cols = core.keep("columns", [128, COLUMN_COUNT], F32)
        with ExitStack() as mix:
            core.x2_hi = mix.enter_context(nc.sbuf_tensor("x2_hi", [128, K8, N], F32R))
            core.x2_lo = mix.enter_context(nc.sbuf_tensor("x2_lo", [128, K8, N], F32R))
            transpose_second_norm(core)
            linear_attention(core)
            core.renew_semaphores()
        core.rows = core.keep("rows", [T, NT, D], F32)
        project_attention(core)
        core.ternary = core.keep("ternary", [128, 3, FF * D // 128], BF16)
        feed_forward(core)
        quantised_forward(core)


_INS = ["x", "src", "dst", "L0_gnn_W", "L0_gnn_a", "L0_mix_proj_mat", "L0_mix_wq", "L0_mix_bq", "L0_mix_wk",
        "L0_mix_bk", "L0_mix_wv", "L0_mix_bv", "L0_mix_wo", "L0_mix_bo", "L0_mix_ln1_g", "L0_mix_ln1_b", "L0_mix_w1",
        "L0_mix_b1", "L0_mix_w2", "L0_mix_b2", "L0_mix_ln2_g", "L0_mix_ln2_b", "L0_ffn_w_gate", "L0_ffn_w_up",
        "L0_ffn_w_down"]


def kernel(**inputs):
    import numpy as _np
    import concourse.bacc as _bacc
    from concourse import mybir as _mybir
    from concourse.bass_utils import run_bass_kernel_spmd as _run

    nc = _bacc.Bacc("TRN2", target_bir_lowering=False, num_devices=1)
    arrays, args = {}, {}
    for name in _INS:
        a = _np.ascontiguousarray(inputs[name])
        arrays[f"in_{name}_dram"] = a
        args[name] = nc.dram_tensor(f"in_{name}_dram", a.shape, _mybir.dt.from_np(a.dtype), kind="ExternalInput").ap()
    out = nc.dram_tensor("out_dram", (N, D), F32, kind="ExternalOutput").ap()
    gps_layer_kernel(nc, args, out)
    r = _run(nc, [arrays], core_ids=[0])
    return r.results[0]["out_dram"]
```

```python
from contextlib import ExitStack

import concourse.bass as bass
from concourse import mybir

ALU = mybir.AluOpType
ACT = mybir.ActivationFunctionType
AX = mybir.AxisListType
F32 = mybir.dt.float32
F32R = mybir.dt.float32r
BF16 = mybir.dt.bfloat16
FP16 = mybir.dt.float16
I32 = mybir.dt.int32
U16 = mybir.dt.uint16

N, D = 1250, 1024
E = 20000
T = 125
NT = N // T
K8 = D // 128
C = 4
GROUP = C * T
NG = E // GROUP
FF = 512
HEADS, DH, KMAP = 16, 64, 128
PAIRS = HEADS // 2
LN_EPS = 1e-5
GNN_EPS = 1e-5
SLOPE = 0.1
FLT_MAX = 3.4028234e38
MAGIC = 12582912.0
TWO_PI = 6.2831850051879883
HALF_PI = 1.5707963267948966
THIRDS = [(0, 418), (418, 416), (834, 416)]
H_EXT = D + 2
H_COLS = H_EXT // 3


def f32(ap):
    return ap.bitcast(F32)


class Core:

    def __init__(self, nc, stack, inputs, out):
        self.nc, self.stack, self.inp, self.out = nc, stack, inputs, out
        self.sems = []
        self.waits_passed = nc.alloc_semaphore(name="waits_passed")

        self.x_in = self.keep("x_in", [T, 2, D], F32)
        self.x_loaded = [nc.alloc_semaphore(name=f"x_loaded{i}") for i in range(2)]
        self.x_base = 0

    def load_x(self, sp, i, slot):
        sp.dma_start(self.x_in[:, slot, :], self.inp["x"][bass.ds(i * T, T), :]).then_inc(self.x_loaded[slot], 16)

    def wait_x(self, engine, i, slot):
        engine.wait_ge(self.x_loaded[slot], self.x_base + 16 + 8 * (i - slot))

    def next_reading(self):
        self.x_base += 8 * NT

    def load_mix(self, sp, which, j):
        weight = self.inp[MIX_WEIGHTS[which]]
        sp.dma_start(self.mix_in[which][:], weight[:, bass.ds(j * 128, 128)].rearrange("(k p) n -> p k n", p=128)
                     ).then_inc(self.mix_loaded[which], 16)

    def passed(self, engine):
        engine.sem_inc(self.waits_passed, 1)

    def sem(self, name):
        self.sems.append(self.nc.alloc_semaphore(name=name))
        return self.sems[-1]

    def renew_semaphores(self):
        self.nc.clear_and_free_semaphores(self.sems)
        self.nc.all_engine_barrier()
        self.sems = []

    def keep(self, name, shape, dt):
        return self.stack.enter_context(self.nc.sbuf_tensor(name, shape, dt))


def spread(vector, rows):
    return vector.rearrange("(a n) -> a n", a=1).to_broadcast([rows, vector.shape[0]])


def count_edges(core, w_hi, w_lo):
    nc, inp = core.nc, core.inp
    x, W = inp["x"], inp["L0_gnn_W"]
    with ExitStack() as ctx:
        def sb(name, shape, dt):
            return ctx.enter_context(nc.sbuf_tensor(name, shape, dt))

        def ps(name, shape, dt=F32):
            return ctx.enter_context(nc.psum_tensor(name, shape, dt))

        edges_i = sb("edges_i", [NG, 2, GROUP], I32)
        edges_f = sb("edges_f", [NG, 2, GROUP], F32)
        bounds = sb("bounds", [NG, 2], F32)
        ends = sb("ends", [T, NG, 2 * C], F32)
        now = sb("now", [T, 2 * C], F32)
        iota_i = sb("iota_i", [T, N], I32)
        iota_h = sb("iota_h", [T, N], FP16)
        tab_i = sb("tab_i", [1, 3, NT, NG], I32)
        tab = sb("tab", [1, 3, NT, NG], F32)
        hit = sb("hit", [1, 3, NT, NG], F32)
        row2 = sb("row2", [1, 2, NG], F32)
        span = sb("span", [1, 4, NT], F32)
        span_i = sb("span_i", [1, NT, 2], I32)
        iota_t = sb("iota_t", [T, T], FP16)
        hot_s = sb("hot_s", [T, C, N], BF16)
        hot_d = sb("hot_d", [T, C, T], BF16)
        zeros = sb("zeros", [T, T], BF16)
        zero_rows = sb("zero_rows", [T, 418], BF16)
        x_in = core.x_in
        junk = sb("junk", [T, D], F32)
        w_in = sb("w_in", [128, 2, D], F32)

        f_in = sb("f_in", [128, 2, FF * D // 128], F32)
        below = sb("below", [128, FF * D // 128], BF16)
        ternary = sb("ternary_out", [128, FF * D // 128], BF16)
        ones = sb("ones", [128, 128], F32)
        mag = sb("magnitude_sums", [128, 3], F32)
        w_scale = sb("w_scale", [128, 3], F32)

        p_ends = ps("p_ends", [128, 512])
        p_bound = ps("p_bound", [128, 512])
        p_cnt = ps("p_cnt", [128, 2, 3, 512])

        s_edges = core.sem("edges_loaded")
        s_efl = core.sem("edges_as_floats")
        s_prep = core.sem("edge_tables_step")
        s_ident = core.ident_ready
        s_iota = core.sem("iotas_written")
        s_iotah = core.sem("iota_half_ready")
        s_tr = core.sem("edge_transposes_done")
        s_span = core.sem("spans_ready")
        s_step = core.sem("span_step")
        s_now = core.sem("group_at_hand")
        s_hot = core.sem("onehots_ready")
        s_used = core.sem("onehot_slots_free")
        s_zero = core.sem("zero_operands_ready")
        s_tile = core.sem("tile_counted")
        s_kept = core.sem("counts_kept")
        s_xfree = core.sem("x_summed")
        s_chain = core.sem("stat_step")
        s_w = [core.sem(f"w_loaded{i}") for i in range(2)]
        s_whi = core.sem("w_hi_done")
        s_wlo = core.sem("w_lo_done")

        s_fin = [core.sem(f"feed_forward_weight_loaded{i}") for i in range(2)]
        s_again = core.sem("up_loaded_again")
        s_mag = core.sem("magnitudes_summed")
        s_tot = core.sem("magnitudes_totalled")
        s_sc = core.sem("weight_scale_step")
        s_scaled = core.sem("weight_scaled")
        s_tern = core.sem("ternary_step")
        s_ones = core.sem("ones_written1")
        s_tst = core.sem("ternary_stored")

        def groups_of(engine, t, registers):
            engine.reg_load(list(registers), span_i[0:1, bass.ds(t, 1), :].rearrange("p t n -> p (t n)"))
            return (engine.snap(registers[0], min_val=0, max_val=NG - 1), engine.snap(registers[1], min_val=1, max_val=NG))

        block = ctx.enter_context(nc.Block())
        GATE, UP, DOWN = 0, 1, 2

        def ffn_weight(n):
            w = (inp["L0_ffn_w_gate"], inp["L0_ffn_w_up"], inp["L0_ffn_w_down"])[n]
            return w.rearrange("(a p) n -> p a n", p=128)

        def in_slot(slot, n):
            return f_in[:, slot, :].rearrange("p (a n) -> p a n", a=8 if n == DOWN else 4)

        LOADS = [(GATE, 0), (UP, 1), (DOWN, 0), (GATE, 1)]

        @block.sync
        def _(sp):
            sp.dma_start(edges_i[:, 0, :], inp["src"].rearrange("(g e) -> g e", g=NG)).then_inc(s_edges, 16)
            sp.dma_start(edges_i[:, 1, :], inp["dst"].rearrange("(g e) -> g e", g=NG)).then_inc(s_edges, 16)
            for n, slot in LOADS:
                if n != GATE and slot == 0:
                    sp.wait_ge(s_mag, 1)
                if n == GATE and slot == 1:
                    sp.wait_ge(s_mag, 2)
                sp.dma_start(in_slot(slot, n), ffn_weight(n)).then_inc(s_fin[slot], 16)
            for k in range(K8):
                if k >= 2:
                    sp.wait_ge(s_wlo, k - 1)
                sp.dma_start(w_in[:, k % 2, :], W[k * 128:(k + 1) * 128, :]).then_inc(s_w[k % 2], 16)

            for p in range(2):
                core.load_x(sp, p, p)
            with sp.Fori(2, NT - 1, 2) as i:
                for p in range(2):
                    sp.wait_ge(s_xfree, i + p - 1)
                    core.load_x(sp, i + p, p)
            for p in range(2):
                sp.wait_ge(s_xfree, NT - 1 + p)
                core.load_x(sp, p, p)

        @block.gpsimd
        def _(pool):
            pool.memset(core.ident[:], 0.0).then_inc(s_prep, 1)
            pool.memset(zeros[:], 0.0).then_inc(s_zero, 1)
            pool.memset(zero_rows[:], 0.0).then_inc(s_zero, 1)
            pool.memset(ones[:], 1.0).then_inc(s_ones, 1)
            pool.iota(tab_i[:, 0, :, :], pattern=[[T, NT], [0, NG]], base=0, channel_multiplier=0).then_inc(s_iota, 1)
            pool.iota(tab_i[:, 1, :, :], pattern=[[T, NT], [0, NG]], base=T, channel_multiplier=0).then_inc(s_iota, 1)
            pool.iota(tab_i[:, 2, :, :], pattern=[[0, NT], [1, NG]], base=-NG, channel_multiplier=0).then_inc(s_iota, 1)
            pool.iota(iota_i[:], pattern=[[1, N]], base=0, channel_multiplier=0).then_inc(s_iota, 1)
            pool.wait_ge(s_prep, 1)
            pool.affine_select(out=core.ident[:], in_=core.ident[:], compare_op=ALU.not_equal, fill=1.0,
                               base=0, pattern=[[-1, 128]], channel_multiplier=1).then_inc(s_ident, 1)
            for k in range(K8):
                pool.wait_ge(s_whi, k + 1)
                pool.tensor_tensor(w_lo[:, k, :], w_in[:, k % 2, :], f32(w_hi[:, k, :]), ALU.subtract).then_inc(s_wlo, 1)
            pool.wait_ge(s_sc, 2)
            for step, (n, slot) in enumerate(((DOWN, 0), (GATE, 1), (UP, 0))):
                pool.wait_ge(s_scaled, step + 1)
                pool.tensor_scalar(below[:], f_in[:, slot, :], -0.5, None, ALU.is_lt)
                pool.wait_ge(s_tst, 16 * step)
                pool.tensor_scalar(ternary[:], f_in[:, slot, :], 0.5, None, ALU.is_gt).then_inc(s_tern, 1)
                pool.wait_ge(s_tern, 2 * step + 1)
                pool.tensor_tensor(ternary[:], ternary[:], below[:], ALU.subtract).then_inc(s_tern, 1)
                pool.wait_ge(s_tern, 2 * step + 2)
                if n == DOWN:
                    pool.dma_start(in_slot(0, UP), ffn_weight(UP)).then_inc(s_again, 16)
                pool.dma_start(core.ternary_dram[n], ternary[:]).then_inc(s_tst, 16)
            pool.wait_ge(s_tst, 48)

        @block.scalar
        def _(act):
            def split_w(k):
                act.wait_ge(s_w[k % 2], 16 * (k // 2 + 1))
                act.activation(w_hi[:, k, :], w_in[:, k % 2, :], ACT.Copy).then_inc(s_whi, 1)

            for n, slot, loads in ((GATE, 0, 1), (UP, 1, 1), (DOWN, 0, 2)):
                act.wait_ge(s_fin[slot], 16 * loads)
                act.wait_ge(s_mag, n)
                act.activation(below[:], f_in[:, slot, :], ACT.Abs, accum_out=mag[:, n:n + 1]).then_inc(s_mag, 1)
            for k in range(K8):
                split_w(k)

            def sums(t, slot):
                core.wait_x(act, t, slot)
                mean, var, col = core.mean, core.var, bass.ds(t, 1)
                act.activation(junk[:], x_in[:, slot, :], ACT.Identity, accum_out=mean[:, col]).then_inc(s_chain, 1)
                act.wait_ge(s_chain, 1 + 3 * t)
                act.mul(core.negmean[:, col], mean[:, col], -1.0 / D).then_inc(s_chain, 1)
                act.wait_ge(s_chain, 2 + 3 * t)
                act.activation(junk[:], x_in[:, slot, :], ACT.Square, bias=core.negmean[:, col],
                               accum_out=var[:, col]).then_inc(s_chain, 1)
                act.wait_ge(s_chain, 3 + 3 * t)
                act.sem_inc(s_xfree, 1)

            def keep_counts(t, par):
                act.wait_ge(s_tile, t + 1)
                for n, (a, w) in enumerate(THIRDS):
                    last = act.activation(core.counts[:, bass.ds(t, 1), a:a + w], p_cnt[0:T, par, n:n + 1, 0:w], ACT.Copy)
                last.then_inc(s_kept, 1)

            def scale_weight(n, slot, s_in, loads):
                act.wait_ge(s_in, 16 * loads)
                act.activation(f_in[:, slot, :], f_in[:, slot, :], ACT.Copy, scale=w_scale[:, n:n + 1]).then_inc(s_scaled, 1)

            for p in range(2):
                sums(p, p)
                keep_counts(p, p)
            act.wait_ge(s_sc, 2)
            scale_weight(DOWN, 0, s_fin[0], 2)
            scale_weight(GATE, 1, s_fin[1], 2)
            for first, last in ((2, NT - 4), (NT - 4, NT)):
                with act.Fori(first, last - 1, 2) as i:
                    for p in range(2):
                        sums(i + p, p)
                        keep_counts(i + p, p)
                if last < NT:
                    scale_weight(UP, 0, s_again, 1)

        @block.vector
        def _(dve):
            dve.wait_ge(s_edges, 32)
            dve.tensor_copy(edges_f[:], edges_i[:]).then_inc(s_efl, 1)
            dve.wait_ge(s_efl, 1)
            dve.tensor_reduce(bounds[:, 0:1], edges_f[:, 1, :], AX.X, ALU.min).then_inc(s_efl, 1)
            dve.tensor_reduce(bounds[:, 1:2], edges_f[:, 1, :], AX.X, ALU.max).then_inc(s_efl, 1)
            dve.wait_ge(s_iota, 4)
            dve.tensor_copy(iota_h[:], iota_i[:]).then_inc(s_iotah, 1)
            dve.tensor_copy(tab[:], tab_i[:]).then_inc(s_iotah, 1)
            dve.wait_ge(s_tr, 1)
            dve.tensor_copy(ends[:], p_ends[0:T, 0:2 * C * NG].rearrange("p (a g) -> p g a", a=2 * C)).then_inc(s_iotah, 1)
            dve.tensor_copy(row2[:], p_bound[0:1, 0:2 * NG].rearrange("p (a g) -> p a g", a=2)).then_inc(s_iotah, 1)
            dve.wait_ge(s_iotah, 4)
            least = row2[:, 0:1, :].to_broadcast([1, NT, NG])
            most = row2[:, 1:2, :].to_broadcast([1, NT, NG])
            step = [0]

            def chain(ins):
                step[0] += 1
                ins.then_inc(s_step, 1)
                dve.wait_ge(s_step, step[0])

            chain(dve.tensor_tensor(hit[:, 0], least, tab[:, 1], ALU.is_lt))
            chain(dve.tensor_tensor(hit[:, 1], most, tab[:, 0], ALU.is_ge))
            chain(dve.tensor_tensor(hit[:, 0], hit[:, 0], hit[:, 1], ALU.mult))
            chain(dve.tensor_tensor(hit[:, 1], hit[:, 0], tab[:, 2], ALU.mult))
            chain(dve.tensor_reduce(span[:, 0], hit[:, 1], AX.X, ALU.min))
            chain(dve.tensor_scalar(span[:, 0], span[:, 0], float(NG), float(NG - 1), ALU.add, ALU.min))
            chain(dve.tensor_scalar(hit[:, 2], tab[:, 2], float(NG + 1), None, ALU.add))
            chain(dve.tensor_tensor(hit[:, 1], hit[:, 0], hit[:, 2], ALU.mult))
            chain(dve.tensor_reduce(span[:, 1], hit[:, 1], AX.X, ALU.max))
            chain(dve.tensor_scalar(span[:, 2], span[:, 0], 1.0, None, ALU.add))
            chain(dve.tensor_tensor(span[:, 3], span[:, 1], span[:, 2], ALU.max))
            chain(dve.tensor_copy(span_i[:, :, 0], span[:, 0]))
            dve.tensor_copy(span_i[:, :, 1], span[:, 3]).then_inc(s_span, 1)
            dve.wait_ge(s_span, 1)

            def onehots(chunks):
                for j in range(C):
                    if j % 2 == 0:
                        dve.wait_ge(s_used, chunks + j + 2)
                    dve.tensor_scalar(hot_s[:, j, :], iota_h[:], now[:, j:j + 1], None, ALU.is_equal)
                    dve.tensor_scalar(hot_d[:, j, :], iota_t[:], now[:, C + j:C + j + 1], None,
                                      ALU.is_equal).then_inc(s_hot, 1)

            with dve.register("chunks_done") as done, dve.register("copies_made") as copies, \
                 dve.register("first_group") as r0, dve.register("past_group") as r1:
                bounds_r = (r0, r1)
                dve.reg_mov(done, 0)
                dve.reg_mov(copies, 0)
                def tile_onehots(t):
                    first, past = groups_of(dve, t, bounds_r)
                    dve.wait_ge(s_hot, dve.snap(done, min_val=0, max_val=NT * NG * C))
                    dve.tensor_copy(iota_t[:], iota_h[:, bass.ds(t * T, T)]).then_inc(s_now, 1)
                    dve.reg_add(copies, copies, 1)
                    with dve.Fori(first, past) as g:
                        before = dve.snap(done, min_val=0, max_val=NT * NG * C)
                        dve.wait_ge(s_hot, before)
                        dve.tensor_copy(now[:], ends[:, bass.ds(g, 1), :].rearrange("p a c -> p (a c)")).then_inc(s_now, 1)
                        dve.reg_add(copies, copies, 1)
                        dve.wait_ge(s_now, dve.snap(copies, min_val=0, max_val=NT * (NG + 1)))
                        onehots(before)
                        dve.reg_add(done, done, C)

                with dve.Fori(0, 2) as t:
                    tile_onehots(t)
                dve.wait_ge(s_tot, 1)
                dve.tensor_scalar(core.w_mean[:], p_bound[:, 0:3], 1.0 / (FF * D), 1e-5, ALU.mult, ALU.max).then_inc(s_sc, 1)
                dve.wait_ge(s_sc, 1)
                dve.reciprocal(w_scale[:], core.w_mean[:]).then_inc(s_sc, 1)
                with dve.Fori(2, NT) as t:
                    tile_onehots(t)

        @block.tensor
        def _(pe):
            pe.wait_ge(s_ident, 1)
            pe.wait_ge(s_efl, 3)
            ident = core.ident
            for a in range(2 * C):
                pe.transpose(p_ends[0:T, a * NG:(a + 1) * NG], edges_f[:, a // C, (a % C) * T:(a % C + 1) * T],
                             ident[0:NG, 0:NG])
            for a in range(2):
                last = pe.transpose(p_bound[0:1, a * NG:(a + 1) * NG], bounds[:, a:a + 1], ident[0:NG, 0:NG])
            last.then_inc(s_tr, 1)
            pe.sem_inc(s_used, C)
            pe.wait_ge(s_zero, 2)
            pe.wait_ge(s_span, 1)

            def count_tile(t, par, done, bounds_r):
                for n, (a, w) in enumerate(THIRDS):
                    pe.matmul(p_cnt[0:T, par, n, 0:w], zeros[:], zero_rows[:, 0:w], start=True, stop=False)
                first, past = groups_of(pe, t, bounds_r)
                with pe.Fori(first, past):
                    before = pe.snap(done, min_val=0, max_val=NT * NG * C)
                    for j in range(C):
                        pe.wait_ge(s_hot, before + j + 1)
                        for n, (a, w) in enumerate(THIRDS):
                            last = pe.matmul(p_cnt[0:T, par, n, 0:w], hot_d[:, j, :], hot_s[:, j, a:a + w],
                                             start=False, stop=False)
                        last.then_inc(s_used, 1)
                    pe.reg_add(done, done, C)
                for n, (a, w) in enumerate(THIRDS):
                    last = pe.matmul(p_cnt[0:T, par, n, 0:w], zeros[:], zero_rows[:, 0:w], start=False, stop=True)
                last.then_inc(s_tile, 1)

            with pe.register("chunks_done") as done, pe.register("first_group") as r0, pe.register("past_group") as r1:
                bounds_r = (r0, r1)
                pe.reg_mov(done, 0)
                for par in range(2):
                    count_tile(par, par, done, bounds_r)
                pe.wait_ge(s_mag, 3)
                pe.wait_ge(s_ones, 1)
                pe.matmul(p_bound[:, 0:3], ones[:], mag[:], start=True, stop=True).then_inc(s_tot, 1)
                with pe.Fori(2, NT - 1, 2) as i:
                    for par in range(2):
                        pe.wait_ge(s_kept, i + par - 1)
                        count_tile(i + par, par, done, bounds_r)


def node_features(core, w_hi, w_lo):
    nc, inp = core.nc, core.inp
    x = inp["x"]
    h_hi, h_lo = core.h_hi, core.h_lo
    with ExitStack() as ctx:
        def sb(name, shape, dt):
            return ctx.enter_context(nc.sbuf_tensor(name, shape, dt))

        def ps(name, shape, dt=F32):
            return ctx.enter_context(nc.psum_tensor(name, shape, dt))

        x_in = core.x_in
        xn = sb("xn", [T, D], F32)
        xt_hi = sb("xt_hi", [128, 2, K8, T], F32R)
        xt_lo = sb("xt_lo", [128, 2, K8, T], F32R)
        a_lr = sb("a_lr", [T, 2 * D], F32)
        p_tr = ps("p_tr", [128, 2, 512])
        p_h = ps("p_h", [128, 2, 2, 512])
        p_junk = ps("p_junk", [128, 2, 512])

        s_a = core.sem("a_loaded")
        s_step = core.sem("rstd_step")
        s_ones = core.sem("h_ones_written")
        s_xn = core.sem("xn_ready")
        s_tr = core.sem("xn_transposed")
        s_thi = core.sem("xt_hi_ready")
        s_tlo = core.sem("xt_lo_ready")
        s_h = core.sem("h_product_done")
        s_hhi = core.sem("h_hi_kept")
        s_hdone = core.sem("h_psum_free")
        s_dot = core.sem("dot_products_done")

        block = ctx.enter_context(nc.Block())

        @block.sync
        def _(sp):
            sp.dma_start(a_lr[:], inp["L0_gnn_a"].to_broadcast([T, 2 * D])).then_inc(s_a, 16)
            with sp.Fori(2, NT - 1, 2) as i:
                for p in range(2):
                    sp.wait_ge(s_xn, i + p - 1)
                    core.load_x(sp, i + p, p)
            for p in range(2):
                sp.wait_ge(s_xn, NT - 1 + p)
                core.load_x(sp, p, p)

        @block.gpsimd
        def _(pool):
            pool.memset(f32(h_hi[:, :, D:D + 1]), 1.0).then_inc(s_ones, 1)
            pool.memset(f32(h_hi[:, :, D + 1:]), 0.0).then_inc(s_ones, 1)
            pool.memset(f32(h_lo[:, :, D:]), 0.0).then_inc(s_ones, 1)
            pool.wait_ge(s_ones, 3)

        @block.scalar
        def _(act):
            act.wait_ge(s_step, 1)
            act.activation(core.root[:], core.var[:], ACT.Sqrt).then_inc(s_step, 1)

            def keep_xt_hi(i, slot, reuse=True):
                act.wait_ge(s_tr, i + 1)
                if reuse:
                    act.wait_ge(s_h, i - 1)
                act.activation(xt_hi[:, slot].rearrange("p (a k) t -> p a (k t)", a=2), p_tr[:, :, 0:4 * T],
                               ACT.Copy).then_inc(s_thi, 1)

            def keep_h_hi(i, slot):
                act.wait_ge(s_h, i + 1)
                act.activation(h_hi[:, bass.ds(i, 1), 0:D], p_h[0:T, slot], ACT.Copy).then_inc(s_hhi, 1)

            keep_xt_hi(0, 0, reuse=False)
            with act.Fori(1, NT - 2, 2) as i:
                for p in range(2):
                    keep_xt_hi(i + p, 1 - p)
                    keep_h_hi(i + p - 1, p)
            keep_xt_hi(NT - 1, 1)
            keep_h_hi(NT - 2, 0)
            keep_h_hi(NT - 1, 1)

        @block.vector
        def _(dve):
            mean, var, root, rstd, tmp = core.negmean, core.var, core.root, core.rstd, core.tmp
            dve.tensor_scalar(var[:], var[:], 1.0 / D, LN_EPS, ALU.mult, ALU.add).then_inc(s_step, 1)
            dve.wait_ge(s_step, 2)
            dve.reciprocal(tmp[:], root[:]).then_inc(s_step, 1)
            dve.wait_ge(s_step, 3)
            dve.tensor_tensor(root[:], var[:], tmp[:], ALU.mult).then_inc(s_step, 1)
            dve.wait_ge(s_step, 4)
            dve.tensor_tensor(var[:], root[:], tmp[:], ALU.mult).then_inc(s_step, 1)
            dve.wait_ge(s_step, 5)
            dve.tensor_scalar(root[:], var[:], -0.5, 1.5, ALU.mult, ALU.add).then_inc(s_step, 1)
            dve.wait_ge(s_step, 6)
            dve.tensor_tensor(rstd[:], root[:], tmp[:], ALU.mult).then_inc(s_step, 1)
            dve.wait_ge(s_step, 7)

            def normalise(i, slot, first=False):
                core.wait_x(dve, i, slot)
                if not first:
                    dve.wait_ge(s_tr, i)
                dve.tensor_scalar(xn[:], x_in[:, slot, :], mean[:, bass.ds(i, 1)], rstd[:, bass.ds(i, 1)],
                                  ALU.add, ALU.mult).then_inc(s_xn, 1)

            def keep_xt_lo(i, slot):
                dve.wait_ge(s_thi, i + 1)
                dve.tensor_tensor(xt_lo[:, slot].rearrange("p (a k) t -> p a (k t)", a=2), p_tr[:, :, 0:4 * T],
                                  f32(xt_hi[:, slot]).rearrange("p (a k) t -> p a (k t)", a=2),
                                  ALU.subtract).then_inc(s_tlo, 1)

            def keep_h(i, slot):
                dve.wait_ge(s_hhi, i + 1)
                dve.tensor_tensor(h_lo[:, bass.ds(i, 1), 0:D].rearrange("p a (b n) -> p (a b) n", b=2), p_h[0:T, slot],
                                  f32(h_hi[:, bass.ds(i, 1), 0:D]).rearrange("p a (b n) -> p (a b) n", b=2), ALU.subtract)
                for n, dot in enumerate((core.al, core.ar)):
                    dve.wait_ge(s_dot, 2 * i + n)
                    last = dve.scalar_tensor_tensor(
                        p_junk[0:T], p_h[0:T, slot], 1.0, a_lr[:, n * D:(n + 1) * D].rearrange("p (b n) -> p b n", b=2),
                        ALU.mult, ALU.mult, accum_out=dot[:, bass.ds(i, 1)])
                    last.then_inc(s_dot, 1)
                dve.wait_ge(s_dot, 2 * i + 2)
                dve.sem_inc(s_hdone, 1)

            normalise(0, 0, first=True)
            keep_xt_lo(0, 0)
            normalise(1, 1)
            dve.wait_ge(s_a, 16)
            with dve.Fori(1, NT - 2, 2) as i:
                for p in range(2):
                    keep_xt_lo(i + p, 1 - p)
                    normalise(i + p + 1, p)
                    keep_h(i + p - 1, p)
            keep_xt_lo(NT - 1, 1)
            keep_h(NT - 2, 0)
            keep_h(NT - 1, 1)

        @block.tensor
        def _(pe):
            def transposes(i, first=False):
                pe.wait_ge(s_xn, i + 1)
                if not first:
                    pe.wait_ge(s_tlo, i)
                for k in range(K8):
                    last = pe.transpose(p_tr[:, k // 4, (k % 4) * T:(k % 4 + 1) * T], xn[:, k * 128:(k + 1) * 128],
                                        core.ident[0:T, 0:T])
                last.then_inc(s_tr, 1)

            def products(i, slot, reuse=True):
                pe.wait_ge(s_tlo, i + 1)
                if reuse:
                    pe.wait_ge(s_hdone, i - 1)
                for n in range(2):
                    cols = slice(n * 512, (n + 1) * 512)
                    for k in range(K8):
                        for m, (left, right) in enumerate(((xt_lo, w_hi), (xt_hi, w_lo), (xt_hi, w_hi))):
                            last = pe.matmul(p_h[0:T, slot, n, :], left[:, slot, k, :], right[:, k, cols],
                                             start=(k == 0 and m == 0), stop=(k == K8 - 1 and m == 2))
                last.then_inc(s_h, 1)

            transposes(0, first=True)
            transposes(1)
            products(0, 0, reuse=False)
            with pe.Fori(1, NT - 2, 2) as i:
                for p in range(2):
                    transposes(i + p + 1)
                    products(i + p, 1 - p)
            products(NT - 1, 1)


def inverse_root(dve, s_step, at, var, root, tmp, rstd):
    dve.wait_ge(s_step, at)
    dve.reciprocal(tmp, root).then_inc(s_step, 1)
    dve.wait_ge(s_step, at + 1)
    dve.tensor_tensor(root, var, tmp, ALU.mult).then_inc(s_step, 1)
    dve.wait_ge(s_step, at + 2)
    dve.tensor_tensor(var, root, tmp, ALU.mult).then_inc(s_step, 1)
    dve.wait_ge(s_step, at + 3)
    dve.tensor_scalar(root, var, -0.5, 1.5, ALU.mult, ALU.add).then_inc(s_step, 1)
    dve.wait_ge(s_step, at + 4)
    dve.tensor_tensor(rstd, root, tmp, ALU.mult).then_inc(s_step, 1)
    dve.wait_ge(s_step, at + 5)


def attend_over_edges(core):
    nc, inp = core.nc, core.inp
    x, h_hi, h_lo, counts = inp["x"], core.h_hi, core.h_lo, core.counts
    with ExitStack() as ctx:
        def sb(name, shape, dt=F32):
            return ctx.enter_context(nc.sbuf_tensor(name, shape, dt))

        al_all = sb("al_all", [T, N])
        z = sb("z", [T, 2, NT, T])
        y = sb("y", [T, 2, NT, T])
        a_hi = sb("a_hi", [T, 2, NT, T], F32R)
        a_lo = sb("a_lo", [T, 2, NT, T], F32R)
        x_in = core.x_in
        low = sb("low", [T, 3, H_COLS])
        high = sb("high", [T, 3, H_COLS])
        elu = sb("elu", [T, 3, H_COLS])
        gnn = sb("gnn", [T, 2, D])
        junk = sb("junk3", [T, D])
        rsum = sb("rsum", [T, 2])
        nb = sb("nb", [T, NT])
        nb2 = sb("nb2", [T, NT])
        sum2 = sb("sum2", [T, NT])
        nmean2 = sb("nmean2", [T, NT])
        p_o = ctx.enter_context(nc.psum_tensor("p_o", [128, 2, 3, 512], F32))

        s_al = core.sem("al_spread_in_psum")
        s_alk = core.sem("al_spread_kept")
        s_nb = core.sem("nb_ready")
        s_z = core.sem("scores_ready")
        s_y = core.sem("leaky_ready")
        s_e = core.sem("edge_exp_ready")
        s_a = core.sem("edge_weights_ready")
        s_ahi = core.sem("a_hi_ready")
        s_alo = core.sem("a_lo_ready")
        s_o = core.sem("attended_in_psum")
        s_rs = core.sem("row_sum_step")
        s_m = core.sem("below_zero_ready")
        s_em = core.sem("below_zero_exp")
        s_hp = core.sem("above_zero_ready")
        s_elu = core.sem("elu_ready")
        s_gnn = core.sem("gnn_tile_ready")
        s_stat = core.sem("second_stat_step")
        s_st = core.gnn_stored
        s_step = core.sem("rstd2_step")

        block = ctx.enter_context(nc.Block())

        @block.sync
        def _(sp):
            for name in COLUMNS:
                sp.dma_start(core.vectors[COLUMN_AT[name], :], inp[name].rearrange("(k p) -> k p", p=128)
                             ).then_inc(core.vectors_loaded, 16)

            def store(i, slot):
                sp.wait_ge(s_gnn, i + 1)
                sp.dma_start(core.gnn_dram[bass.ds(i * T, T), :], gnn[:, slot, :]).then_inc(s_st[slot], 16)

            with sp.Fori(2, NT - 1, 2) as i:
                for p in range(2):
                    store(i + p - 2, p)
                    sp.wait_ge(s_stat, 4 * (i + p) - 4)
                    core.load_x(sp, i + p, p)
            for i in range(NT - 2, NT):
                store(i, i % 2)
                core.load_x(sp, i - NT + 2, i % 2)
        @block.gpsimd
        def _(pool):
            def weights_lo(i, slot):
                pool.wait_ge(s_ahi, i + 1)
                pool.tensor_tensor(a_lo[:, slot], z[:, slot], f32(a_hi[:, slot]), ALU.subtract).then_inc(s_alo, 1)

            def add_x(i, slot, reuse=True):
                pool.wait_ge(s_elu, i + 1)
                if reuse:
                    pool.wait_ge(s_st[slot], 8 * (i - slot))
                pool.tensor_tensor(gnn[:, slot, :], elu[:].rearrange("p a n -> p (a n)")[:, 0:D], x_in[:, slot, :],
                                   ALU.add).then_inc(s_gnn, 1)

            weights_lo(0, 0)
            weights_lo(1, 1)
            for i in range(2):
                weights_lo(i + 2, i)
                add_x(i, i, reuse=False)
            with pool.Fori(4, NT - 1, 2) as i:
                for p in range(2):
                    weights_lo(i + p, p)
                    add_x(i + p - 2, p)
            add_x(NT - 2, 0)
            add_x(NT - 1, 1)

        @block.scalar
        def _(act):
            act.wait_ge(s_al, 1)
            for b in range(3):
                w = min(4, NT - 4 * b) * T
                last = act.activation(al_all[:, 4 * b * T:4 * b * T + w], p_o[0:T, 1, b, 0:w], ACT.Copy)
            last.then_inc(s_alk, 1)

            def exps(i, slot):
                act.wait_ge(s_y, i + 1)
                act.activation(y[:, slot], y[:, slot], ACT.Exp, scale=-1.0).then_inc(s_e, 1)

            def weights_hi(i, slot, reuse=True):
                act.wait_ge(s_a, i + 1)
                if reuse:
                    act.wait_ge(s_o, i - 1)
                act.activation(a_hi[:, slot], z[:, slot], ACT.Copy).then_inc(s_ahi, 1)

            def stats(i, slot):
                core.wait_x(act, i, slot)
                col = bass.ds(i, 1)
                act.wait_ge(s_stat, 4 * i)
                act.activation(junk[:], x_in[:, slot, :], ACT.Identity, scale=core.rstd[:, col], bias=nb[:, col],
                               accum_out=sum2[:, col]).then_inc(s_stat, 1)
                act.wait_ge(s_stat, 4 * i + 1)
                act.mul(nmean2[:, col], sum2[:, col], -1.0 / D).then_inc(s_stat, 1)
                act.wait_ge(s_stat, 4 * i + 2)
                act.activation(nb2[:, col], nmean2[:, col], ACT.Identity, bias=nb[:, col]).then_inc(s_stat, 1)
                act.wait_ge(s_stat, 4 * i + 3)
                act.activation(junk[:], x_in[:, slot, :], ACT.Square, scale=core.rstd[:, col], bias=nb2[:, col],
                               accum_out=core.var[:, col]).then_inc(s_stat, 1)

            def elu_parts(i, slot):
                act.wait_ge(s_m, i + 1)
                act.wait_ge(s_elu, i)
                act.activation(high[:], p_o[0:T, slot, :, 0:H_COLS], ACT.Relu, scale=rsum[:, 1:2]).then_inc(s_hp, 1)
                act.activation(low[:], low[:], ACT.Exp).then_inc(s_em, 1)

            exps(0, 0)
            weights_hi(0, 0, reuse=False)
            exps(1, 1)
            weights_hi(1, 1, reuse=False)
            act.wait_ge(s_nb, 1)
            stats(0, 0)
            with act.Fori(2, NT - 1, 2) as i:
                for p in range(2):
                    exps(i + p, p)
                    weights_hi(i + p, p)
                    elu_parts(i + p - 2, p)
                    stats(i + p - 1, 1 - p)
            stats(NT - 1, 1)
            elu_parts(NT - 2, 0)
            act.wait_ge(s_step, 1)
            act.activation(core.root[:], core.var[:], ACT.Sqrt).then_inc(s_step, 1)
            elu_parts(NT - 1, 1)

        @block.vector
        def _(dve):
            dve.tensor_tensor(nb[:], core.negmean[:], core.rstd[:], ALU.mult).then_inc(s_nb, 1)
            dve.wait_ge(s_alk, 1)

            def scores(i, slot, reuse=True):
                if reuse:
                    dve.wait_ge(s_alo, i - 1)
                dve.tensor_tensor(z[:, slot], al_all[:, bass.ds(i * T, T)].rearrange("p (a s) -> p a s", a=1).to_broadcast([T, NT, T]),
                                  core.ar[:].rearrange("p (d a) -> p d a", a=1).to_broadcast([T, NT, T]), ALU.add).then_inc(s_z, 1)
                dve.wait_ge(s_z, i + 1)
                dve.scalar_tensor_tensor(y[:, slot], z[:, slot], SLOPE, z[:, slot], ALU.mult, ALU.max).then_inc(s_y, 1)

            def weights(i, slot):
                dve.wait_ge(s_e, i + 1)
                dve.scalar_tensor_tensor(z[:, slot], y[:, slot], FLT_MAX, counts[:, :, bass.ds(i * T, T)],
                                         ALU.min, ALU.mult).then_inc(s_a, 1)

            def elu_parts(i, slot):
                dve.wait_ge(s_o, i + 1)
                dve.wait_ge(s_hp, i)
                dve.tensor_scalar(rsum[:, 0:1], p_o[0:T, slot, 2, D - 2 * H_COLS:D - 2 * H_COLS + 1], GNN_EPS, None,
                                  ALU.add).then_inc(s_rs, 1)
                dve.wait_ge(s_rs, 2 * i + 1)
                dve.reciprocal(rsum[:, 1:2], rsum[:, 0:1]).then_inc(s_rs, 1)
                dve.wait_ge(s_rs, 2 * i + 2)
                dve.tensor_scalar(low[:], p_o[0:T, slot, :, 0:H_COLS], rsum[:, 1:2], 0.0, ALU.mult, ALU.min).then_inc(s_m, 1)

            def elu_sum(i):
                dve.wait_ge(s_em, i + 1)
                dve.wait_ge(s_hp, i + 1)
                dve.wait_ge(s_gnn, i)
                dve.scalar_tensor_tensor(elu[:], low[:], -1.0, high[:], ALU.add, ALU.add).then_inc(s_elu, 1)

            scores(0, 0, reuse=False)
            weights(0, 0)
            scores(1, 1, reuse=False)
            weights(1, 1)
            with dve.Fori(2, NT - 1, 2) as i:
                for p in range(2):
                    scores(i + p, p)
                    weights(i + p, p)
                    elu_parts(i + p - 2, p)
                    elu_sum(i + p - 2)
            elu_parts(NT - 2, 0)
            elu_sum(NT - 2)
            dve.wait_ge(s_stat, 4 * NT)
            dve.tensor_scalar(core.var[:], core.var[:], 1.0 / D, LN_EPS, ALU.mult, ALU.add).then_inc(s_step, 1)
            inverse_root(dve, s_step, 2, core.var[:], core.root[:], core.tmp[:], core.rstd2[:])
            dve.tensor_tensor(core.ln_scale[:], core.rstd[:], core.rstd2[:], ALU.mult).then_inc(s_step, 1)
            dve.tensor_tensor(core.ln_shift[:], nb2[:], core.rstd2[:], ALU.mult).then_inc(s_step, 1)
            dve.tensor_copy(core.xn_shift[:], nb[:]).then_inc(s_step, 1)
            dve.wait_ge(s_step, 10)
            elu_parts(NT - 1, 1)
            elu_sum(NT - 1)

        @block.tensor
        def _(pe):
            for i in range(NT):
                last = pe.matmul(p_o[0:T, 1, i // 4, (i % 4) * T:(i % 4 + 1) * T], core.al[:, i:i + 1].to_broadcast([T, T]),
                                 core.ident[0:T, 0:T], start=True, stop=True)
            last.then_inc(s_al, 1)

            def products(i, slot, reuse=True):
                pe.wait_ge(s_alo, i + 1)
                if reuse:
                    pe.wait_ge(s_em, i - 1)
                    pe.wait_ge(s_hp, i - 1)
                for n in range(3):
                    cols = slice(n * H_COLS, (n + 1) * H_COLS)
                    for d in range(NT):
                        for m, (left, right) in enumerate(((a_lo, h_hi), (a_hi, h_lo), (a_hi, h_hi))):
                            last = pe.matmul(p_o[0:T, slot, n, 0:H_COLS], left[:, slot, d, :], right[:, d, cols],
                                             start=(d == 0 and m == 0), stop=(d == NT - 1 and m == 2))
                last.then_inc(s_o, 1)

            products(0, 0, reuse=False)
            pe.wait_ge(s_alk, 1)
            products(1, 1, reuse=False)
            with pe.Fori(2, NT - 1, 2) as i:
                for p in range(2):
                    products(i + p, p)


VALUE, KEY, QUERY = 0, 1, 2
MIX_WEIGHTS = ["L0_mix_wv", "L0_mix_wk", "L0_mix_wq"]
COLUMNS = ["L0_mix_ln1_g", "L0_mix_ln1_b", "L0_mix_bk", "L0_mix_bv", "L0_mix_bq", "L0_mix_ln2_g", "L0_mix_ln2_b",
           "L0_mix_b1"]
COLUMN_AT = {name: slice(n * K8, n * K8 + (FF // 128 if name == "L0_mix_b1" else K8)) for n, name in enumerate(COLUMNS)}
COLUMN_COUNT = COLUMN_AT["L0_mix_b1"].stop


def transpose_second_norm(core):
    nc, inp = core.nc, core.inp
    x, x2_hi, x2_lo = inp["x"], core.x2_hi, core.x2_lo
    with ExitStack() as ctx:
        def sb(name, shape, dt=F32):
            return ctx.enter_context(nc.sbuf_tensor(name, shape, dt))

        x_in = core.x_in
        w_in, w_hi, w_lo = core.mix_in, core.mix_hi, core.mix_lo
        z = sb("z4", [T, 2, D])
        scaled = sb("scaled4", [128, 2, K8, T])
        x2 = sb("x2", [128, 2, K8, T])
        p_t = ctx.enter_context(nc.psum_tensor("p_t", [128, 2, 2, 512], F32))

        p_col = ctx.enter_context(nc.psum_tensor("p_col", [128, 512], F32))

        s_vt = core.sem("vectors_transposed")
        s_gb = core.sem("columns_ready")
        s_z = core.sem("z4_ready")
        s_t = core.sem("z4_transposed")
        s_g = core.sem("scaled4_ready")
        s_x2 = core.sem("x2_ready")
        s_hi = core.sem("x2_hi_ready")
        s_lo = core.sem("x2_lo_ready")

        block = ctx.enter_context(nc.Block())

        @block.sync
        def _(sp):
            for which in range(3):
                core.load_mix(sp, which, 0)
            with sp.Fori(2, NT - 1, 2) as i:
                for p in range(2):
                    sp.wait_ge(s_z, i + p - 1)
                    core.load_x(sp, i + p, p)
            for p in range(2):
                sp.wait_ge(s_z, NT - 1 + p)
                core.load_x(sp, p, p)
            for p in range(2):
                sp.wait_ge(core.gnn_stored[p], 16 * NT // 2)

        @block.scalar
        def _(act):
            def normalise(i, slot, reuse=True):
                core.wait_x(act, i, slot)
                if reuse:
                    act.wait_ge(s_t, i - 1)
                act.activation(z[:, slot], x_in[:, slot], ACT.Identity, scale=core.ln_scale[:, bass.ds(i, 1)],
                               bias=core.ln_shift[:, bass.ds(i, 1)]).then_inc(s_z, 1)

            def keep_hi(i, slot):
                act.wait_ge(s_x2, i + 1)
                act.activation(x2_hi[:, :, bass.ds(i * T, T)], x2[:, slot], ACT.Copy).then_inc(s_hi, 1)

            normalise(0, 0, reuse=False)
            normalise(1, 1, reuse=False)
            for which in range(3):
                act.wait_ge(core.mix_loaded[which], 16)
                act.activation(w_hi[which][:], w_in[which][:], ACT.Copy).then_inc(core.mix_hi_ready[which], 1)
            with act.Fori(2, NT - 1, 2) as i:
                for p in range(2):
                    normalise(i + p, p)
                    keep_hi(i + p - 2, p)
            keep_hi(NT - 2, 0)
            keep_hi(NT - 1, 1)

        @block.tensor
        def _(pe):
            def transposes(i, slot, reuse=True):
                pe.wait_ge(s_z, i + 1)
                if reuse:
                    pe.wait_ge(s_g, i - 1)
                for k in range(K8):
                    last = pe.transpose(p_t[:, slot, k // 4, (k % 4) * T:(k % 4 + 1) * T],
                                        z[:, slot, k * 128:(k + 1) * 128], core.ident[0:T, 0:T])
                last.then_inc(s_t, 1)

            pe.wait_ge(core.vectors_loaded, 16 * len(COLUMNS))
            count = COLUMN_COUNT
            pe.transpose(p_col[:, 0:count], core.vectors[:], core.ident[0:count, 0:count]).then_inc(s_vt, 1)
            transposes(0, 0, reuse=False)
            transposes(1, 1, reuse=False)
            with pe.Fori(2, NT - 1, 2) as i:
                for p in range(2):
                    transposes(i + p, p)

        @block.vector
        def _(dve):
            dve.wait_ge(s_vt, 1)
            dve.tensor_copy(core.cols[:], p_col[:, 0:COLUMN_COUNT]).then_inc(s_gb, 1)
            dve.wait_ge(s_gb, 1)
            g = core.cols[:, COLUMN_AT["L0_mix_ln1_g"]]

            def halves(ap):
                return ap.rearrange("p (a k) t -> p a k t", a=2)

            def scale(i, slot, reuse=True):
                dve.wait_ge(s_t, i + 1)
                if reuse:
                    dve.wait_ge(s_x2, i - 1)
                dve.tensor_tensor(halves(scaled[:, slot]), p_t[:, slot, :, 0:4 * T].rearrange("p a (k t) -> p a k t", k=4),
                                  halves(g.rearrange("p (k t) -> p k t", t=1)).to_broadcast([128, 2, 4, T]),
                                  ALU.mult).then_inc(s_g, 1)

            def keep_lo(i, slot):
                dve.wait_ge(s_hi, i + 1)
                cols = bass.ds(i * T, T)
                dve.tensor_tensor(x2_lo[:, :, cols], x2[:, slot], f32(x2_hi[:, :, cols]), ALU.subtract).then_inc(s_lo, 1)

            scale(0, 0, reuse=False)
            scale(1, 1, reuse=False)
            for which in range(3):
                dve.wait_ge(core.mix_hi_ready[which], 1)
                dve.tensor_tensor(w_lo[which][:], w_in[which][:], f32(w_hi[which][:]), ALU.subtract).then_inc(core.mix_lo_ready[which], 1)
            with dve.Fori(2, NT - 1, 2) as i:
                for p in range(2):
                    scale(i + p, p)
                    keep_lo(i + p - 2, p)
            keep_lo(NT - 2, 0)
            keep_lo(NT - 1, 1)

        @block.gpsimd
        def _(pool):
            pool.wait_ge(s_gb, 1)
            b = core.cols[:, COLUMN_AT["L0_mix_ln1_b"]]

            def shift(i, slot, reuse=True):
                pool.wait_ge(s_g, i + 1)
                if reuse:
                    pool.wait_ge(s_lo, i - 1)
                pool.tensor_tensor(x2[:, slot], scaled[:, slot], b.rearrange("p (k t) -> p k t", t=1).to_broadcast([128, K8, T]),
                                   ALU.add).then_inc(s_x2, 1)

            shift(0, 0, reuse=False)
            shift(1, 1, reuse=False)
            with pool.Fori(2, NT - 1, 2) as i:
                for p in range(2):
                    shift(i + p, p)


STEPS = 5
CHUNK = 2 * T
V_GROUPS = [(0, 3), (3, 3), (6, 4)]


def linear_attention(core):
    nc, inp = core.nc, core.inp
    x2_hi, x2_lo = core.x2_hi, core.x2_lo
    with ExitStack() as ctx:
        def sb(name, shape, dt=F32):
            return ctx.enter_context(nc.sbuf_tensor(name, shape, dt))

        def ps(name, shape):
            return ctx.enter_context(nc.psum_tensor(name, shape, F32))

        w_in, w_hi, w_lo = core.mix_in, core.mix_hi, core.mix_lo
        bias = [core.cols[:, COLUMN_AT[f"L0_mix_b{n}"]] for n in "vkq"]
        proj = sb("proj", [128, 2, KMAP])
        proj_hi = sb("proj_hi", [128, 2, KMAP], F32R)
        proj_lo = sb("proj_lo", [128, 2, KMAP], F32R)
        half_pi = sb("half_pi", [128, 1])
        k_hi = sb("k_hi", [128, N], F32R)
        k_lo = sb("k_lo", [128, N], F32R)
        q_hi = sb("q_hi", [128, N], F32R)
        q_lo = sb("q_lo", [128, N], F32R)
        v_t = sb("v_t", [128, N])
        v_hi = sb("v_hi", [T, NT, 128], F32R)
        v_lo = sb("v_lo", [T, NT, 128], F32R)
        whole = sb("whole_turns", [128, 2, 512])
        part = sb("part_turn", [128, 2, 512])
        away = whole
        cs = sb("cos_sin", [128, 2, 1024])
        cs_hi = sb("cos_sin_hi", [128, 2, 1024], F32R)
        cs_lo = sb("cos_sin_lo", [128, 2, 1024], F32R)
        kv_t = sb("kv_t", [128, 4, 128])
        kv_hi = sb("kv_hi", [128, 4, 128], F32R)
        kv_lo = sb("kv_lo", [128, 4, 128], F32R)
        attn_t = sb("attn_t", [128, N])
        p_w = ps("p_w", [128, 3, 512])
        p_p = ps("p_p", [128, 2, 512])
        p_kv = ps("p_kv", [128, 512])
        p_at = ps("p_at", [128, 512])
        p_tr = ps("p_tr5", [128, 4, 128])

        s_w, s_whi, s_wlo = core.mix_loaded, core.mix_hi_ready, core.mix_lo_ready
        s_zero = core.sem("zeros_written5")
        s_proj = core.sem("projection_loaded")
        s_prep = core.sem("projection_step")
        s_prod = core.sem("third_product_done")
        s_kqhi = core.sem("key_or_query_hi_kept")
        s_klo = core.sem("keys_kept")
        s_qlo = core.sem("queries_kept")
        s_vt = core.sem("values_kept")
        s_tr = core.sem("transposes_done5")
        s_trhi = core.sem("transposed_hi_kept")
        s_trlo = core.sem("transposed_kept")
        s_p = core.sem("phases_in_psum")
        s_whole = core.sem("whole_turns_ready")
        s_part = core.sem("part_turns_ready")
        s_away = core.sem("part_turns_abs_ready")
        s_cs = core.sem("cos_sin_ready")
        s_cshi = core.sem("cos_sin_hi_ready")
        s_cslo = [core.sem(f"cos_sin_lo_ready{i}") for i in range(2)]
        s_added = core.sem("step_added_to_kv")
        s_kvt = core.sem("kv_copied")
        s_at = core.sem("attention_in_psum")
        s_atk = core.sem("attention_kept")
        s_st = core.attention_stored
        wo_in, wo_hi, wo_lo = w_in, x2_hi[:, :, 0:D], x2_lo[:, :, 0:D]
        s_wo = [core.sem(f"wo_loaded{i}") for i in range(3)]
        s_wohi = core.sem("wo_hi_ready")
        s_wolo = core.sem("wo_lo_ready")

        block = ctx.enter_context(nc.Block())

        def done(j, k):
            return 2 * STEPS * j + k + 1

        def slot_free(engine, sem, j, k):
            if isinstance(j, int) and j == 0 and k < 2:
                return
            engine.wait_ge(sem, 2 * STEPS * j + k - 1)

        def lo_done(j, k):
            return STEPS * j + k // 2 + 1

        def keys_view(buf, slot):
            return buf[0:T, slot].rearrange("p (i h c m) -> p i h c m", i=2, h=2, c=2)

        def step_view(buf, k, c):
            if k < STEPS:
                return buf[0:T, k % 2].rearrange("p (i c m) -> p i c m", i=4, c=2)[:, :, c, :]
            return buf[:, k % 2, 0:4 * CHUNK].rearrange("p (h c t) -> p h c t", h=2, c=2)[:, :, c, :]

        def flat(buf, k):
            return buf[0:T, k % 2, 0:512] if k < STEPS else buf[:, k % 2, 0:2 * CHUNK]

        def rows(buf, k):
            if k < STEPS:
                return flat(buf, k).rearrange("p (i m) -> p i m", i=4)
            return flat(buf, k).rearrange("p (h t) -> p h t", h=2)

        def full(buf, k):
            return buf[0:T, k % 2, :] if k < STEPS else buf[:, k % 2, 0:4 * CHUNK]

        @block.sync
        def _(sp):
            sp.wait_ge(s_zero, 1)
            for h in range(2):
                sp.dma_start(proj[h * DH:(h + 1) * DH, h, :], inp["L0_mix_proj_mat"]).then_inc(s_proj, 16)

            def store(j):
                sp.wait_ge(s_atk, STEPS * j + STEPS)
                sp.dma_start(core.attn_dram[bass.ds(j * 128, 128), :], attn_t[:]).then_inc(s_st, 16)

            with sp.Fori(0, PAIRS - 1) as j:
                for which in (KEY, VALUE, QUERY):
                    sp.wait_ge(s_wlo[which], j + 1)
                    core.load_mix(sp, which, j + 1)
                store(j)
            for k in range(K8):
                if k < 3:
                    sp.wait_ge(s_wlo[k], PAIRS)
                else:
                    sp.wait_ge(s_wolo, k - 2)
                sp.dma_start(wo_in[k % 3][:].rearrange("p k n -> p (k n)"), inp["L0_mix_wo"][k * 128:(k + 1) * 128, :]
                             ).then_inc(s_wo[k % 3], 16)
            store(PAIRS - 1)

        @block.gpsimd
        def _(pool):
            pool.memset(proj[:], 0.0).then_inc(s_zero, 1)
            pool.memset(half_pi[:], HALF_PI).then_inc(s_zero, 1)
            pool.memset(f32(kv_hi[:]), 0.0).then_inc(s_zero, 1)
            pool.memset(f32(kv_lo[:]), 0.0).then_inc(s_zero, 1)

            def split_lo(which, j):
                pool.wait_ge(s_whi[which], j + 1)
                pool.tensor_tensor(w_lo[which][:], w_in[which][:], f32(w_hi[which][:]), ALU.subtract).then_inc(s_wlo[which], 1)

            def keep_lo(j, k):
                pool.wait_ge(s_cshi, done(j, k))
                pool.tensor_tensor(full(cs_lo, k), full(cs, k), f32(full(cs_hi, k)), ALU.subtract).then_inc(s_cslo[0], 1)

            pool.wait_ge(s_proj, 32)
            pool.tensor_scalar(proj[:], proj[:], 1.0 / (DH ** 0.5 * 2 * 3.141592653589793), None, ALU.mult).then_inc(s_prep, 1)
            pool.wait_ge(s_prep, 1)
            pool.tensor_copy(proj_hi[:], proj[:]).then_inc(s_prep, 1)
            pool.wait_ge(s_prep, 2)
            pool.tensor_tensor(proj_lo[:], proj[:], f32(proj_hi[:]), ALU.subtract).then_inc(s_prep, 1)

            def pair(j, more):
                keep_lo(j, 0)
                if more:
                    split_lo(KEY, j + 1)
                keep_lo(j, 2)
                if more:
                    split_lo(VALUE, j + 1)
                keep_lo(j, 4)
                if more:
                    split_lo(QUERY, j + 1)
                keep_lo(j, 6)
                keep_lo(j, 8)

            with pool.Fori(0, PAIRS - 1) as j:
                pair(j, True)
            pair(PAIRS - 1, False)

        @block.scalar
        def _(act):
            def split_hi(which, j):
                act.wait_ge(s_w[which], 16 * j + 16)
                act.activation(w_hi[which][:], w_in[which][:], ACT.Copy).then_inc(s_whi[which], 1)

            def keep_run(which, j, n):
                a, w = THIRDS[n]
                act.wait_ge(s_prod, 9 * j + 3 * which + n + 1)
                core.passed(act)
                out = (v_t, k_hi, q_hi)[which]
                act.activation(out[:, a:a + w], p_w[:, n, 0:w], ACT.Identity, bias=bias[which][:, bass.ds(j, 1)]
                               ).then_inc(s_vt if which == VALUE else s_kqhi, 1)

            def keep_v(j, group):
                first, count = V_GROUPS[group]
                act.wait_ge(s_tr, 4 * j + group + 1)
                act.activation(v_hi[:, first:first + count, :], p_tr[0:T, 0:count, :], ACT.Copy).then_inc(s_trhi, 1)

            def keep_kv(j):
                act.wait_ge(s_tr, 4 * j + 4)
                for h in range(2):
                    last = act.activation(kv_hi[:, 2 * h:2 * h + 2, h * DH:(h + 1) * DH],
                                          p_tr[:, 2 * h:2 * h + 2, h * DH:(h + 1) * DH], ACT.Copy, scale=1.0 / KMAP)
                last.then_inc(s_trhi, 1)

            def cos_sin(j, k):
                act.wait_ge(s_part, done(j, k))
                if not (isinstance(j, int) and j == 0 and k < 2):
                    act.wait_ge(s_cslo[k % 2], lo_done(j, k) - 1)
                act.activation(step_view(cs, k, 1), rows(part, k), ACT.Sin, scale=TWO_PI)
                act.wait_ge(s_away, done(j, k))
                act.activation(step_view(cs, k, 0), rows(away, k), ACT.Sin, scale=TWO_PI,
                               bias=half_pi[0:T if k < STEPS else 128, :]).then_inc(s_cs, 1)
                act.wait_ge(s_cs, done(j, k))
                if k < 2:
                    if not (isinstance(j, int) and j == 0):
                        act.wait_ge(s_at, STEPS * j + k - 1)
                elif k < STEPS + 2:
                    act.wait_ge(s_added, STEPS * j + k - 1)
                else:
                    act.wait_ge(s_at, STEPS * j + k - 1 - STEPS)
                act.activation(full(cs_hi, k), full(cs, k), ACT.Copy).then_inc(s_cshi, 1)

            def wo_high(k):
                if k == 0:
                    act.wait_ge(s_prod, 9 * PAIRS)
                act.wait_ge(s_wo[k % 3], 16 * (k // 3 + 1))
                act.activation(wo_hi[:, k, :], wo_in[k % 3][:].rearrange("p k n -> p (k n)"), ACT.Copy).then_inc(s_wohi, 1)

            def keep_attention(j, c):
                act.wait_ge(s_at, STEPS * j + c + 1)
                act.activation(attn_t[:, c * CHUNK:(c + 1) * CHUNK], p_at[:, 0:CHUNK], ACT.Copy).then_inc(s_atk, 1)

            for n in range(3):
                keep_run(VALUE, 0, n)
            for n in range(3):
                keep_run(KEY, 0, n)
            act.wait_ge(s_zero, 4)
            for group in range(3):
                keep_v(0, group)
            cos_sin(0, 0)
            cos_sin(0, 1)

            def pair(j, more):
                keep_run(QUERY, j, 0)
                if more:
                    split_hi(KEY, j + 1)
                cos_sin(j, 2)
                keep_run(QUERY, j, 1)
                if more:
                    split_hi(VALUE, j + 1)
                cos_sin(j, 3)
                keep_run(QUERY, j, 2)
                cos_sin(j, 4)
                if more:
                    keep_run(VALUE, j + 1, 0)
                    split_hi(QUERY, j + 1)
                cos_sin(j, 5)
                if more:
                    keep_run(VALUE, j + 1, 1)
                cos_sin(j, 6)
                if not more:
                    wo_high(0)
                keep_kv(j)
                if more:
                    keep_run(VALUE, j + 1, 2)
                act.wait_ge(s_st, 16 * j)
                keep_attention(j, 0)
                cos_sin(j, 7)
                if more:
                    keep_run(KEY, j + 1, 0)
                    keep_v(j + 1, 0)
                else:
                    wo_high(1)
                    wo_high(2)
                keep_attention(j, 1)
                cos_sin(j, 8)
                if more:
                    keep_run(KEY, j + 1, 1)
                    keep_v(j + 1, 1)
                else:
                    wo_high(3)
                    wo_high(4)
                keep_attention(j, 2)
                cos_sin(j, 9)
                if more:
                    keep_v(j + 1, 2)
                else:
                    wo_high(5)
                keep_attention(j, 3)
                if more:
                    cos_sin(j + 1, 0)
                    keep_run(KEY, j + 1, 2)
                else:
                    wo_high(6)
                keep_attention(j, 4)
                if more:
                    cos_sin(j + 1, 1)
                else:
                    wo_high(7)

            with act.Fori(0, PAIRS - 1) as j:
                pair(j, True)
            pair(PAIRS - 1, False)

        @block.vector
        def _(dve):
            def keep_run(which, j, n):
                a, w = THIRDS[n]
                dve.wait_ge(s_kqhi, 6 * j + (3 if which == QUERY else 0) + n + 1)
                hi, lo, s = (k_hi, k_lo, s_klo) if which == KEY else (q_hi, q_lo, s_qlo)
                dve.scalar_tensor_tensor(lo[:, a:a + w], p_w[:, n, 0:w], bias[which][:, bass.ds(j, 1)], f32(hi[:, a:a + w]),
                                         ALU.add, ALU.subtract).then_inc(s, 1)

            def keep_v(j, group):
                first, count = V_GROUPS[group]
                dve.wait_ge(s_trhi, 4 * j + group + 1)
                dve.tensor_tensor(v_lo[:, first:first + count, :], p_tr[0:T, 0:count, :],
                                  f32(v_hi[:, first:first + count, :]), ALU.subtract).then_inc(s_trlo, 1)

            def keep_kv(j):
                dve.wait_ge(s_trhi, 4 * j + 4)
                for h in range(2):
                    block_h = (slice(None), slice(2 * h, 2 * h + 2), slice(h * DH, (h + 1) * DH))
                    last = dve.scalar_tensor_tensor(kv_lo[block_h], p_tr[block_h], 1.0 / KMAP, f32(kv_hi[block_h]),
                                                    ALU.mult, ALU.subtract)
                last.then_inc(s_trlo, 1)

            def phases(j, k):
                dve.wait_ge(s_p, done(j, k))
                slot_free(dve, s_cs, j, k)
                dve.tensor_scalar(flat(whole, k), flat(p_p, k), MAGIC, -MAGIC, ALU.add, ALU.add).then_inc(s_whole, 1)
                dve.wait_ge(s_whole, done(j, k))
                dve.tensor_tensor(flat(part, k), flat(p_p, k), flat(whole, k), ALU.subtract).then_inc(s_part, 1)
                dve.wait_ge(s_part, done(j, k))
                dve.scalar_tensor_tensor(flat(away, k), flat(part, k), -1.0, flat(part, k), ALU.mult, ALU.min).then_inc(s_away, 1)

            def keep_lo(j, k):
                dve.wait_ge(s_cshi, done(j, k))
                dve.tensor_tensor(full(cs_lo, k), full(cs, k), f32(full(cs_hi, k)), ALU.subtract).then_inc(s_cslo[1], 1)

            def wo_low(k):
                dve.wait_ge(s_wohi, k + 1)
                dve.tensor_tensor(wo_lo[:, k, :], wo_in[k % 3][:].rearrange("p k n -> p (k n)"), f32(wo_hi[:, k, :]),
                                  ALU.subtract).then_inc(s_wolo, 1)

            def copy_kv(j):
                dve.wait_ge(s_added, STEPS * (j + 1))
                dve.tensor_copy(kv_t[:], p_kv[:].rearrange("p (b m) -> p b m", b=4)).then_inc(s_kvt, 1)

            for n in range(3):
                keep_run(KEY, 0, n)
            dve.wait_ge(s_zero, 4)
            for group in range(3):
                keep_v(0, group)
            phases(0, 0)
            phases(0, 1)

            def pair(j, more):
                keep_run(QUERY, j, 0)
                keep_lo(j, 1)
                phases(j, 2)
                keep_run(QUERY, j, 1)
                phases(j, 3)
                keep_run(QUERY, j, 2)
                keep_lo(j, 3)
                phases(j, 4)
                phases(j, 5)
                phases(j, 6)
                copy_kv(j)
                keep_lo(j, 5)
                keep_kv(j)
                phases(j, 7)
                if more:
                    keep_run(KEY, j + 1, 0)
                    keep_v(j + 1, 0)
                else:
                    wo_low(0)
                keep_lo(j, 7)
                phases(j, 8)
                if more:
                    keep_run(KEY, j + 1, 1)
                    keep_v(j + 1, 1)
                else:
                    wo_low(1)
                    wo_low(2)
                phases(j, 9)
                if more:
                    keep_v(j + 1, 2)
                else:
                    wo_low(3)
                    wo_low(4)
                keep_lo(j, 9)
                if more:
                    phases(j + 1, 0)
                    keep_run(KEY, j + 1, 2)
                    phases(j + 1, 1)
                else:
                    for k in range(5, K8):
                        wo_low(k)

            with dve.Fori(0, PAIRS - 1) as j:
                pair(j, True)
            pair(PAIRS - 1, False)

        @block.tensor
        def _(pe):
            def product(which, j, n, first=0, past=K8):
                a, w = THIRDS[n]
                if first == 0:
                    pe.wait_ge(s_wlo[which], j + 1)
                for k in range(first, past):
                    for m, (left, right) in enumerate(((w_lo, x2_hi), (w_hi, x2_lo), (w_hi, x2_hi))):
                        last = pe.matmul(p_w[:, n, 0:w], left[which][:, k, :], right[:, k, a:a + w],
                                         start=(k == 0 and m == 0), stop=(k == K8 - 1 and m == 2))
                if past == K8:
                    last.then_inc(s_prod, 1)

            def value_run(j, n, first=0, past=K8):
                if first == 0:
                    pe.wait_ge(s_qlo, 3 * j - 2 + n)
                product(VALUE, j, n, first, past)

            def key_run(j, n, first=0, past=K8):
                if first == 0:
                    pe.wait_ge(s_vt, 3 * j + n + 1)
                product(KEY, j, n, first, past)

            def query_run(j, n):
                pe.wait_ge(s_klo, 3 * j + n + 1)
                product(QUERY, j, n)

            def transpose_v(j, group):
                first, count = V_GROUPS[group]
                pe.wait_ge(s_vt, 3 * j + group + 1)
                pe.wait_ge(s_trlo, 4 * j + group)
                for i in range(count):
                    tile = slice((first + i) * T, (first + i + 1) * T)
                    last = pe.transpose(p_tr[0:T, i, :], v_t[:, tile], core.ident[:])
                last.then_inc(s_tr, 1)

            def transpose_kv(j):
                pe.wait_ge(s_kvt, j + 1)
                pe.wait_ge(s_trlo, 4 * j + 3)
                for b in range(4):
                    last = pe.transpose(p_tr[:, b, :], kv_t[:, b, :], core.ident[:])
                last.then_inc(s_tr, 1)

            def key_phases(j, k):
                pe.wait_ge(s_klo, 3 * j + (2 * T * (k + 1) - 1) // 417 + 1)
                slot_free(pe, s_part, j, k)
                for i in range(2):
                    tile = slice((2 * k + i) * T, (2 * k + i + 1) * T)
                    for m, (left, right) in enumerate(((k_lo, proj_hi), (k_hi, proj_lo), (k_hi, proj_hi))):
                        last = pe.matmul(p_p[0:T, k % 2, i * 256:(i + 1) * 256], left[:, tile], right[:].rearrange("p h m -> p (h m)"),
                                         start=(m == 0), stop=(m == 2))
                last.then_inc(s_p, 1)

            def query_phases(j, k):
                c = k - STEPS
                pe.wait_ge(s_qlo, 3 * j + (CHUNK * (c + 1) - 1) // 417 + 1)
                slot_free(pe, s_part, j, k)
                for h in range(2):
                    for m, (left, right) in enumerate(((proj_lo, q_hi), (proj_hi, q_lo), (proj_hi, q_hi))):
                        last = pe.matmul(p_p[:, k % 2, h * CHUNK:(h + 1) * CHUNK], left[:, h, :], right[:, c * CHUNK:(c + 1) * CHUNK],
                                         start=(m == 0), stop=(m == 2))
                last.then_inc(s_p, 1)

            def accumulate_kv(j, k):
                if k == 0:
                    pe.wait_ge(s_kvt, j)
                pe.wait_ge(s_trlo, 4 * j + (1, 2, 2, 3, 3)[k])
                pe.wait_ge(s_cslo[k % 2], lo_done(j, k))
                hi, lo = keys_view(cs_hi, k % 2), keys_view(cs_lo, k % 2)
                for i in range(2):
                    for m, (left, right) in enumerate(((v_lo, hi), (v_hi, lo), (v_hi, hi))):
                        last = pe.matmul(p_kv[:], left[:, 2 * k + i, :], right[:, i].rearrange("p h c m -> p (h c m)"),
                                         start=(k == 0 and i == 0 and m == 0), stop=(k == STEPS - 1 and i == 1 and m == 2))
                last.then_inc(s_added, 1)

            def attend(j, k):
                c = k - STEPS
                pe.wait_ge(s_trlo, 4 * j + 4)
                pe.wait_ge(s_cslo[k % 2], lo_done(j, k))
                pe.wait_ge(s_atk, STEPS * j + c)
                for b in range(4):
                    cols = slice(b * CHUNK, (b + 1) * CHUNK)
                    for m, (left, right) in enumerate(((kv_lo, cs_hi), (kv_hi, cs_lo), (kv_hi, cs_hi))):
                        last = pe.matmul(p_at[:, 0:CHUNK], left[:, b, :], right[:, k % 2, cols],
                                         start=(b == 0 and m == 0), stop=(b == 3 and m == 2))
                last.then_inc(s_at, 1)

            for n in range(3):
                product(VALUE, 0, n)
            for n in range(3):
                key_run(0, n)
            for group in range(3):
                transpose_v(0, group)
            pe.wait_ge(s_prep, 3)
            key_phases(0, 0)
            key_phases(0, 1)

            def pair(j, more):
                half = K8 // 2
                for k in range(3):
                    query_run(j, k)
                    accumulate_kv(j, k)
                    if k + 2 < STEPS:
                        key_phases(j, k + 2)
                for k in range(3, STEPS):
                    if more:
                        value_run(j + 1, k - 3)
                    accumulate_kv(j, k)
                    query_phases(j, k + 2)
                if more:
                    value_run(j + 1, 2, 0, half)
                transpose_kv(j)
                if more:
                    value_run(j + 1, 2, half, K8)
                attend(j, 5)
                query_phases(j, 7)
                if more:
                    key_run(j + 1, 0)
                    transpose_v(j + 1, 0)
                attend(j, 6)
                query_phases(j, 8)
                if more:
                    key_run(j + 1, 1)
                    transpose_v(j + 1, 1)
                attend(j, 7)
                query_phases(j, 9)
                if more:
                    key_run(j + 1, 2, 0, half)
                    transpose_v(j + 1, 2)
                attend(j, 8)
                if more:
                    key_phases(j + 1, 0)
                    key_run(j + 1, 2, half, K8)
                attend(j, 9)
                if more:
                    key_phases(j + 1, 1)

            with pe.Fori(0, PAIRS - 1) as j:
                pair(j, True)
            pair(PAIRS - 1, False)


def column_stats(act, s_stat, count, junk, rows_in, sums, neg_mean, squares, scale=None, shift=None, both=None):
    act.wait_ge(s_stat, count)
    if scale is None:
        act.activation(junk, rows_in, ACT.Identity, accum_out=sums).then_inc(s_stat, 1)
    else:
        act.activation(junk, rows_in, ACT.Identity, scale=scale, bias=shift, accum_out=sums).then_inc(s_stat, 1)
    act.wait_ge(s_stat, count + 1)
    act.mul(neg_mean, sums, -1.0 / D).then_inc(s_stat, 1)
    act.wait_ge(s_stat, count + 2)
    act.activation(junk, rows_in, ACT.Square, bias=neg_mean, accum_out=squares).then_inc(s_stat, 1)


def project_attention(core):
    nc, inp, x1 = core.nc, core.inp, core.rows
    W1_PARTS = K8 // 2
    with ExitStack() as ctx:
        def sb(name, shape, dt=F32):
            return ctx.enter_context(nc.sbuf_tensor(name, shape, dt))

        w_in = sb("w1_in", [128, 2, D])
        w_hi, w_lo = core.x2_hi[:, :, 0:D], core.x2_lo[:, :, 0:D]
        at_in = sb("at_in", [128, 2, K8, T])
        at_hi = sb("at_hi", [128, 2, K8, T], F32R)
        at_lo = sb("at_lo", [128, 2, K8, T], F32R)
        bo = sb("bo", [T, D])
        x_in = xn = core.x_in
        junk = sb("junk6", [T, D])
        sums = sb("sums6", [T, NT])
        p_o = ctx.enter_context(nc.psum_tensor("p_o6", [128, 2, 2, 512], F32))

        s_w = [core.sem(f"w1_loaded{i}") for i in range(2)]
        s_whi = core.sem("w1_hi_ready")
        s_wlo = core.sem("w1_lo_ready")
        s_bo = core.sem("bo_loaded")
        s_in = [core.sem(f"attention_loaded{i}") for i in range(2)]
        s_ahi = core.sem("at_hi_ready")
        s_alo = core.sem("at_lo_ready")
        s_xn = core.sem("xn6_ready")
        s_xb = core.sem("xn_plus_bo_ready")
        s_o = core.sem("wo_product_done")
        s_x1 = core.sem("x1_ready")
        s_stat = core.sem("x1_stat_step")
        s_step = core.sem("rstd6_step")

        block = ctx.enter_context(nc.Block())

        @block.sync
        def _(sp):
            def load(i, slot):
                sp.dma_start(at_in[:, slot], core.attn_dram[:, bass.ds(i * T, T)].rearrange("(k p) t -> p k t", p=128)
                             ).then_inc(s_in[slot], 16)

            sp.wait_ge(core.attention_stored, 16 * PAIRS)
            load(0, 0)
            sp.dma_start(bo[:], spread(inp["L0_mix_bo"], T)).then_inc(s_bo, 16)
            load(1, 1)
            for n in range(W1_PARTS):
                if n >= 2:
                    sp.wait_ge(s_wlo, n - 1)
                sp.dma_start(w_in[:, n % 2, :].rearrange("p (a f) -> p a f", a=2),
                             inp["L0_mix_w1"][n * 256:(n + 1) * 256, :].rearrange("(a p) f -> p a f", p=128)
                             ).then_inc(s_w[n % 2], 16)
            with sp.Fori(2, NT - 1, 2) as i:
                for p in range(2):
                    sp.wait_ge(s_alo, i + p - 1)
                    sp.wait_ge(s_x1, i + p - 1)
                    load(i + p, p)
                    core.load_x(sp, i + p, p)

        @block.scalar
        def _(act):
            def attention_hi(i, slot, reuse=True):
                act.wait_ge(s_in[slot], 16 + 8 * (i - slot))
                if reuse:
                    act.wait_ge(s_o, i - 1)
                act.activation(at_hi[:, slot], at_in[:, slot], ACT.Copy).then_inc(s_ahi, 1)

            def residual(i, slot):
                core.wait_x(act, i, slot)
                act.activation(xn[:, slot], x_in[:, slot], ACT.Identity, scale=core.rstd[:, bass.ds(i, 1)],
                               bias=core.xn_shift[:, bass.ds(i, 1)]).then_inc(s_xn, 1)

            def stats(i):
                col = bass.ds(i, 1)
                act.wait_ge(s_x1, i + 1)
                column_stats(act, s_stat, 3 * i, junk[:], x1[:, col, :].rearrange("p a n -> p (a n)"), sums[:, col],
                             core.negmean[:, col], core.var[:, col])

            attention_hi(0, 0, reuse=False)
            residual(0, 0)
            attention_hi(1, 1, reuse=False)
            residual(1, 1)
            for n in range(W1_PARTS):
                act.wait_ge(s_w[n % 2], 16 * (n // 2 + 1))
                act.activation(core.w1_hi[:, 2 * n:2 * n + 2, :], w_in[:, n % 2, :].rearrange("p (a f) -> p a f", a=2),
                               ACT.Copy).then_inc(s_whi, 1)
            stats(0)
            with act.Fori(2, NT - 1, 2) as i:
                for p in range(2):
                    attention_hi(i + p, p)
                    residual(i + p, p)
                    stats(i + p - 1)
            stats(NT - 1)
            act.wait_ge(s_step, 1)
            act.activation(core.root[:], core.var[:], ACT.Sqrt).then_inc(s_step, 1)

        @block.gpsimd
        def _(pool):
            def add_bias(i, slot):
                pool.wait_ge(s_xn, i + 1)
                pool.tensor_tensor(xn[:, slot], xn[:, slot], bo[:], ALU.add).then_inc(s_xb, 1)

            pool.wait_ge(s_bo, 16)
            add_bias(0, 0)
            add_bias(1, 1)
            with pool.Fori(2, NT - 1, 2) as i:
                for p in range(2):
                    add_bias(i + p, p)

        @block.vector
        def _(dve):
            def attention_lo(i, slot):
                dve.wait_ge(s_ahi, i + 1)
                dve.tensor_tensor(at_lo[:, slot], at_in[:, slot], f32(at_hi[:, slot]), ALU.subtract).then_inc(s_alo, 1)

            def add(i, slot):
                dve.wait_ge(s_o, i + 1)
                dve.wait_ge(s_xb, i + 1)
                dve.tensor_tensor(x1[:, bass.ds(i, 1), :].rearrange("p a (b n) -> p (a b) n", b=2), p_o[0:T, slot],
                                  xn[:, slot].rearrange("p (b n) -> p b n", b=2), ALU.add).then_inc(s_x1, 1)

            attention_lo(0, 0)
            attention_lo(1, 1)
            add(0, 0)
            for n in range(W1_PARTS):
                part = slice(2 * n, 2 * n + 2)
                dve.wait_ge(s_whi, n + 1)
                dve.tensor_tensor(core.w1_lo[:, part, :], w_in[:, n % 2, :].rearrange("p (a f) -> p a f", a=2),
                                  f32(core.w1_hi[:, part, :]), ALU.subtract).then_inc(s_wlo, 1)
            with dve.Fori(2, NT - 1, 2) as i:
                for p in range(2):
                    attention_lo(i + p, p)
                    add(i + p - 1, 1 - p)
            add(NT - 1, 1)
            dve.wait_ge(s_stat, 3 * NT)
            dve.tensor_scalar(core.var[:], core.var[:], 1.0 / D, LN_EPS, ALU.mult, ALU.add).then_inc(s_step, 1)
            inverse_root(dve, s_step, 2, core.var[:], core.root[:], core.tmp[:], core.rstd[:])
            dve.tensor_tensor(core.ln_shift[:], core.negmean[:], core.rstd[:], ALU.mult).then_inc(s_step, 1)
            dve.wait_ge(s_step, 8)

        @block.tensor
        def _(pe):
            def products(i, slot, reuse=True):
                pe.wait_ge(s_alo, i + 1)
                if reuse:
                    pe.wait_ge(s_x1, i - 1)
                for k in range(K8):
                    for m, (left, right) in enumerate(((at_lo, w_hi), (at_hi, w_lo), (at_hi, w_hi))):
                        for n in range(2):
                            last = pe.matmul(p_o[0:T, slot, n, :], left[:, slot, k, :], right[:, k, n * 512:(n + 1) * 512],
                                             start=(k == 0 and m == 0), stop=(k == K8 - 1 and m == 2))
                last.then_inc(s_o, 1)

            products(0, 0, reuse=False)
            products(1, 1, reuse=False)
            with pe.Fori(2, NT - 1, 2) as i:
                for p in range(2):
                    products(i + p, p)


def feed_forward(core):
    nc, inp, rows = core.nc, core.inp, core.rows
    F4 = FF // 128
    g2, b2c = core.cols[:, COLUMN_AT["L0_mix_ln2_g"]], core.cols[:, COLUMN_AT["L0_mix_ln2_b"]]
    b1c = core.cols[:, COLUMN_AT["L0_mix_b1"]]
    with ExitStack() as ctx:
        def sb(name, shape, dt=F32):
            return ctx.enter_context(nc.sbuf_tensor(name, shape, dt))

        w_in = sb("w12_in", [128, 2, D])
        w1_hi, w1_lo = core.w1_hi, core.w1_lo
        w2_hi = sb("w2_hi", [128, F4, D], F32R)
        w2_lo = sb("w2_lo", [128, F4, D], F32R)
        b2 = sb("b2", [T, D])
        z = sb("z7", [T, 2, D])
        scaled = sb("scaled7", [128, K8, T])
        x2 = sb("x2_7", [128, 2, K8, T])
        x2_hi = sb("x2_hi7", [128, K8, CHUNK], F32R)
        x2_lo = sb("x2_lo7", [128, K8, CHUNK], F32R)
        hid = sb("hidden", [128, F4, CHUNK])
        hid_hi = sb("hidden_hi", [128, F4, CHUNK], F32R)
        hid_lo = sb("hidden_lo", [128, F4, CHUNK], F32R)
        gnn_in = core.x_in
        junk = sb("junk7", [T, D])
        sums = sb("sums7", [T, NT])
        p_t = ctx.enter_context(nc.psum_tensor("p_t7", [128, 2, 512], F32))
        p_1 = ctx.enter_context(nc.psum_tensor("p_hidden", [128, 2, 512], F32))
        p_2 = ctx.enter_context(nc.psum_tensor("p_w2", [128, 2, 2, 512], F32))

        s_w = [core.sem(f"w12_loaded{i}") for i in range(2)]
        s_whi = core.sem("w12_hi_ready")
        s_wlo = core.sem("w12_lo_ready")
        s_b2 = core.sem("b2_loaded")
        s_g = [core.sem(f"gnn_loaded{i}") for i in range(2)]
        s_q = core.sem("ternary_weights_loaded")
        s_z = core.sem("z7_ready")
        s_t = core.sem("z7_transposed")
        s_sc = core.sem("scaled7_ready")
        s_x2 = core.sem("x2_7_ready")
        s_xhi = core.sem("x2_hi7_ready")
        s_xlo = core.sem("x2_lo7_ready")
        s_1 = core.sem("hidden_product_done")
        s_h = core.sem("hidden_ready")
        s_hhi = core.sem("hidden_hi_ready")
        s_hlo = core.sem("hidden_lo_ready")
        s_gb = core.sem("gnn_plus_b2_ready")
        s_xg = core.sem("residuals_ready")
        s_2 = core.sem("w2_product_done")
        s_y = core.sem("y_ready")
        s_stat = core.sem("y_stat_step")
        s_step = core.sem("rstd7_step")

        block = ctx.enter_context(nc.Block())
        CH = NT // 2

        @block.sync
        def _(sp):
            def load(i, slot):
                sp.dma_start(gnn_in[:, slot], core.gnn_dram[bass.ds(i * T, T), :]).then_inc(s_g[slot], 16)

            for n in range(F4):
                if n >= 2:
                    sp.wait_ge(s_wlo, n - 1)
                sp.dma_start(w_in[:, n % 2, :], inp["L0_mix_w2"][n * 128:(n + 1) * 128, :]).then_inc(s_w[n % 2], 16)
            sp.dma_start(b2[:], spread(inp["L0_mix_b2"], T)).then_inc(s_b2, 16)
            load(0, 0)
            load(1, 1)
            for n in range(3):
                sp.dma_start(core.ternary[:, n, :], core.ternary_dram[n]).then_inc(s_q, 16)
            with sp.Fori(2, NT - 1, 2) as i:
                for p in range(2):
                    sp.wait_ge(s_xg, i + p - 1)
                    load(i + p, p)
            sp.wait_ge(s_q, 48)

        @block.scalar
        def _(act):
            def split(n):
                act.wait_ge(s_w[n % 2], 16 * (n // 2 + 1))
                act.activation(w2_hi[:, n, :], w_in[:, n % 2, :], ACT.Copy).then_inc(s_whi, 1)

            def normalise(i, slot, reuse=True):
                if reuse:
                    act.wait_ge(s_t, i - 1)
                col = bass.ds(i, 1)
                act.activation(z[:, slot], rows[:, col, :].rearrange("p a n -> p (a n)"), ACT.Identity,
                               scale=core.rstd[:, col], bias=core.ln_shift[:, col]).then_inc(s_z, 1)

            def x2_half(c, half):
                act.wait_ge(s_x2, 2 * c + half + 1)
                act.wait_ge(s_1, F4 * c)
                act.activation(x2_hi[:, :, half * T:(half + 1) * T], x2[:, half], ACT.Copy).then_inc(s_xhi, 1)

            def hidden(c, f):
                act.wait_ge(s_1, F4 * c + f + 1)
                act.wait_ge(s_hlo, 2 * c)
                act.activation(hid[:, f, :], p_1[:, f % 2, 0:CHUNK], ACT.Relu, bias=b1c[:, f:f + 1]).then_inc(s_h, 1)

            def stats(i):
                col = bass.ds(i, 1)
                act.wait_ge(s_y, i + 1)
                column_stats(act, s_stat, 3 * i, junk[:], rows[:, col, :].rearrange("p a n -> p (a n)"), sums[:, col],
                             core.negmean[:, col], core.var[:, col])

            normalise(0, 0, reuse=False)
            normalise(1, 1, reuse=False)
            x2_half(0, 0)
            x2_half(0, 1)
            for n in range(F4):
                split(n)

            def chunk(c, more, first=False):
                if more:
                    normalise(2 * c + 2, 0)
                    normalise(2 * c + 3, 1)
                for f in range(F4):
                    hidden(c, f)
                if more:
                    x2_half(c + 1, 0)
                if not first:
                    stats(2 * c - 2)
                    stats(2 * c - 1)
                if more:
                    x2_half(c + 1, 1)

            chunk(0, True, first=True)
            with act.Fori(1, CH - 1) as c:
                chunk(c, True)
            chunk(CH - 1, False)
            stats(NT - 2)
            stats(NT - 1)
            act.wait_ge(s_step, 1)
            act.activation(core.root[:], core.var[:], ACT.Sqrt).then_inc(s_step, 1)

        @block.gpsimd
        def _(pool):
            def residual(i, slot):
                pool.wait_ge(s_g[slot], 16 + 8 * (i - slot))
                pool.tensor_tensor(gnn_in[:, slot], gnn_in[:, slot], b2[:], ALU.add).then_inc(s_gb, 1)
                pool.wait_ge(s_gb, i + 1)
                pool.wait_ge(s_z, i + 1)
                pool.tensor_tensor(rows[:, bass.ds(i, 1), :].rearrange("p a n -> p (a n)"),
                                   rows[:, bass.ds(i, 1), :].rearrange("p a n -> p (a n)"), gnn_in[:, slot],
                                   ALU.add).then_inc(s_xg, 1)

            for n in range(F4):
                pool.wait_ge(s_whi, n + 1)
                pool.tensor_tensor(w2_lo[:, n, :], w_in[:, n % 2, :], f32(w2_hi[:, n, :]), ALU.subtract).then_inc(s_wlo, 1)
            pool.wait_ge(s_b2, 16)
            with pool.Fori(0, NT - 1, 2) as i:
                for p in range(2):
                    residual(i + p, p)

        @block.vector
        def _(dve):
            def affine(i, slot, reuse=True):
                dve.wait_ge(s_t, i + 1)
                dve.wait_ge(s_x2, i)
                dve.tensor_tensor(scaled[:].rearrange("p (a k) t -> p a k t", a=2),
                                  p_t[:, :, 0:4 * T].rearrange("p a (k t) -> p a k t", k=4),
                                  g2.rearrange("p (a k t) -> p a k t", a=2, t=1).to_broadcast([128, 2, 4, T]),
                                  ALU.mult).then_inc(s_sc, 1)
                dve.wait_ge(s_sc, i + 1)
                if reuse:
                    dve.wait_ge(s_xlo, i - 1)
                dve.tensor_tensor(x2[:, slot], scaled[:], b2c.rearrange("p (k t) -> p k t", t=1).to_broadcast([128, K8, T]),
                                  ALU.add).then_inc(s_x2, 1)

            def x2_half(c, half):
                dve.wait_ge(s_xhi, 2 * c + half + 1)
                cols = slice(half * T, (half + 1) * T)
                dve.tensor_tensor(x2_lo[:, :, cols], x2[:, half], f32(x2_hi[:, :, cols]), ALU.subtract).then_inc(s_xlo, 1)

            def hidden_halves(c, part):
                tiles = slice(2 * part, 2 * part + 2)
                dve.wait_ge(s_h, F4 * c + 2 * part + 2)
                dve.wait_ge(s_2, 2 * c)
                dve.tensor_copy(hid_hi[:, tiles], hid[:, tiles]).then_inc(s_hhi, 1)
                dve.wait_ge(s_hhi, 2 * c + part + 1)
                dve.tensor_tensor(hid_lo[:, tiles], hid[:, tiles], f32(hid_hi[:, tiles]), ALU.subtract).then_inc(s_hlo, 1)

            def add(i, slot):
                dve.wait_ge(s_2, i + 1)
                dve.wait_ge(s_xg, i + 1)
                out = rows[:, bass.ds(i, 1), :].rearrange("p a (b n) -> p (a b) n", b=2)
                dve.tensor_tensor(out, p_2[0:T, slot], out, ALU.add).then_inc(s_y, 1)

            affine(0, 0, reuse=False)
            affine(1, 1, reuse=False)
            x2_half(0, 0)
            x2_half(0, 1)

            def chunk(c, more):
                hidden_halves(c, 0)
                if more:
                    affine(2 * c + 2, 0)
                hidden_halves(c, 1)
                if more:
                    affine(2 * c + 3, 1)
                    x2_half(c + 1, 0)
                    x2_half(c + 1, 1)
                add(2 * c, 0)
                add(2 * c + 1, 1)

            with dve.Fori(0, CH - 1) as c:
                chunk(c, True)
            chunk(CH - 1, False)
            dve.wait_ge(s_stat, 3 * NT)
            dve.tensor_scalar(core.var[:], core.var[:], 1.0 / D, LN_EPS, ALU.mult, ALU.add).then_inc(s_step, 1)
            inverse_root(dve, s_step, 2, core.var[:], core.root[:], core.tmp[:], core.rstd[:])
            dve.tensor_tensor(core.ln_shift[:], core.negmean[:], core.rstd[:], ALU.mult).then_inc(s_step, 1)
            dve.wait_ge(s_step, 8)

        @block.tensor
        def _(pe):
            def transposes(i, slot, reuse=True):
                pe.wait_ge(s_z, i + 1)
                if reuse:
                    pe.wait_ge(s_sc, i)
                for k in range(K8):
                    last = pe.transpose(p_t[:, k // 4, (k % 4) * T:(k % 4 + 1) * T], z[:, slot, k * 128:(k + 1) * 128],
                                        core.ident[0:T, 0:T])
                last.then_inc(s_t, 1)

            def hidden(c, f, first=False):
                if f == 0:
                    pe.wait_ge(s_xlo, 2 * c + 2)
                if not (first and f < 2):
                    pe.wait_ge(s_h, F4 * c + f - 1)
                for k in range(K8):
                    for m, (left, right) in enumerate(((w1_lo, x2_hi), (w1_hi, x2_lo), (w1_hi, x2_hi))):
                        last = pe.matmul(p_1[:, f % 2, 0:CHUNK], left[:, k, f * 128:(f + 1) * 128], right[:, k, :],
                                         start=(k == 0 and m == 0), stop=(k == K8 - 1 and m == 2))
                last.then_inc(s_1, 1)

            def outer(c, first=False):
                pe.wait_ge(s_hlo, 2 * c + 2)
                if first:
                    pe.wait_ge(s_wlo, F4)
                for i in range(2):
                    if not first:
                        pe.wait_ge(s_y, 2 * c + i - 1)
                    tile = slice(i * T, (i + 1) * T)
                    for n in range(2):
                        for f in range(F4):
                            for m, (left, right) in enumerate(((hid_lo, w2_hi), (hid_hi, w2_lo), (hid_hi, w2_hi))):
                                last = pe.matmul(p_2[0:T, i, n, :], left[:, f, tile], right[:, f, n * 512:(n + 1) * 512],
                                                 start=(f == 0 and m == 0), stop=(f == F4 - 1 and m == 2))
                    last.then_inc(s_2, 1)

            def chunk(c, more, first=False):
                for f in range(F4):
                    hidden(c, f, first)
                    if more and f == 1:
                        transposes(2 * c + 2, 0)
                if more:
                    transposes(2 * c + 3, 1)
                outer(c, first)

            transposes(0, 0, reuse=False)
            transposes(1, 1)
            chunk(0, True, first=True)
            with pe.Fori(1, CH - 1) as c:
                chunk(c, True)
            chunk(CH - 1, False)


def quantised_forward(core):
    nc, rows, out = core.nc, core.rows, core.out
    F4 = FF // 128
    with ExitStack() as ctx:
        def sb(name, shape, dt=F32):
            return ctx.enter_context(nc.sbuf_tensor(name, shape, dt))

        def ps(name, shape, dt=F32):
            return ctx.enter_context(nc.psum_tensor(name, shape, dt))

        ident_b = sb("ident_b", [128, 128], BF16)
        w_gate = sb("gate_t", [128, K8, FF], BF16)
        w_up = sb("up_t", [128, K8, FF], BF16)
        w_down = sb("down_t", [128, F4, D], BF16)
        z = sb("z8", [T, 2, D])
        most = sb("most", [T, 2, 3])
        small = sb("limited8", [T, 2, D])
        lifted = sb("lifted8", [T, 2, D])
        xq = sb("x_rounded", [T, 2, D], BF16)
        xt = sb("x_rounded_t", [128, 2, K8, T], BF16)
        factor = sb("factors", [T, NT, 3])
        gate = sb("gate", [T, FF])
        hid = sb("hidden8", [T, FF])
        most2 = sb("most_hidden", [T, 3])
        small2 = sb("limited_hidden", [T, FF])
        lifted2 = sb("lifted_hidden", [T, FF])
        hq = sb("hidden_rounded", [T, FF], BF16)
        ht = sb("hidden_rounded_t", [128, F4, T], BF16)
        result = sb("result", [T, 2, D])
        p_tr = ps("p_tr8", [128, 2, K8, 128], BF16)
        p_gu = ps("p_gate_up", [128, 2, 2, 512])
        p_d = ps("p_down", [128, 2, 512])

        s_ib = core.sem("ident_b_ready")
        s_wt = core.sem("weights_transposed")
        s_wk = [core.sem(f"weights_kept{i}") for i in range(2)]
        s_z = core.sem("z8_ready")
        s_m = core.sem("row_scale_step")
        s_small = core.sem("limited8_ready")
        s_lift = core.sem("lifted8_ready")
        s_xq = core.sem("x_rounded_ready")
        s_xt = core.sem("x_transposed8")
        s_xk = core.sem("x_transposed_kept")
        s_gu = core.sem("gate_up_done")
        s_gate = core.sem("silu_ready")
        s_hid = core.sem("hidden8_ready")
        s_m2 = core.sem("hidden_scale_step")
        s_small2 = core.sem("limited_hidden_ready")
        s_lift2 = core.sem("lifted_hidden_ready")
        s_hq = core.sem("hidden_rounded_ready")
        s_ht = core.sem("hidden_transposed")
        s_hk = core.sem("hidden_transposed_kept")
        s_d = core.sem("down_done")
        s_dk = core.sem("down_kept")
        s_out = core.sem("result_ready")
        s_st = [core.sem(f"result_stored{i}") for i in range(2)]

        block = ctx.enter_context(nc.Block())

        def rounds(n):
            matrix, part = n // 4, n % 4
            if matrix < 2:
                blocks = [(part * 8 + k) * 128 for k in range(K8)]
                target = (w_gate, w_up)[matrix][:, :, part * 128:(part + 1) * 128]
                return blocks, target, (lambda p: p)
            blocks = [((2 * part + a) * F4 + k) * 128 for k in range(F4) for a in range(2)]
            target = w_down[:, :, part * 256:(part + 1) * 256]
            return blocks, target, (lambda p: p.rearrange("p (k a) n -> p k (a n)", a=2))

        @block.sync
        def _(sp):
            def store(i, slot):
                sp.wait_ge(s_out, i + 1)
                sp.dma_start(out[bass.ds(i * T, T), :], result[:, slot]).then_inc(s_st[slot], 16)

            with sp.Fori(0, NT - 1, 2) as i:
                for p in range(2):
                    store(i + p, p)
            for p in range(2):
                sp.wait_ge(s_st[p], 16 * NT // 2)

        @block.gpsimd
        def _(pool):
            pool.tensor_copy(ident_b[:], core.ident[:]).then_inc(s_ib, 1)

            def finish(i, slot):
                pool.wait_ge(s_dk, i + 1)
                pool.tensor_tensor(result[:, slot], result[:, slot], rows[:, bass.ds(i, 1), :].rearrange("p a n -> p (a n)"),
                                   ALU.add).then_inc(s_out, 1)

            with pool.Fori(0, NT - 1, 2) as i:
                for p in range(2):
                    finish(i + p, p)

        @block.scalar
        def _(act):
            def normalise(i, slot, reuse=True):
                if reuse:
                    act.wait_ge(s_small, i - 1)
                col = bass.ds(i, 1)
                act.activation(z[:, slot], rows[:, col, :].rearrange("p a n -> p (a n)"), ACT.Identity,
                               scale=core.rstd[:, col], bias=core.ln_shift[:, col]).then_inc(s_z, 1)

            def round_x(i, slot, reuse=True):
                act.wait_ge(s_lift, i + 1)
                if reuse:
                    act.wait_ge(s_xt, i - 1)
                act.activation(xq[:, slot], lifted[:, slot], ACT.Copy, bias=-MAGIC).then_inc(s_xq, 1)

            def silu(i, slot):
                act.wait_ge(s_gu, i + 1)
                act.wait_ge(s_hid, i)
                act.activation(gate[:], p_gu[0:T, slot, 0, :], ACT.Silu, scale=factor[:, bass.ds(i, 1), 0:1].rearrange("p a b -> p (a b)")).then_inc(s_gate, 1)

            def round_hidden(i):
                act.wait_ge(s_lift2, i + 1)
                act.wait_ge(s_ht, i)
                act.activation(hq[:], lifted2[:], ACT.Copy, bias=-MAGIC).then_inc(s_hq, 1)

            def keep_down(i, slot, reuse=True):
                act.wait_ge(s_d, i + 1)
                if reuse:
                    act.wait_ge(s_st[slot], 8 * (i - slot))
                act.activation(result[:, slot].rearrange("p (b n) -> p b n", b=2), p_d[0:T], ACT.Copy,
                               scale=factor[:, bass.ds(i, 1), 2:3].rearrange("p a b -> p (a b)")).then_inc(s_dk, 1)

            def keep_x(i, slot, reuse=True):
                act.wait_ge(s_xt, i + 1)
                if reuse:
                    act.wait_ge(s_gu, i - 1)
                act.activation(xt[:, slot], p_tr[:, 0, :, 0:T], ACT.Copy).then_inc(s_xk, 1)

            def keep_hidden(i):
                act.wait_ge(s_ht, i + 1)
                act.wait_ge(s_d, i)
                act.activation(ht[:], p_tr[:, 1, 0:F4, 0:T], ACT.Copy).then_inc(s_hk, 1)

            normalise(0, 0, reuse=False)
            normalise(1, 1, reuse=False)

            def keep_weights(first, past):
                for n in range(first, past, 2):
                    blocks, target, view = rounds(n)
                    act.wait_ge(s_wt, n + 1)
                    act.activation(target, view(p_tr[:, 1]), ACT.Copy).then_inc(s_wk[1], 1)

            keep_weights(1, 8)
            round_x(0, 0, reuse=False)
            keep_x(0, 0, reuse=False)
            keep_weights(9, 12)
            round_x(1, 1, reuse=False)
            keep_x(1, 1, reuse=False)
            normalise(2, 0)

            def tile(i, slot, ahead=3, first=False, reuse=True):
                silu(i, slot)
                if not first:
                    keep_hidden(i - 1)
                    if ahead > 0:
                        keep_x(i + 1, 1 - slot)
                if ahead > 1:
                    round_x(i + 2, slot)
                if not first:
                    keep_down(i - 1, 1 - slot, reuse=reuse)
                if ahead > 2:
                    normalise(i + 3, 1 - slot)
                round_hidden(i)

            tile(0, 0, first=True)
            tile(1, 1, reuse=False)
            tile(2, 0, reuse=False)
            with act.Fori(3, NT - 4, 2) as i:
                for p in range(2):
                    tile(i + p, 1 - p)
            tile(NT - 3, 1, ahead=2)
            tile(NT - 2, 0, ahead=1)
            tile(NT - 1, 1, ahead=0)
            keep_hidden(NT - 1)
            keep_down(NT - 1, 1)

        @block.vector
        def _(dve):
            def factor_of(i, n):
                return factor[:, bass.ds(i, 1), n:n + 1].rearrange("p a b -> p (a b)")

            def row_scale(i, values, most, s, factors):
                dve.tensor_reduce(most[:, 0:1], values, AX.X, ALU.max, apply_absolute_value=True).then_inc(s, 1)
                dve.wait_ge(s, 3 * i + 1)
                dve.tensor_scalar(most[:, 1:2], most[:, 0:1], 1e-5, 1.0 / 127.0, ALU.max, ALU.mult).then_inc(s, 1)
                dve.wait_ge(s, 3 * i + 2)
                for n in factors:
                    dve.tensor_tensor(factor_of(i, n), most[:, 1:2], core.w_mean[0:T, n:n + 1], ALU.mult)
                dve.reciprocal(most[:, 2:3], most[:, 1:2]).then_inc(s, 1)
                dve.wait_ge(s, 3 * i + 3)

            def round_up(i, values, scale, small, lifted, s_small, s_lift):
                dve.tensor_scalar(small, values, scale, 127.0, ALU.mult, ALU.min).then_inc(s_small, 1)
                dve.wait_ge(s_small, i + 1)
                dve.tensor_scalar(lifted, small, -128.0, MAGIC, ALU.max, ALU.add).then_inc(s_lift, 1)

            def scale_x(i, slot, reuse=True):
                dve.wait_ge(s_z, i + 1)
                if reuse:
                    dve.wait_ge(s_lift, i - 1)
                row_scale(i, z[:, slot], most[:, slot], s_m, (0, 1))
                if reuse:
                    dve.wait_ge(s_xq, i - 1)
                round_up(i, z[:, slot], most[:, slot, 2:3], small[:, slot], lifted[:, slot], s_small, s_lift)

            def hidden(i, slot):
                dve.wait_ge(s_gate, i + 1)
                dve.wait_ge(s_small2, i)
                dve.scalar_tensor_tensor(hid[:], p_gu[0:T, slot, 1, :], factor_of(i, 1), gate[:], ALU.mult,
                                         ALU.mult).then_inc(s_hid, 1)
                dve.wait_ge(s_hid, i + 1)
                row_scale(i, hid[:], most2, s_m2, (2,))
                dve.wait_ge(s_lift2, i)
                dve.wait_ge(s_hq, i)
                round_up(i, hid[:], most2[:, 2:3], small2[:], lifted2[:], s_small2, s_lift2)

            scale_x(0, 0, reuse=False)

            def keep_weights(first, past):
                for n in range(first, past, 2):
                    blocks, target, view = rounds(n)
                    dve.wait_ge(s_wt, n + 1)
                    dve.tensor_copy(target, view(p_tr[:, 0])).then_inc(s_wk[0], 1)

            keep_weights(0, 8)
            scale_x(1, 1, reuse=False)
            keep_weights(8, 12)

            def tile(i, slot, more=True):
                if more:
                    scale_x(i + 2, slot)
                hidden(i, slot)

            scale_x(2, 0)
            hidden(0, 0)
            scale_x(3, 1)
            hidden(1, 1)
            scale_x(4, 0)
            hidden(2, 0)
            with dve.Fori(3, NT - 3, 2) as i:
                for p in range(2):
                    tile(i + p, 1 - p)
            tile(NT - 3, 1)
            tile(NT - 2, 0, more=False)
            tile(NT - 1, 1, more=False)

        @block.tensor
        def _(pe):
            pe.wait_ge(s_ib, 1)
            def transpose_weights(first, past):
                for n in range(first, past):
                    if n >= 2:
                        pe.wait_ge(s_wk[n % 2], n // 2)
                    blocks, _, _ = rounds(n)
                    for b, at in enumerate(blocks):
                        last = pe.transpose(p_tr[:, n % 2, b, :], core.ternary[:, n // 4, at:at + 128], ident_b[:])
                    last.then_inc(s_wt, 1)

            def transpose_x(i, slot):
                pe.wait_ge(s_xq, i + 1)
                pe.wait_ge(s_xk, i)
                for k in range(K8):
                    last = pe.transpose(p_tr[:, 0, k, 0:T], xq[:, slot, k * 128:(k + 1) * 128], ident_b[0:T, 0:T])
                last.then_inc(s_xt, 1)

            def gate_up(i, slot, reuse=True):
                pe.wait_ge(s_xk, i + 1)
                if reuse:
                    pe.wait_ge(s_hid, i - 1)
                for n, w in enumerate((w_gate, w_up)):
                    for k in range(K8):
                        last = pe.matmul(p_gu[0:T, slot, n, :], xt[:, slot, k, :], w[:, k, :], start=(k == 0), stop=(k == K8 - 1))
                last.then_inc(s_gu, 1)

            def transpose_hidden(i):
                pe.wait_ge(s_hq, i + 1)
                pe.wait_ge(s_hk, i)
                for k in range(F4):
                    last = pe.transpose(p_tr[:, 1, k, 0:T], hq[:, k * 128:(k + 1) * 128], ident_b[0:T, 0:T])
                last.then_inc(s_ht, 1)

            def down(i):
                pe.wait_ge(s_hk, i + 1)
                pe.wait_ge(s_dk, i)
                for n in range(2):
                    for k in range(F4):
                        last = pe.matmul(p_d[0:T, n, :], ht[:, k, :], w_down[:, k, n * 512:(n + 1) * 512],
                                         start=(k == 0), stop=(k == F4 - 1))
                last.then_inc(s_d, 1)

            transpose_weights(0, 8)
            for p in range(2):
                pe.wait_ge(s_wk[p], 4)
            transpose_x(0, 0)
            gate_up(0, 0, reuse=False)
            transpose_weights(8, 12)
            for p in range(2):
                pe.wait_ge(s_wk[p], 6)
            transpose_x(1, 1)
            gate_up(1, 1, reuse=False)
            transpose_hidden(0)
            transpose_x(2, 0)
            down(0)
            with pe.Fori(2, NT - 3, 2) as i:
                for p in range(2):
                    gate_up(i + p, p)
                    transpose_hidden(i + p - 1)
                    transpose_x(i + p + 1, 1 - p)
                    down(i + p - 1)
            gate_up(NT - 2, 0)
            transpose_hidden(NT - 3)
            transpose_x(NT - 1, 1)
            down(NT - 3)
            gate_up(NT - 1, 1)
            transpose_hidden(NT - 2)
            down(NT - 2)
            transpose_hidden(NT - 1)
            down(NT - 1)


def gps_layer_kernel(nc, inputs, out):
    with ExitStack() as stack:
        core = Core(nc, stack, inputs, out)
        core.ident = core.keep("ident", [128, 128], F32)
        core.ident_ready = core.sem("ident_ready")
        core.mean = core.keep("row_sums", [T, NT], F32)
        core.negmean = core.keep("neg_means", [T, NT], F32)
        core.var = core.keep("variances", [T, NT], F32)
        core.root = core.keep("roots", [T, NT], F32)
        core.tmp = core.keep("first_rstd", [T, NT], F32)
        core.rstd = core.keep("rstd", [T, NT], F32)
        core.rstd2 = core.keep("rstd2", [T, NT], F32)
        core.ln_scale = core.keep("ln_scale", [T, NT], F32)
        core.ln_shift = core.keep("ln_shift", [T, NT], F32)
        core.xn_shift = core.keep("xn_shift", [T, NT], F32)
        core.gnn_dram = nc.dram_tensor("gnn_dram", (N, D), F32).ap()
        core.ternary_dram = [nc.dram_tensor(f"ternary_dram{n}", (128, FF * D // 128), BF16).ap() for n in range(3)]
        core.w_mean = core.keep("w_mean", [128, 3], F32)
        core.al = core.keep("al", [T, NT], F32)
        core.ar = core.keep("ar", [T, NT], F32)
        core.vectors = core.keep("vectors", [COLUMN_COUNT, 128], F32)
        core.vectors_loaded = core.sem("vectors_loaded")
        core.cols = core.keep("columns", [128, COLUMN_COUNT], F32)
        core.gnn_stored = [core.sem(f"gnn_stored{i}") for i in range(2)]
        core.attention_stored = nc.alloc_semaphore(name="attention_stored")
        core.mix_loaded, core.mix_hi_ready, core.mix_lo_ready = (
            [nc.alloc_semaphore(name=f"{what}_{n}") for n in "vkq"] for what in ("weights_loaded", "weights_hi", "weights_lo"))
        with ExitStack() as gnn:
            core.counts = gnn.enter_context(nc.sbuf_tensor("counts", [T, NT, N], U16))
            with nc.sbuf_tensor("w_hi", [128, K8, D], F32R, side="right") as w_hi, \
                 nc.sbuf_tensor("w_lo", [128, K8, D], F32R, side="right") as w_lo:
                count_edges(core, w_hi, w_lo)
                core.next_reading()
                core.h_hi = gnn.enter_context(nc.sbuf_tensor("h_hi", [T, NT, H_EXT], F32R))
                core.h_lo = gnn.enter_context(nc.sbuf_tensor("h_lo", [T, NT, H_EXT], F32R))
                node_features(core, w_hi, w_lo)
                core.next_reading()
            attend_over_edges(core)
            core.next_reading()
        core.attn_dram = nc.dram_tensor("attn_dram", (D, N), F32).ap()
        with ExitStack() as mix:
            core.x2_hi = mix.enter_context(nc.sbuf_tensor("x2_hi", [128, K8, N], F32R))
            core.x2_lo = mix.enter_context(nc.sbuf_tensor("x2_lo", [128, K8, N], F32R))
            with ExitStack() as pairs:
                core.mix_in, core.mix_hi, core.mix_lo = (
                    [pairs.enter_context(nc.sbuf_tensor(f"mix_{part}_{n}", [128, K8, 128], dt)) for n in "vkq"]
                    for part, dt in (("in", F32), ("hi", F32R), ("lo", F32R)))
                transpose_second_norm(core)
                core.next_reading()
                core.renew_semaphores()
                linear_attention(core)
            core.rows = stack.enter_context(nc.sbuf_tensor("rows", [T, NT, D], F32, side="right"))
            second = stack.enter_context(ExitStack())
            core.w1_hi = second.enter_context(nc.sbuf_tensor("w1_hi", [128, K8, FF], F32R, side="right"))
            core.w1_lo = second.enter_context(nc.sbuf_tensor("w1_lo", [128, K8, FF], F32R, side="right"))
            project_attention(core)
        core.ternary = core.keep("ternary", [128, 3, FF * D // 128], BF16)
        feed_forward(core)
        second.close()
        quantised_forward(core)


_INS = ["x", "src", "dst", "L0_gnn_W", "L0_gnn_a", "L0_mix_proj_mat", "L0_mix_wq", "L0_mix_bq", "L0_mix_wk",
        "L0_mix_bk", "L0_mix_wv", "L0_mix_bv", "L0_mix_wo", "L0_mix_bo", "L0_mix_ln1_g", "L0_mix_ln1_b", "L0_mix_w1",
        "L0_mix_b1", "L0_mix_w2", "L0_mix_b2", "L0_mix_ln2_g", "L0_mix_ln2_b", "L0_ffn_w_gate", "L0_ffn_w_up",
        "L0_ffn_w_down"]


def kernel(**inputs):
    import numpy as _np
    import concourse.bacc as _bacc
    from concourse import mybir as _mybir
    from concourse.bass_utils import run_bass_kernel_spmd as _run

    nc = _bacc.Bacc("TRN2", target_bir_lowering=False, num_devices=1)
    arrays, args = {}, {}
    for name in _INS:
        a = _np.ascontiguousarray(inputs[name])
        arrays[f"in_{name}_dram"] = a
        args[name] = nc.dram_tensor(f"in_{name}_dram", a.shape, _mybir.dt.from_np(a.dtype), kind="ExternalInput").ap()
    out = nc.dram_tensor("out_dram", (N, D), F32, kind="ExternalOutput").ap()
    gps_layer_kernel(nc, args, out)
    r = _run(nc, [arrays], core_ids=[0])
    return r.results[0]["out_dram"]
```
